# Optimizing a Trainium2 kernel written in Bass

```python
import numpy as np
import jax
import jax.numpy as jnp

def _softmax(x, axis=-1):
    return jax.nn.softmax(x, axis=axis)
def _gelu(x):
    return jax.nn.gelu(x, approximate=True)
def _silu(x):
    return jax.nn.silu(x)
def _sigmoid(x):
    return jax.nn.sigmoid(x)
def _layernorm(x, axis=-1, eps=1e-5):
    m = jnp.mean(x, axis=axis, keepdims=True)
    v = jnp.var(x, axis=axis, keepdims=True)
    return (x - m) / jnp.sqrt(v + eps)
def _scatter_add(tgt, idx, src, axis=0):
    return tgt.at[idx].add(src)
def _segment_sum(src, seg, n):
    return jax.ops.segment_sum(src, seg, n)

kernel_name = 'mk_conv_attn_hybrid_d2_conv_nchw256_968c66'

def setup_inputs(seed: int = 0):
    np.random.seed(seed)
    _w = jnp.asarray
    def _rec_inputs():
        import jax
        import jax.numpy as jnp
        _gk = jax.random.key(seed)
        x = -0.0009896 + 1 * jax.random.normal(jax.random.fold_in(_gk, 1), (2, 256, 56, 56), jnp.float32)
        return x
    x = _rec_inputs()
    def _L0_conv_setup():
        import jax, jax.numpy as jnp
        import numpy as np
        WS = 7

        def _attn_idx(H, W, ws):
            Ho, Wo = (H - (ws - 1), W - (ws - 1))
            idx = np.arange(Ho * Wo, dtype=np.int64).reshape(Ho, Wo)
            pad = ws // 2
            idx = np.pad(idx, pad, mode='edge')
            return jnp.asarray(idx.reshape(-1))

        def _bias_idx(H, W, ws):
            rep_h = np.ones(ws, dtype=np.int64)
            rep_h[ws // 2] = H - (ws - 1)
            rep_w = np.ones(ws, dtype=np.int64)
            rep_w[ws // 2] = W - (ws - 1)
            idx_h = np.repeat(np.arange(ws), rep_h)
            idx_w = np.repeat(np.arange(ws), rep_w)
            bias_hw = idx_h[:, None] * (2 * ws - 1) + idx_w[None, :]
            idx_k = (np.arange(ws)[:, None] * (2 * ws - 1) + np.arange(ws)).reshape(-1)
            bias_idx = bias_hw.reshape(-1)[:, None] + idx_k[None, :]
            return jnp.asarray(bias_idx)
        key = jax.random.key(seed)
        k0, k1, k2, k3 = jax.random.split(key, 4)
        B, C, H, W = (2, 256, 56, 56)
        nh = 8
        x = jax.random.normal(k0, (B, C, H, W), jnp.float32)
        qkv_w = jax.random.normal(k1, (3 * C, C), jnp.float32) * 0.02
        qkv_b = jnp.zeros((3 * C,), jnp.float32)
        proj_w = jax.random.normal(k2, (C, C), jnp.float32) * 0.02
        proj_b = jnp.zeros((C,), jnp.float32)
        relative_bias = jax.random.normal(k3, ((2 * WS - 1) ** 2, nh), jnp.float32) * 0.02
        return {'x': x, 'qkv_w': qkv_w, 'qkv_b': qkv_b, 'proj_w': proj_w, 'proj_b': proj_b, 'relative_bias': relative_bias}
    _L0_conv_all = _L0_conv_setup()
    _L0_conv_in = {k: v for k, v in _L0_conv_all.items() if k in ('qkv_w', 'qkv_b', 'proj_w', 'proj_b', 'relative_bias', )}
    del _L0_conv_all

    def _L1_attn_setup():
        import jax, jax.numpy as jnp
        import numpy as np
        import math
        B, T, C = (4, 2048, 256)
        H = 8
        HD = C // H
        key = jax.random.key(seed)
        k1, k2, k3 = jax.random.split(key, 3)
        x = jax.random.normal(k1, (B, T, C), dtype=jnp.float32)
        w_qkv = jax.random.normal(k2, (C, 3 * C), dtype=jnp.float32) * (1.0 / math.sqrt(C))
        b_qkv = jnp.zeros((3 * C,), dtype=jnp.float32)
        w_proj = jax.random.normal(k3, (C, C), dtype=jnp.float32) * (1.0 / math.sqrt(C))
        b_proj = jnp.zeros((C,), dtype=jnp.float32)
        return {'x': x, 'w_qkv': w_qkv, 'b_qkv': b_qkv, 'w_proj': w_proj, 'b_proj': b_proj}
    _L1_attn_all = _L1_attn_setup()
    _L1_attn_in = {k: v for k, v in _L1_attn_all.items() if k in ('w_qkv', 'b_qkv', 'w_proj', 'b_proj', )}
    del _L1_attn_all

    def _L1_ffn_setup():
        import jax, jax.numpy as jnp
        import numpy as np
        NUM_EXPERTS = 8
        TOP_K = 2
        B, S, D = (8, 8192, 256)

        def _moe(tokens, router_w, w1, b1, w2, b2):
            N = tokens.shape[0]
            E = router_w.shape[0]
            logits = tokens.astype(jnp.float32) @ router_w.astype(jnp.float32).T
            probs = jax.nn.softmax(logits, axis=-1)
            rw, re = jax.lax.top_k(probs, TOP_K)
            if TOP_K > 1:
                rw = rw / jnp.maximum(rw.sum(-1, keepdims=True), 1e-12)
            rw = rw.astype(tokens.dtype)
            combine = jnp.zeros((N, E), tokens.dtype).at[jnp.arange(N)[:, None], re].set(rw)
            out = tokens
            for e in range(E):
                h = jax.nn.gelu(tokens @ w1[e] + b1[e], approximate=False)
                y = h @ w2[e] + b2[e]
                out = out + combine[:, e:e + 1] * y
            return out
        key = jax.random.key(seed)
        ks = jax.random.split(key, 4)
        scale = 1.0 / np.sqrt(D).astype(np.float32)
        return {'input_embeddings': jax.random.normal(ks[0], (B, S, D), jnp.float32), 'router_w': jax.random.normal(ks[1], (NUM_EXPERTS, D), jnp.float32) * scale, 'w1': jax.random.normal(ks[2], (NUM_EXPERTS, D, D), jnp.float32) * scale, 'b1': jnp.zeros((NUM_EXPERTS, D), jnp.float32), 'w2': jax.random.normal(ks[3], (NUM_EXPERTS, D, D), jnp.float32) * scale, 'b2': jnp.zeros((NUM_EXPERTS, D), jnp.float32)}
    _L1_ffn_all = _L1_ffn_setup()
    _L1_ffn_in = {k: v for k, v in _L1_ffn_all.items() if k in ('router_w', 'w1', 'b1', 'w2', 'b2', )}
    del _L1_ffn_all

    return {
        "x": x,
        "L0_conv_qkv_w": _L0_conv_in["qkv_w"],
        "L0_conv_qkv_b": _L0_conv_in["qkv_b"],
        "L0_conv_proj_w": _L0_conv_in["proj_w"],
        "L0_conv_proj_b": _L0_conv_in["proj_b"],
        "L0_conv_relative_bias": _L0_conv_in["relative_bias"],
        "L1_attn_w_qkv": _L1_attn_in["w_qkv"],
        "L1_attn_b_qkv": _L1_attn_in["b_qkv"],
        "L1_attn_w_proj": _L1_attn_in["w_proj"],
        "L1_attn_b_proj": _L1_attn_in["b_proj"],
        "L1_ffn_router_w": _L1_ffn_in["router_w"],
        "L1_ffn_w1": _L1_ffn_in["w1"],
        "L1_ffn_b1": _L1_ffn_in["b1"],
        "L1_ffn_w2": _L1_ffn_in["w2"],
        "L1_ffn_b2": _L1_ffn_in["b2"],
    }

def reference(x, L0_conv_qkv_w, L0_conv_qkv_b, L0_conv_proj_w, L0_conv_proj_b, L0_conv_relative_bias, L1_attn_w_qkv, L1_attn_b_qkv, L1_attn_w_proj, L1_attn_b_proj, L1_ffn_router_w, L1_ffn_w1, L1_ffn_b1, L1_ffn_w2, L1_ffn_b2):
    import jax
    import jax.numpy as jnp
    def _L0_conv_ref(x, qkv_w, qkv_b, proj_w, proj_b, relative_bias):
        import jax, jax.numpy as jnp
        import numpy as np
        WS = 7

        def _attn_idx(H, W, ws):
            Ho, Wo = (H - (ws - 1), W - (ws - 1))
            idx = np.arange(Ho * Wo, dtype=np.int64).reshape(Ho, Wo)
            pad = ws // 2
            idx = np.pad(idx, pad, mode='edge')
            return jnp.asarray(idx.reshape(-1))

        def _bias_idx(H, W, ws):
            rep_h = np.ones(ws, dtype=np.int64)
            rep_h[ws // 2] = H - (ws - 1)
            rep_w = np.ones(ws, dtype=np.int64)
            rep_w[ws // 2] = W - (ws - 1)
            idx_h = np.repeat(np.arange(ws), rep_h)
            idx_w = np.repeat(np.arange(ws), rep_w)
            bias_hw = idx_h[:, None] * (2 * ws - 1) + idx_w[None, :]
            idx_k = (np.arange(ws)[:, None] * (2 * ws - 1) + np.arange(ws)).reshape(-1)
            bias_idx = bias_hw.reshape(-1)[:, None] + idx_k[None, :]
            return jnp.asarray(bias_idx)
        B, C, H, W = x.shape
        ws = WS
        nh = relative_bias.shape[1]
        hd = C // nh
        scale = hd ** (-0.5)
        L = (H - ws + 1) * (W - ws + 1)
        qkv = jnp.einsum('oc,bchw->bohw', qkv_w, x) + qkv_b[None, :, None, None]
        q, k, v = (qkv[:, :C], qkv[:, C:2 * C], qkv[:, 2 * C:])
        q = q * scale

        def unfold(t):
            p = jax.lax.conv_general_dilated_patches(t, (ws, ws), (1, 1), 'VALID')
            return p.reshape(B, C, L, ws * ws)
        attn_idx = _attn_idx(H, W, ws)
        bias_idx = _bias_idx(H, W, ws)
        k_u = unfold(k).reshape(B, nh, hd, L, ws * ws).transpose(0, 1, 3, 2, 4)
        v_u = unfold(v).reshape(B, nh, hd, L, ws * ws).transpose(0, 1, 3, 4, 2)
        k_g = k_u[:, :, attn_idx]
        v_g = v_u[:, :, attn_idx]
        qh = q.reshape(B, nh, hd, H * W).transpose(0, 1, 3, 2)
        attn = jnp.einsum('bnld,bnldk->bnlk', qh, k_g)
        bias = jnp.transpose(relative_bias[bias_idx], (2, 0, 1))
        attn = attn + bias[None]
        out = jnp.einsum('bnlk,bnlkd->bnld', attn, v_g)
        out = jnp.transpose(out, (0, 1, 3, 2)).reshape(B, C, H, W)
        out = jnp.einsum('oc,bchw->bohw', proj_w, out) + proj_b[None, :, None, None]
        return out

    def _L1_attn_ref(x, w_qkv, b_qkv, w_proj, b_proj):
        import jax, jax.numpy as jnp
        import numpy as np
        import math
        B, T, C = (4, 2048, 256)
        H = 8
        HD = C // H
        Bq, Tq, Cq = x.shape
        qkv = x @ w_qkv + b_qkv
        q, k, v = jnp.split(qkv, 3, axis=-1)
        q = q.reshape(Bq, Tq, H, HD).transpose(0, 2, 1, 3)
        k = k.reshape(Bq, Tq, H, HD).transpose(0, 2, 1, 3)
        v = v.reshape(Bq, Tq, H, HD).transpose(0, 2, 1, 3)
        att = jnp.einsum('bhqd,bhkd->bhqk', q, k) * (1.0 / math.sqrt(HD))
        causal = jnp.tril(jnp.ones((Tq, Tq), dtype=bool))
        att = jnp.where(causal[None, None], att, jnp.float32(-jnp.inf))
        att = jax.nn.softmax(att, axis=-1)
        y = jnp.einsum('bhqk,bhkd->bhqd', att, v)
        y = y.transpose(0, 2, 1, 3).reshape(Bq, Tq, Cq)
        return y @ w_proj + b_proj

    def _L1_ffn_ref(input_embeddings, router_w, w1, b1, w2, b2):
        import jax, jax.numpy as jnp
        import numpy as np
        NUM_EXPERTS = 8
        TOP_K = 2
        B, S, D = (8, 8192, 256)

        def _moe(tokens, router_w, w1, b1, w2, b2):
            N = tokens.shape[0]
            E = router_w.shape[0]
            logits = tokens.astype(jnp.float32) @ router_w.astype(jnp.float32).T
            probs = jax.nn.softmax(logits, axis=-1)
            rw, re = jax.lax.top_k(probs, TOP_K)
            if TOP_K > 1:
                rw = rw / jnp.maximum(rw.sum(-1, keepdims=True), 1e-12)
            rw = rw.astype(tokens.dtype)
            combine = jnp.zeros((N, E), tokens.dtype).at[jnp.arange(N)[:, None], re].set(rw)
            out = tokens
            for e in range(E):
                h = jax.nn.gelu(tokens @ w1[e] + b1[e], approximate=False)
                y = h @ w2[e] + b2[e]
                out = out + combine[:, e:e + 1] * y
            return out
        b, s, d = input_embeddings.shape
        tokens = input_embeddings.reshape(b * s, d)
        return _moe(tokens, router_w, w1, b1, w2, b2).reshape(b, s, d)

    def _gn(v, G=32, eps=1e-5):
        B_, C_, H_, W_ = v.shape
        g = v.reshape(B_, G, C_ // G, H_, W_)
        m = jnp.mean(g, axis=(2, 3, 4), keepdims=True)
        s = jnp.var(g, axis=(2, 3, 4), keepdims=True)
        return ((g - m) / jnp.sqrt(s + eps)).reshape(v.shape)

    def _ln_c(v, eps=1e-6):
        m = jnp.mean(v, axis=1, keepdims=True)
        s = jnp.var(v, axis=1, keepdims=True)
        return (v - m) / jnp.sqrt(s + eps)

    def _ln_t(v, eps=1e-5):
        m = jnp.mean(v, axis=-1, keepdims=True)
        s = jnp.var(v, axis=-1, keepdims=True)
        return (v - m) / jnp.sqrt(s + eps)

    def _to_tokens(v):
        B_, C_, H_, W_ = v.shape
        return v.reshape(B_, C_, H_ * W_).transpose(0, 2, 1)
    def _from_tokens(t, like):
        B_, C_, H_, W_ = like.shape
        return t.transpose(0, 2, 1).reshape(B_, C_, H_, W_)

    x = x + _L0_conv_ref(_gn(x), L0_conv_qkv_w, L0_conv_qkv_b, L0_conv_proj_w, L0_conv_proj_b, L0_conv_relative_bias)
    t = _to_tokens(x)
    t = t + _L1_attn_ref(_ln_t(t), L1_attn_w_qkv, L1_attn_b_qkv, L1_attn_w_proj, L1_attn_b_proj)
    t = t + _L1_ffn_ref(_ln_t(t), L1_ffn_router_w, L1_ffn_w1, L1_ffn_b1, L1_ffn_w2, L1_ffn_b2)
    x = _from_tokens(t, x)
    return x


_drawn_inputs = setup_inputs


def setup_inputs(seed=0):
    import zlib

    import numpy as np

    out = dict(_drawn_inputs(seed))
    spreads = {'L0_conv_qkv_b': (0.0, 0.1),
     'L0_conv_proj_b': (0.0, 0.1),
     'L1_attn_b_qkv': (0.0, 0.1),
     'L1_attn_b_proj': (0.0, 0.1),
     'L1_ffn_b1': (0.0, 0.321),
     'L1_ffn_b2': (0.0, 0.1)}
    factors = {}
    for name, (base, spread) in spreads.items():
        noise = np.random.default_rng([zlib.crc32(name.encode()), seed]).standard_normal(out[name].shape)
        drawn = base * np.exp(spread * noise) if base else spread * noise
        out[name] = jnp.asarray(drawn.astype(out[name].dtype))
    for name, factor in factors.items():
        out[name] = (out[name] * factor).astype(out[name].dtype)
    return out
```

```python
from contextlib import ExitStack

import numpy as np

import concourse.bass as bass
from concourse import mybir

F32 = mybir.dt.float32
BF16 = mybir.dt.bfloat16
ALU = mybir.AluOpType
ACT = mybir.ActivationFunctionType
AX = mybir.AxisListType

IMAGES, CH, SIDE = 2, 256, 56
TOK = SIDE * SIDE
HEADS, HD = 8, 32
CC = CH // 128
HC = HEADS // CC
TT = 2 * SIDE
NT = TOK // TT
SUP = 4 * TT
NS = TOK // SUP
SCALE = float(HD) ** -0.5

WS = 7
K2 = WS * WS
WIN = SIDE - WS + 1
L = WIN * WIN
HALF = WS // 2
DY, DX, T4 = 356, 51, 4
WCOLS = WS * WS * T4
TAB0 = 147
TABN = TAB0 + 2 * (NT - 1) + 6 * (WS - 1) + 1
PADN = TABN + WIN + SIDE + 2
EDGE = 3
BH = WIN // 2

NEG = -1e30
LOUD_EPS = 1e-5
EXPERTS = 8


def neighbourhood_mask():
    m = np.zeros((TT, NT, WS, WS, T4), np.uint8)
    for tile in range(NT):
        for dy in range(WS):
            for dx in range(WS):
                for p in range(TT):
                    r, c = 2 * tile + p // SIDE - dy, p % SIDE - dx
                    if not (0 <= r < WIN and 0 <= c < WIN):
                        continue
                    f = (WS * dy + dx) * L + r * WIN + c
                    t = f // K2 - (2 * tile + DY * dy + DX * dx)
                    assert 0 <= t < T4
                    m[p, tile, dy, dx, t] = 1
    assert m.sum() == K2 * L
    return m.reshape(TT, NT * WCOLS)


def border_plan():
    left = [0] + [(WIN - i + (i - 1) // WS) * SIDE + (i - 1) % WS for i in range(1, WIN)]
    right = [(WIN - 2 - i + i // WS) * SIDE + i % WS + 1 for i in range(WIN - 1)]
    right.append((SIDE - 1) * SIDE + WS)
    top = [K2 * i for i in range(WIN)]
    bottom = [K2 * i + WIN for i in range(WIN)]
    plan = []
    for side, starts in enumerate((left, right, top, bottom)):
        order = list(range(WIN))[::-1] if side < 2 else list(range(WIN))
        for half in range(2):
            at = order[half * BH:(half + 1) * BH]
            corner = None if side < 2 else (0, BH - 1)[half]
            plan.append((side, at, [starts[i] for i in at], corner))
    return plan


def runs(starts):
    out, i = [], 0
    while i < len(starts):
        n, step = 1, 0
        if i + 1 < len(starts) and starts[i + 1] > starts[i]:
            step = starts[i + 1] - starts[i]
            while i + n < len(starts) and starts[i + n] == starts[i] + n * step:
                n += 1
        out.append((i, starts[i], step, n))
        i += n
    return out


def hybrid_kernel(nc, x, qkv0_t, qkv0_b, proj0_t, proj0_b, rel_bias, w_qkv, b_qkv, w_proj, b_proj,
                  router_t, w1, b1, w2, b2, ident_in, ident_b_in, group_in, nmask_in, causal_q_in,
                  causal_k_in, out):
    dram = lambda name, shape, dt: nc.dram_tensor(name, shape, dt, kind="Internal").ap()
    v_rows = dram("v_rows", [CC, TOK, 128], F32)
    v_top = dram("v_top", [CC, L, 128], F32)
    v_bottom = dram("v_bottom", [CC, L, 128], F32)
    bias_pad = dram("bias_pad", [PADN, HEADS], F32)
    parts = dram("parts", [2, CC, 3, 128, TOK], BF16)
    resid = dram("resid", [IMAGES, TOK, CH], F32)
    normed_t = dram("normed_t", [IMAGES, CH, TOK], F32)

    ctx = ExitStack()
    sems = []

    def sem(name):
        s = ctx.enter_context(nc.semaphore(name))
        sems.append(s)
        return s

    def persist(name, shape, dt):
        return ctx.enter_context(nc.sbuf_tensor(name, shape, dt))

    with ctx:
        ps = [ctx.enter_context(nc.psum_tensor(f"bank{i}", [128, 512], F32)) for i in range(8)]
        ident = persist("ident", [128, 128], F32)
        ident_b = persist("ident_b", [128, 128], BF16)
        eps = persist("eps", [128, 1], F32)
        tiles = persist("tiles", [128, NT, CH], F32)
        wide = persist("wide", [128, CC, TOK], F32)
        stats = persist("stats", [128, NT, 2], F32)

        const_in = sem("const_in")
        const_set = sem("const_set")

        with ExitStack() as mem, nc.Block() as block:
            zero = mem.enter_context(nc.sbuf_tensor("zero", [128, 64], F32))
            inner = mem.enter_context(nc.sbuf_tensor("inner", [K2, HEADS], F32))
            zero_set = sem("zero_set")
            pad_out = sem("pad_out")
            inner_in = sem("inner_in")

            @block.gpsimd
            def _(pool):
                pool.memset(zero[:], 0.0).then_inc(zero_set, 1)
                pool.memset(eps[:], LOUD_EPS).then_inc(const_set, 1)

            @block.sync
            def _(sp):
                sp.dma_start(ident[:], ident_in).then_inc(const_in, 16)
                sp.dma_start(ident_b[:], ident_b_in).then_inc(const_in, 16)
                for ki in range(WS):
                    row = (HALF + ki) * (2 * WS - 1) + HALF
                    sp.dma_start(inner[ki * WS:(ki + 1) * WS, :], rel_bias[row:row + WS, :]).then_inc(inner_in, 16)
                sp.wait_ge(zero_set, 1)
                flat = bias_pad.rearrange("a b -> (a b)")
                n, per = PADN * HEADS, 32
                rows = n // per
                for at in range(0, rows, 128):
                    k = min(128, rows - at)
                    sp.dma_start(flat[at * per:(at + k) * per].rearrange("(p a) -> p a", p=k),
                                 zero[0:k, 0:per]).then_inc(pad_out, 16)
                rest = n - rows * per
                if rest:
                    sp.dma_start(flat[rows * per:n].rearrange("(p a) -> p a", p=1), zero[0:1, 0:rest]).then_inc(pad_out, 16)
                chunks = (rows + 127) // 128 + (1 if rest else 0)
                sp.wait_ge(pad_out, 16 * chunks)
                sp.wait_ge(inner_in, 16 * WS)
                sp.dma_start(bias_pad[TAB0:TAB0 + K2, :], inner[:]).then_inc(pad_out, 16)
                sp.wait_ge(pad_out, 16 * (chunks + 1))
                sp.wait_ge(const_in, 32)

        args = dict(nc=nc, sem=sem, ps=ps, ident=ident, ident_b=ident_b, eps=eps, tiles=tiles, wide=wide, stats=stats)
        first = len(sems)
        with nc.Fori(0, IMAGES) as image:
            neighbourhood_layer(image, x=x, qkv0_t=qkv0_t, qkv0_b=qkv0_b, proj0_t=proj0_t, proj0_b=proj0_b,
                                rel_bias=rel_bias, group_in=group_in, nmask_in=nmask_in, v_rows=v_rows,
                                v_top=v_top, v_bottom=v_bottom, bias_pad=bias_pad, **args)
            with nc.sbuf_tensor("values", [128, NT, CH], F32) as values:
                project_qkv(values=values, w_qkv=w_qkv, b_qkv=b_qkv, parts=parts, **args)
                causal_attention(values=values, parts=parts, causal_q_in=causal_q_in, causal_k_in=causal_k_in, **args)
            attention_out(image, w_proj=w_proj, b_proj=b_proj, resid=resid, normed_t=normed_t, **args)
            for s in sems[first:]:
                nc.sync.sem_clear(s)
            nc.all_engine_barrier()
        expert_layer(resid=resid, normed_t=normed_t, router_t=router_t, w1=w1, b1=b1, w2=w2, b2=b2, out=out, **args)


def neighbourhood_layer(image, nc, sem, ps, ident, ident_b, eps, tiles, wide, stats, x, qkv0_t, qkv0_b,
                        proj0_t, proj0_b, rel_bias, group_in, nmask_in, v_rows, v_top, v_bottom, bias_pad):
    plan = border_plan()
    NB = len(plan)
    ITEMS = NT + NB
    QX = BH * HC * EDGE
    QC = HC * EDGE * EDGE

    with ExitStack() as mem:
        def sb(name, shape, dt=F32):
            return mem.enter_context(nc.sbuf_tensor(name, shape, dt))

        xn = sb("xn", [128, CC, TOK])
        q_diag = sb("q_diag", [128, HC, L])
        q_border = sb("q_border", [128, 4, WIN, HC, EDGE])
        q_corner = sb("q_corner", [128, 4, HC, EDGE * EDGE])
        keys = sb("keys", [128, TOK])
        key_list = sb("key_list", [128, L])
        summed = sb("summed", [128, L])
        v_tile = sb("v_tile", [128, 4, 128])
        biased = sb("biased", [128, 2, HC * WCOLS])
        scores = sb("scores", [128, 2, HC * WCOLS])
        wqkv = sb("wqkv", [128, CC, 3 * CH])
        wproj = sb("wproj", [128, CC, CH])
        qkb = sb("qkb", [128, 2 * CC])
        vb_row = sb("vb_row", [128, CH])
        pb_row = sb("pb_row", [128, CH])
        table = sb("table", [128, TABN, HEADS])
        class_bias = sb("class_bias", [K2, K2, HEADS])
        nmask = sb("nmask", [128, NT * WCOLS], BF16)
        group = sb("group", [128, 128])
        raw = sb("raw", [128, CC, 7, 6])
        chan = sb("chan", [128, CC, 2])
        gmean = sb("gmean", [128, CC])
        dev = sb("dev", [128, CC])
        dev2 = sb("dev2", [128, CC])
        spread = sb("spread", [128, CC])
        std = sb("std", [128, CC])
        rstd = sb("rstd", [128, CC])
        t_raw = sb("t_raw", [128, NT, 6])

        tiles_flat = tiles[:].rearrange("p a b -> p (a b)")
        v_border = [tiles_flat[:, i * BH * 128:(i + 1) * BH * 128].rearrange("p (a b) -> p a b", b=128) for i in range(2)]
        queries = tiles_flat[:, BH * 128:BH * 128 + TOK]
        q_grid = queries.rearrange("p (a b) -> p a b", b=SIDE)
        k_grid = keys[:].rearrange("p (a b) -> p a b", b=SIDE)
        o_grid = wide[:].rearrange("p c (a b) -> p c a b", b=SIDE)
        x_again = q_diag[:].rearrange("p a b -> p (a b)")[:, 0:CC * TOK].rearrange("p (c t) -> p c t", c=CC)

        x_in, w_in, tab_in, class_in = sem("x_in"), sem("w_in"), sem("tab_in"), sem("class_in")
        cleared, summed_clear = sem("cleared"), sem("summed_clear")
        raw_done, chan_done, gm_ready, gm_copied = sem("raw_done"), sem("chan_done"), sem("gm_ready"), sem("gm_copied")
        dev_done, gv_ready, std_done, xn_ready = sem("dev_done"), sem("gv_ready"), sem("std_done"), sem("xn_ready")
        qk_ready, q_evac, k_evac = sem("qk_ready"), sem("q_evac"), sem("k_evac")
        diag_done, border_q_done, list_done = sem("diag_done"), sem("border_q_done"), sem("list_done")
        v_ready, v_evac, v_unfolded = sem("v_ready"), sem("v_evac"), sem("v_unfolded")
        v_out = [sem(f"v_out{i}") for i in range(4)]
        vb_in = [sem("vb_in0"), sem("vb_in1")]
        s_ready, bias_done, mask_done, border_done = sem("s_ready"), sem("bias_done"), sem("mask_done"), sem("border_done")
        o_ready, o_used, summed_done, placed = sem("o_ready"), sem("o_used"), sem("summed_done"), sem("placed")
        xres_in, p_ready, p_done, ts_done = sem("xres_in"), sem("p_ready"), sem("p_done"), sem("ts_done")

        def mains(n):
            return (n // ITEMS) * NT + min(n % ITEMS, NT)

        def borders(n):
            return n - mains(n)

        loads, reached, count = [], [], [0, 0]
        for k in range(CC * NB):
            side, at, starts, corner = plan[k % NB]
            loads.append(runs(starts))
            count[k % 2] += 16 * len(loads[-1])
            reached.append(count[k % 2])

        block = mem.enter_context(nc.Block())

        @block.sync
        def _(sp):
            for c in range(CC):
                sp.dma_start(wide[:, c, :], x[bass.ds(image * CH + c * 128, 128), :]).then_inc(x_in, 16)
            sp.dma_start(group[:], group_in).then_inc(w_in, 16)
            sp.dma_start(wqkv[:], qkv0_t.rearrange("(c p) o -> p c o", p=128)).then_inc(w_in, 16)
            with nc.allow_non_contiguous_dma(reason="a bias by channel"):
                sp.dma_start(qkb[:], qkv0_b[0:2 * CH].rearrange("(c p) -> p c", p=128)).then_inc(w_in, 16)
            sp.dma_start(vb_row[0:TT, :], qkv0_b[2 * CH:3 * CH].rearrange("(a c) -> a c", a=1).broadcast_to([TT, CH])).then_inc(w_in, 16)
            sp.dma_start(pb_row[0:TT, :], proj0_b.rearrange("(a c) -> a c", a=1).broadcast_to([TT, CH])).then_inc(w_in, 16)
            sp.dma_start(wproj[:], proj0_t.rearrange("(c p) o -> p c o", p=128)).then_inc(w_in, 16)
            for half in range(2):
                src = bass.AP(bias_pad.tensor, half * WIN * HEADS, [[HEADS, SIDE], [1, TABN * HEADS]])
                sp.dma_start(table[half * SIDE:(half + 1) * SIDE].rearrange("p a b -> p (a b)"), src).then_inc(tab_in, 16)
            sp.dma_start(nmask[0:TT, :], nmask_in).then_inc(tab_in, 16)
            for c in range(CC):
                for r in range(NT):
                    sp.wait_ge(v_evac, c * NT + r + 1)
                    sp.dma_start(v_rows[c, r * TT:(r + 1) * TT, :], v_tile[0:TT, r % 4, :]).then_inc(v_out[r % 4], 16)
                for i in range(4):
                    sp.wait_ge(v_out[i], 16 * NT // 4 * (c + 1))
                for dst, off in ((v_top, 0), (v_bottom, (WS - 1) * SIDE + WS - 1)):
                    src = bass.AP(v_rows.tensor, (c * TOK + off) * 128, [[SIDE * 128, WIN], [1, WIN * 128]])
                    sp.dma_start(dst[c].rearrange("(a b) d -> a (b d)", a=WIN), src).then_inc(v_unfolded, 16)
                sp.wait_ge(v_unfolded, 32 * (c + 1))
                for k in range(NB):
                    n, kk = c * ITEMS + NT + k, c * NB + k
                    if k >= 2:
                        sp.wait_ge(o_ready, n - 1)
                    elif k == 1:
                        sp.wait_ge(diag_done, HC * (c + 1))
                        sp.wait_ge(border_q_done, c + 1)
                    if k < 2 and c:
                        sp.wait_ge(o_ready, c * ITEMS)
                    base = (v_rows, v_rows, v_top, v_bottom)[plan[k][0]]
                    rows = TOK if plan[k][0] < 2 else L
                    for slot, start, step, cnt in loads[kk]:
                        src = bass.AP(base.tensor, (c * rows + start) * 128, [[128, K2], [step * 128, cnt], [1, 128]])
                        sp.dma_start(v_border[kk % 2][0:K2, slot:slot + cnt, :], src).then_inc(vb_in[kk % 2], 16)
            sp.wait_ge(s_ready, CC * ITEMS)
            for c in range(CC):
                sp.dma_start(x_again[:, c, :], x[bass.ds(image * CH + c * 128, 128), :]).then_inc(xres_in, 16)

        @block.gpsimd
        def _(pool):
            pool.memset(q_diag[:], 0.0).then_inc(cleared, 1)
            pool.memset(q_border[:], 0.0).then_inc(cleared, 1)
            pool.memset(q_corner[:], 0.0).then_inc(cleared, 1)
            for c in range(CC):
                if c:
                    pool.wait_ge(placed, c)
                pool.memset(summed[:], 0.0).then_inc(summed_clear, 1)
                pool.wait_ge(tab_in, 48)
                for r in range(NT):
                    n = c * ITEMS + r
                    pool.wait_ge(bias_done, mains(n) + 1)
                    if n >= 2:
                        pool.wait_ge(o_ready, n - 1)
                    m = nmask[0:TT, r * WCOLS:(r + 1) * WCOLS]
                    pool.tensor_tensor(scores[0:TT, n % 2, :].rearrange("p (h w) -> p h w", h=HC),
                                       biased[0:TT, n % 2, :].rearrange("p (h w) -> p h w", h=HC),
                                       bass.AP(m.tensor, m.offset, [list(m.ap[0]), [0, HC], [1, WCOLS]]),
                                       ALU.mult).then_inc(mask_done, 1)

        @block.scalar
        def _(act):
            for ih in range(WS):
                for iw in range(WS):
                    at = ih * (2 * WS - 1) + iw
                    src = bass.AP(rel_bias.tensor, at * HEADS, [[(2 * WS - 1) * HEADS, WS], [HEADS, WS], [1, HEADS]])
                    act.dma_start(class_bias[:, ih * WS + iw, :], src).then_inc(class_in, 16)
            act.wait_ge(gv_ready, 1)
            act.activation(std[:], spread[:], ACT.Sqrt, bias=eps[:, 0:1]).then_inc(std_done, 1)
            for c in range(CC):
                if c:
                    act.wait_ge(s_ready, c * ITEMS)
                for j in range(NS):
                    act.wait_ge(qk_ready, c * 2 * NS + NS + j + 1)
                    act.activation(keys[:, j * SUP:(j + 1) * SUP], ps[(c * 2 * NS + NS + j) % 4][:, 0:SUP], ACT.Identity,
                                   bias=qkb[:, CC + c:CC + c + 1]).then_inc(k_evac, 1)
                act.wait_ge(q_evac, NS * (c + 1))
                if c == 0:
                    act.wait_ge(cleared, 3)
                for h in range(HC):
                    q = slice(32 * h, 32 * h + 32)
                    act.copy(q_border[q, 0, :, h, :], q_grid[q, HALF:HALF + WIN, 0:EDGE])
                    act.copy(q_border[q, 1, :, h, :], q_grid[q, HALF:HALF + WIN, SIDE - EDGE:SIDE])
                    act.copy(q_border[q, 2, :, h, :], q_grid[q, 0:EDGE, HALF:HALF + WIN].rearrange("p a b -> p b a"))
                    act.copy(q_border[q, 3, :, h, :], q_grid[q, SIDE - EDGE:SIDE, HALF:HALF + WIN].rearrange("p a b -> p b a"))
                    for k in range(4):
                        hs, ws = (SIDE - EDGE) * (k // 2), (SIDE - EDGE) * (k % 2)
                        last = act.copy(q_corner[q, k, h, :].rearrange("p (a b) -> p a b", b=EDGE),
                                                q_grid[q, hs:hs + EDGE, ws:ws + EDGE])
                last.then_inc(border_q_done, 1)
                act.wait_ge(k_evac, NS * (c + 1))
                for side in (2, 3):
                    if side == 3:
                        act.wait_ge(s_ready, c * ITEMS + NT + 6)
                    o = (WS - 1) * (side - 2)
                    act.activation(key_list[:].rearrange("p (a b) -> p a b", b=WIN), k_grid[:, o:o + WIN, o:o + WIN],
                                   ACT.Copy).then_inc(list_done, 1)
                    if side == 2:
                        act.wait_ge(summed_done, NT * (c + 1))
                        act.activation(o_grid[:, c, HALF:HALF + WIN, HALF:HALF + WIN],
                                       summed[:].rearrange("p (a b) -> p a b", b=WIN), ACT.Copy).then_inc(placed, 1)

        @block.vector
        def _(dve):
            dve.wait_ge(x_in, 16 * CC)
            for c in range(CC):
                for j in range(NS):
                    dve.bn_stats(raw[:, c, j, :], wide[:, c, j * SUP:(j + 1) * SUP]).then_inc(raw_done, 1)
            for c in range(CC):
                dve.wait_ge(raw_done, NS * (c + 1))
                dve.bn_aggr(chan[:, c, :], raw[:, c].rearrange("p a b -> p (a b)")).then_inc(chan_done, 1)
            dve.wait_ge(gm_ready, 1)
            dve.tensor_copy(gmean[:], ps[6][:, 0:CC]).then_inc(gm_copied, 1)
            dve.wait_ge(gm_copied, 1)
            dve.wait_ge(chan_done, CC)
            dve.tensor_tensor(dev[:], chan[:, :, 0], gmean[:], ALU.subtract).then_inc(dev_done, 1)
            dve.wait_ge(dev_done, 1)
            dve.tensor_tensor(dev2[:], dev[:], dev[:], ALU.mult).then_inc(dev_done, 1)
            dve.wait_ge(dev_done, 2)
            dve.tensor_tensor(dev[:], dev2[:], chan[:, :, 1], ALU.add).then_inc(dev_done, 1)
            dve.wait_ge(gm_ready, 2)
            dve.tensor_copy(spread[:], ps[7][:, 0:CC]).then_inc(gv_ready, 1)
            dve.wait_ge(std_done, 1)
            dve.reciprocal(rstd[:], std[:]).then_inc(std_done, 1)
            dve.wait_ge(std_done, 2)
            for c in range(CC):
                dve.tensor_scalar(xn[:, c, :], wide[:, c, :], gmean[:, c:c + 1], rstd[:, c:c + 1], ALU.subtract,
                                  ALU.mult).then_inc(xn_ready, 1)
            dve.wait_ge(class_in, 16 * K2)

            def add_bias(n):
                c, i = divmod(n, ITEMS)
                dve.wait_ge(s_ready, n + 1)
                if i < NT:
                    if mains(n) >= 2:
                        dve.wait_ge(mask_done, mains(n) - 1)
                    for h in range(HC):
                        tab = table[:]
                        tab = bass.AP(tab.tensor, tab.offset + (TAB0 + 2 * i) * HEADS + c * HC + h,
                                      [[tab.ap[0][0], TT], [6 * HEADS, WS], [0, WS], [-K2 * HEADS, T4]])
                        split = lambda a: a.rearrange("p (y x t) -> p y x t", y=WS, x=WS)
                        at = h % 2 * WCOLS
                        ins = dve.tensor_tensor(split(biased[0:TT, n % 2, h * WCOLS:(h + 1) * WCOLS]),
                                                split(ps[2 * (n % 2) + h // 2][0:TT, at:at + WCOLS]), tab, ALU.add)
                    ins.then_inc(bias_done, 1)
                else:
                    side, at, starts, corner = plan[i - NT]
                    dve.wait_ge(o_ready, n - 1)
                    cb = class_bias[:]
                    k0, dk = ((HALF * WS, 1), (HALF * WS + HALF + 1, 1), (HALF, WS), ((HALF + 1) * WS + HALF, WS))[side]
                    bias = bass.AP(cb.tensor, cb.offset + k0 * HEADS + c * HC,
                                   [list(cb.ap[0]), [0, BH], [1, HC], [dk * HEADS, EDGE]])
                    sv = lambda a: a.rearrange("p (l h q) -> p l h q", l=BH, h=HC)
                    bank = ps[2 * (n % 2)]
                    ins = dve.tensor_tensor(sv(scores[0:K2, n % 2, 0:QX]), sv(bank[0:K2, 0:QX]), bias, ALU.add)
                    if corner is not None:
                        kh, kw = side - 2, 0 if corner == 0 else 1
                        k0 = kh * (HALF + 1) * WS + kw * (HALF + 1)
                        bias = bass.AP(cb.tensor, cb.offset + k0 * HEADS + c * HC,
                                       [list(cb.ap[0]), [1, HC], [WS * HEADS, EDGE], [HEADS, EDGE]])
                        sc = lambda a: a.rearrange("p (h a b) -> p h a b", h=HC, a=EDGE)
                        ins = dve.tensor_tensor(sc(scores[0:K2, n % 2, QX:QX + QC]), sc(bank[0:K2, QX:QX + QC]), bias, ALU.add)
                    ins.then_inc(border_done, 1)

            def evac_values(n):
                c, i = divmod(n, ITEMS)
                m = c * NT + i
                dve.wait_ge(v_ready, m + 1)
                if m >= 4:
                    dve.wait_ge(o_ready, c * ITEMS + i - 3)
                    dve.wait_ge(v_out[m % 4], 16 * (m // 4))
                dve.tensor_tensor(v_tile[0:TT, i % 4, :], ps[4][0:TT, 0:128], vb_row[0:TT, c * 128:(c + 1) * 128],
                                  ALU.add).then_inc(v_evac, 1)

            def take_out(n):
                c, i = divmod(n, ITEMS)
                dve.wait_ge(o_ready, n + 1)
                bank = ps[5 + n % 2]
                if i < NT:
                    if i:
                        dve.wait_ge(summed_done, c * NT + i)
                    s = summed[:]
                    win = bass.AP(s.tensor, s.offset + 2 * i, [list(s.ap[0]), [DY, WS], [DX, WS], [1, T4]])
                    o = bank[:, 0:WCOLS].rearrange("p (y x t) -> p y x t", y=WS, x=WS)
                    dve.tensor_tensor(win, o, win, ALU.add).then_inc(summed_done, 1)
                else:
                    side, at, starts, corner = plan[i - NT]
                    lo = min(at)
                    for h in range(HC):
                        q = slice(32 * h, 32 * h + 32)
                        o = bank[q, 0:QX].rearrange("p (l h q) -> p l h q", l=BH, h=HC)[:, :, h, :]
                        g = o_grid[q, c]
                        rows = slice(HALF + lo, HALF + lo + BH)
                        if side == 0:
                            dst = g[:, rows, 0:EDGE]
                        elif side == 1:
                            dst = g[:, rows, SIDE - EDGE:SIDE]
                        elif side == 2:
                            dst = g[:, 0:EDGE, rows].rearrange("p a b -> p b a")
                        else:
                            dst = g[:, SIDE - EDGE:SIDE, rows].rearrange("p a b -> p b a")
                        ins = dve.tensor_copy(dst, o)
                        if corner is not None:
                            hs, ws = (SIDE - EDGE) * (side - 2), 0 if corner == 0 else SIDE - EDGE
                            o = bank[q, QX:QX + QC].rearrange("p (h a b) -> p h a b", h=HC, a=EDGE)[:, h]
                            ins = dve.tensor_copy(g[:, hs:hs + EDGE, ws:ws + EDGE], o)
                    ins.then_inc(o_used, 1)

            for c in range(CC):
                if c:
                    dve.wait_ge(o_ready, c * ITEMS)
                for j in range(NS):
                    dve.wait_ge(qk_ready, c * 2 * NS + j + 1)
                    if j == 0:
                        dve.wait_ge(w_in, 16 * 6)
                    dve.tensor_scalar(queries[:, j * SUP:(j + 1) * SUP], ps[(c * 2 * NS + j) % 4][:, 0:SUP], qkb[:, c:c + 1],
                                      SCALE, ALU.add, ALU.mult).then_inc(q_evac, 1)
                dve.wait_ge(q_evac, NS * (c + 1))
                dve.wait_ge(cleared, 3)
                for h in range(HC):
                    q = slice(32 * h, 32 * h + 32)
                    dve.tensor_copy(q_diag[q, h, :].rearrange("p (a b) -> p a b", b=WIN),
                                    q_grid[q, HALF:HALF + WIN, HALF:HALF + WIN]).then_inc(diag_done, 1)
                dve.wait_ge(summed_clear, c + 1)
                dve.wait_ge(tab_in, 48)
                for i in range(ITEMS):
                    n = c * ITEMS + i
                    if i < NT:
                        evac_values(n)
                    add_bias(n)
                    if i:
                        take_out(n - 1)
                take_out(c * ITEMS + ITEMS - 1)
            for i in range(NT + 1):
                if i < NT:
                    dve.wait_ge(p_ready, i + 1)
                    dve.tensor_tensor(tiles[0:TT, i, :], ps[i % 4][0:TT, 0:CH], pb_row[0:TT, :], ALU.add).then_inc(p_done, 1)
                if i:
                    dve.wait_ge(p_done, i)
                    dve.bn_stats(t_raw[0:TT, i - 1, :], tiles[0:TT, i - 1, :]).then_inc(ts_done, 1)
            for i in range(NT):
                dve.wait_ge(ts_done, i + 1)
                dve.bn_aggr(stats[0:TT, i, :], t_raw[0:TT, i, :])

        @block.tensor
        def _(pe):
            pe.wait_ge(w_in, 16 * 6)
            pe.wait_ge(chan_done, CC)
            pe.matmul(ps[6][:, 0:CC], group[:], chan[:, :, 0], start=True, stop=True).then_inc(gm_ready, 1)
            pe.wait_ge(dev_done, 3)
            pe.matmul(ps[7][:, 0:CC], group[:], dev[:], start=True, stop=True).then_inc(gm_ready, 1)
            pe.wait_ge(xn_ready, CC)

            def scores_of(n):
                c, i = divmod(n, ITEMS)
                if i < NT:
                    m = c * NT + i
                    if m:
                        pe.wait_ge(v_evac, m)
                    for k in range(CC):
                        mm = pe.matmul(ps[4][0:TT, 0:128], xn[:, k, i * TT:(i + 1) * TT],
                                       wqkv[:, k, 2 * CH + c * 128:2 * CH + (c + 1) * 128], start=(k == 0), stop=(k == CC - 1))
                    mm.then_inc(v_ready, 1)
                if n >= 2:
                    pe.wait_ge(bias_done, mains(n - 1))
                    if borders(n - 1):
                        pe.wait_ge(border_done, borders(n - 1))
                if i < NT:
                    qd = q_diag[:]
                    for h in range(HC):
                        win = bass.AP(qd.tensor, qd.offset + h * L + 2 * i, [list(qd.ap[0]), [DY, WS], [DX, WS], [1, T4]])
                        at = h % 2 * WCOLS
                        mm = pe.matmul(ps[2 * (n % 2) + h // 2][0:TT, at:at + WCOLS], keys[:, i * TT:(i + 1) * TT], win,
                                       start=True, stop=True)
                    mm.then_inc(s_ready, 1)
                else:
                    side, at, starts, corner = plan[i - NT]
                    if i == NT:
                        pe.wait_ge(border_q_done, c + 1)
                    if side == 2:
                        pe.wait_ge(list_done, 2 * c + 1)
                    if side == 3:
                        pe.wait_ge(list_done, 2 * c + 2)
                    src = keys if side < 2 else key_list
                    for slot in range(BH):
                        s, col = starts[slot], (at[slot] - min(at)) * HC * EDGE
                        mm = pe.matmul(ps[2 * (n % 2)][0:K2, col:col + HC * EDGE], src[:, s:s + K2],
                                       q_border[:, side, at[slot], :, :].rearrange("p a b -> p (a b)"), start=True, stop=True)
                    if corner is not None:
                        s = starts[corner]
                        k = 2 * (side - 2) + (0 if corner == 0 else 1)
                        mm = pe.matmul(ps[2 * (n % 2)][0:K2, QX:QX + QC], src[:, s:s + K2],
                                       q_corner[:, k, :, :].rearrange("p a b -> p (a b)"), start=True, stop=True)
                    mm.then_inc(s_ready, 1)

            def weigh_values(n):
                c, i = divmod(n, ITEMS)
                if n >= 2:
                    pe.wait_ge(summed_done, mains(n - 1))
                    if borders(n - 1):
                        pe.wait_ge(o_used, borders(n - 1))
                bank = ps[5 + n % 2]
                if i < NT:
                    pe.wait_ge(mask_done, mains(n) + 1)
                    for h in range(HC):
                        mm = pe.matmul(bank[32 * h:32 * h + 32, 0:WCOLS], v_tile[0:TT, i % 4, 32 * h:32 * h + 32],
                                       scores[0:TT, n % 2, h * WCOLS:(h + 1) * WCOLS], start=True, stop=True)
                    mm.then_inc(o_ready, 1)
                else:
                    kk = c * NB + i - NT
                    side, at, starts, corner = plan[i - NT]
                    pe.wait_ge(border_done, borders(n) + 1)
                    pe.wait_ge(vb_in[kk % 2], reached[kk])
                    for slot in range(BH):
                        col = (at[slot] - min(at)) * HC * EDGE
                        cols = slice(col, col + HC * EDGE)
                        mm = pe.matmul(bank[:, cols], v_border[kk % 2][0:K2, slot, :], scores[0:K2, n % 2, cols], start=True, stop=True)
                    if corner is not None:
                        mm = pe.matmul(bank[:, QX:QX + QC], v_border[kk % 2][0:K2, corner, :], scores[0:K2, n % 2, QX:QX + QC],
                                       start=True, stop=True)
                    mm.then_inc(o_ready, 1)

            for c in range(CC):
                if c:
                    pe.wait_ge(bias_done, mains(c * ITEMS))
                    pe.wait_ge(border_done, borders(c * ITEMS))
                for m in range(2 * NS):
                    if m >= 4:
                        if m - 4 < NS:
                            pe.wait_ge(q_evac, c * NS + m - 3)
                        else:
                            pe.wait_ge(k_evac, c * NS + m - 3 - NS)
                    kind, j = divmod(m, NS)
                    bank = ps[(c * 2 * NS + m) % 4]
                    for k in range(CC):
                        mm = pe.matmul(bank[:, 0:SUP], wqkv[:, k, kind * CH + c * 128:kind * CH + (c + 1) * 128],
                                       xn[:, k, j * SUP:(j + 1) * SUP], start=(k == 0), stop=(k == CC - 1))
                    mm.then_inc(qk_ready, 1)
                pe.wait_ge(k_evac, NS * (c + 1))
                pe.wait_ge(q_evac, NS * (c + 1))
                pe.wait_ge(diag_done, HC * (c + 1))
                for i in range(ITEMS):
                    scores_of(c * ITEMS + i)
                    if i:
                        weigh_values(c * ITEMS + i - 1)
                weigh_values(c * ITEMS + ITEMS - 1)
            pe.wait_ge(o_used, CC * NB)
            pe.wait_ge(placed, CC)
            pe.wait_ge(xres_in, 16 * CC)
            for i in range(NT):
                if i >= 4:
                    pe.wait_ge(p_done, i - 3)
                bank = ps[i % 4]
                pe.matmul(bank[0:TT, 0:CH], wide[:, 0, i * TT:(i + 1) * TT], wproj[:, 0, :], start=True, stop=False)
                for c in range(CC):
                    pe.matmul(bank[0:TT, c * 128:(c + 1) * 128], x_again[:, c, i * TT:(i + 1) * TT], ident[:],
                              start=False, stop=False, skip_group_check=True)
                mm = pe.matmul(bank[0:TT, 0:CH], wide[:, 1, i * TT:(i + 1) * TT], wproj[:, 1, :], start=False, stop=True)
                mm.then_inc(p_ready, 1)


def project_qkv(nc, sem, ps, ident, ident_b, eps, tiles, wide, stats, values, w_qkv, b_qkv, parts):
    with ExitStack() as mem:
        def sb(name, shape, dt=F32):
            return mem.enter_context(nc.sbuf_tensor(name, shape, dt))

        w = sb("w1_qkv", [128, CC, 3 * CH])
        qkb = sb("b1_qk", [128, 2 * CC])
        vb_row = sb("vb1_row", [128, CH])
        std = sb("std1", [128, NT])
        rstd = sb("rstd1", [128, NT])
        xhat = sb("xhat", [128, 4, CH])
        full = sb("full", [128, 4, SUP])
        rest = sb("rest", [128, 4, SUP])
        split = sb("split", [128, 4, 3, SUP], BF16)

        w_in, std_done, rstd_done, xhat_done = sem("b_w_in"), sem("b_std_done"), sem("b_rstd_done"), sem("b_xhat_done")
        turned, turned_evac = sem("b_turned"), sem("b_turned_evac")
        qk_ready, full_done, hi_done, rest_done = sem("b_qk_ready"), sem("b_full_done"), sem("b_hi_done"), sem("b_rest_done")
        mid_done, lo_done = sem("b_mid_done"), sem("b_lo_done")
        parts_out = [sem(f"b_parts_out{i}") for i in range(4)]
        v_ready, v_evac = sem("b_v_ready"), sem("b_v_evac")
        UNITS = 2 * CC * NS

        def unit(m):
            kind, rem = divmod(m, CC * NS)
            return kind, rem // NS, rem % NS

        block = mem.enter_context(nc.Block())

        @block.sync
        def _(sp):
            sp.dma_start(w[:], w_qkv.rearrange("(c p) o -> p c o", p=128)).then_inc(w_in, 16)
            with nc.allow_non_contiguous_dma(reason="a bias by channel"):
                sp.dma_start(qkb[:], b_qkv[0:2 * CH].rearrange("(c p) -> p c", p=128)).then_inc(w_in, 16)
            sp.dma_start(vb_row[0:TT, :], b_qkv[2 * CH:3 * CH].rearrange("(a c) -> a c", a=1).broadcast_to([TT, CH])).then_inc(w_in, 16)
            for m in range(UNITS):
                kind, c, j = unit(m)
                sp.wait_ge(lo_done, m + 1)
                sp.wait_ge(mid_done, m + 1)
                sp.dma_start(parts[kind, c, :, :, j * SUP:(j + 1) * SUP].rearrange("s p t -> p s t"), split[:, m % 4]).then_inc(parts_out[m % 4], 16)
            for i in range(4):
                sp.wait_ge(parts_out[i], 16 * UNITS // 4)

        @block.scalar
        def _(act):
            act.activation(std[0:TT, :], stats[0:TT, :, 1], ACT.Sqrt, bias=eps[0:TT, 0:1]).then_inc(std_done, 1)
            for i in range(NT):
                act.wait_ge(turned, i + 1)
                act.activation(wide[:, :, i * TT:(i + 1) * TT], ps[i % 4][:, 0:2 * TT].rearrange("p (c t) -> p c t", c=CC),
                               ACT.Copy).then_inc(turned_evac, 1)
            for m in range(UNITS + 1):
                if m < UNITS:
                    act.wait_ge(full_done, m + 1)
                    if m >= 4:
                        act.wait_ge(parts_out[m % 4], 16 * (m // 4))
                    act.activation(split[:, m % 4, 0, :], full[:, m % 4, :], ACT.Copy).then_inc(hi_done, 1)
                if m:
                    act.wait_ge(rest_done, m)
                    act.activation(split[:, (m - 1) % 4, 1, :], rest[:, (m - 1) % 4, :], ACT.Copy).then_inc(mid_done, 1)

        @block.gpsimd
        def _(pool):
            for m in range(UNITS):
                pool.wait_ge(mid_done, m + 1)
                pool.tensor_tensor(split[:, m % 4, 2, :], rest[:, m % 4, :], split[:, m % 4, 1, :], ALU.subtract).then_inc(lo_done, 1)

        @block.vector
        def _(dve):
            dve.wait_ge(std_done, 1)
            dve.reciprocal(rstd[0:TT, :], std[0:TT, :]).then_inc(rstd_done, 1)
            dve.wait_ge(rstd_done, 1)
            for i in range(NT):
                if i >= 4:
                    dve.wait_ge(turned, i - 3)
                dve.tensor_scalar(xhat[0:TT, i % 4, :], tiles[0:TT, i, :], stats[0:TT, i, 0:1], rstd[0:TT, i:i + 1],
                                  ALU.subtract, ALU.mult).then_inc(xhat_done, 1)
            dve.wait_ge(w_in, 48)
            for m in range(UNITS + 1):
                if m < UNITS:
                    kind, c, j = unit(m)
                    dve.wait_ge(qk_ready, m + 1)
                    if m >= 4:
                        dve.wait_ge(hi_done, m - 3)
                        dve.wait_ge(rest_done, m - 3)
                    bias = qkb[:, kind * CC + c:kind * CC + c + 1]
                    dve.tensor_scalar(full[:, m % 4, :], ps[m % 4][:, 0:SUP], bias, SCALE if kind == 0 else 1.0,
                                      ALU.add, ALU.mult).then_inc(full_done, 1)
                if m:
                    k = m - 1
                    dve.wait_ge(hi_done, k + 1)
                    if k >= 4:
                        dve.wait_ge(lo_done, k - 3)
                    dve.tensor_tensor(rest[:, k % 4, :], full[:, k % 4, :], split[:, k % 4, 0, :], ALU.subtract).then_inc(rest_done, 1)
            for i in range(NT):
                dve.wait_ge(v_ready, i + 1)
                dve.tensor_tensor(values[0:TT, i, :], ps[4 + i % 4][0:TT, 0:CH], vb_row[0:TT, :], ALU.add).then_inc(v_evac, 1)

        @block.tensor
        def _(pe):
            for i in range(NT):
                pe.wait_ge(xhat_done, i + 1)
                if i >= 4:
                    pe.wait_ge(turned_evac, i - 3)
                for c in range(CC):
                    mm = pe.transpose(ps[i % 4][:, c * TT:(c + 1) * TT], xhat[0:TT, i % 4, c * 128:(c + 1) * 128], ident[0:TT, 0:TT])
                mm.then_inc(turned, 1)
            pe.wait_ge(turned_evac, NT)
            pe.wait_ge(w_in, 48)
            for m in range(UNITS):
                kind, c, j = unit(m)
                if m >= 4:
                    pe.wait_ge(full_done, m - 3)
                for k in range(CC):
                    mm = pe.matmul(ps[m % 4][:, 0:SUP], w[:, k, kind * CH + c * 128:kind * CH + (c + 1) * 128],
                                   wide[:, k, j * SUP:(j + 1) * SUP], start=(k == 0), stop=(k == CC - 1))
                mm.then_inc(qk_ready, 1)
            for i in range(NT):
                if i >= 4:
                    pe.wait_ge(v_evac, i - 3)
                for k in range(CC):
                    mm = pe.matmul(ps[4 + i % 4][0:TT, 0:CH], wide[:, k, i * TT:(i + 1) * TT], w[:, k, 2 * CH:3 * CH],
                                   start=(k == 0), stop=(k == CC - 1))
                mm.then_inc(v_ready, 1)


def causal_attention(nc, sem, ps, ident, ident_b, eps, tiles, wide, stats, values, parts, causal_q_in, causal_k_in):
    with ExitStack() as mem:
        def sb(name, shape, dt=F32):
            return mem.enter_context(nc.sbuf_tensor(name, shape, dt))

        q1 = [sb(f"q1_{h}", [128, TOK], BF16) for h in range(HC)]
        k1 = [sb(f"k1_{h}", [128, TOK], BF16) for h in range(HC)]
        q2 = [sb(f"q2_{h}", [65, TOK], BF16) for h in range(HC)]
        k2 = [sb(f"k2_{h}", [65, TOK], BF16) for h in range(HC)]
        probs = sb("probs", [128, 2 * HC, SUP])
        causal_q = sb("causal_q", [TT, TT], BF16)
        causal_k = sb("causal_k", [TT, TT], BF16)
        ones = sb("ones", [128, 32])
        top = sb("top", [128, HC, 4, NS])
        most = sb("most", [128, HC, 4])
        minus = sb("minus", [128, HC, 4], BF16)
        recip = sb("recip", [128, 2, SUP])

        m_in, ones_set = sem("c_m_in"), sem("c_ones_set")
        stack_in = [sem(f"c_stack_in{h}") for h in range(HC)]
        max_ready, max_done, most_done, minus_done = sem("c_max_ready"), sem("c_max_done"), sem("c_most_done"), sem("c_minus_done")
        row_ready, row_copied = sem("c_row_ready"), sem("c_row_copied")
        st_ready, exp_done, pv_done = sem("c_st_ready"), sem("c_exp_done"), sem("c_pv_done")
        sum_ready, recip_done, y_done = sem("c_sum_ready"), sem("c_recip_done"), sem("c_y_done")

        ST, MX, ROW, ACC, DEN = [0, 1, 2], [3, 4], 5, 6, 7

        def max_units(c, s):
            out = []
            for h in range(HC):
                for ii in range(4):
                    out += [("max", c, s, h, ii, kc) for kc in range(s + 1)]
                out.append(("row", c, s, h))
            return out

        def main_units(c, s):
            out = []
            for j in range(4 * s + 4):
                out += [("st", c, s, j, h) for h in range(HC)]
                if j:
                    out.append(("pv", c, s, j - 1))
            out.append(("pv", c, s, 4 * s + 3))
            return out

        order = []
        for c in range(CC):
            order += max_units(c, 0)
            for s in range(NS):
                a = main_units(c, s)
                b = max_units(c, s + 1) if s + 1 < NS else []
                na, nb = 0, 0
                while na < len(a) or nb < len(b):
                    if nb < len(b) and nb * len(a) <= na * len(b):
                        order.append(b[nb])
                        nb += 1
                    else:
                        order.append(a[na])
                        na += 1
        number = {}
        for kind in ("max", "row", "st", "pv"):
            number.update({u: n for n, u in enumerate([u for u in order if u[0] == kind])})

        block = mem.enter_context(nc.Block())

        @block.sync
        def _(sp):
            sp.dma_start(causal_q[:], causal_q_in).then_inc(m_in, 16)
            sp.dma_start(causal_k[:], causal_k_in).then_inc(m_in, 16)
            for c in range(CC):
                if c:
                    sp.wait_ge(pv_done, number[("pv", c, 0, 0)])
                for h in range(HC):
                    p = lambda kind, term: parts[kind, c, term, 32 * h:32 * h + 32, :]
                    for dst, src in ((q1[h][0:32, :], p(0, 0)), (q1[h][32:64, :], p(0, 1)), (q1[h][64:96, :], p(0, 2)),
                                     (q1[h][96:128, :], p(0, 0)), (k1[h][0:32, :], p(1, 0)), (k1[h][32:64, :], p(1, 0)),
                                     (k1[h][64:96, :], p(1, 0)), (k1[h][96:128, :], p(1, 1)), (q2[h][0:32, :], p(0, 1)),
                                     (q2[h][32:64, :], p(0, 0)), (k2[h][0:32, :], p(1, 1)), (k2[h][32:64, :], p(1, 2))):
                        sp.dma_start(dst, src).then_inc(stack_in[h], 16)

        @block.gpsimd
        def _(pool):
            pool.memset(ones[:], 1.0).then_inc(ones_set, 1)
            pool.wait_ge(ones_set, 1)
            for h in range(HC):
                pool.memset(k2[h][64:65, :], 1.0).then_inc(ones_set, 1)

        @block.scalar
        def _(act):
            for u in order:
                if u[0] == "row":
                    _, c, s, h = u
                    act.wait_ge(row_ready, number[u] + 1)
                    act.activation(q2[h][64:65, s * SUP:(s + 1) * SUP], ps[ROW][64:65, 0:SUP], ACT.Copy).then_inc(row_copied, 1)
                if u[0] == "st":
                    _, c, s, j, h = u
                    n, qs = number[u], max(0, j - 4 * s) * TT
                    act.wait_ge(st_ready, n + 1)
                    if n >= 2 * HC:
                        act.wait_ge(pv_done, n // HC - 1)
                    act.activation(probs[0:TT, n % (2 * HC), qs:SUP], ps[ST[n % 3]][0:TT, qs:SUP], ACT.Exp).then_inc(exp_done, 1)

        @block.vector
        def _(dve):
            for u in order:
                if u[0] == "max":
                    _, c, s, h, ii, kc = u
                    n = number[u]
                    cols = SUP if kc < s else (ii + 1) * TT
                    dve.wait_ge(max_ready, n + 1)
                    dve.tensor_reduce(top[0:TT, h, ii, kc:kc + 1], ps[MX[n % 2]][0:TT, 0:cols], AX.X, ALU.max).then_inc(max_done, 1)
                    if (ii, kc) == (3, s):
                        r = number[("row", c, s, h)]
                        dve.wait_ge(max_done, n + 1)
                        dve.tensor_reduce(most[0:TT, h, :], top[0:TT, h, :, 0:s + 1], AX.X, ALU.max).then_inc(most_done, 1)
                        dve.wait_ge(most_done, r + 1)
                        if r >= HC:
                            dve.wait_ge(row_ready, r - HC + 1)
                        dve.tensor_scalar(minus[0:TT, h, :], most[0:TT, h, :], -1.0, None, ALU.mult).then_inc(minus_done, 1)
                if u[0] == "pv" and u[3] == 4 * u[2] + 3:
                    _, c, s, _ = u
                    n = c * NS + s
                    dve.wait_ge(sum_ready, n + 1)
                    dve.reciprocal(recip[:, n % 2, :], ps[DEN][:, 0:SUP]).then_inc(recip_done, 1)
                    dve.wait_ge(recip_done, n + 1)
                    dve.tensor_tensor(wide[:, c, s * SUP:(s + 1) * SUP], ps[ACC][:, 0:SUP], recip[:, n % 2, :], ALU.mult).then_inc(y_done, 1)

        @block.tensor
        def _(pe):
            pe.wait_ge(m_in, 32)
            pe.wait_ge(ones_set, 1 + HC)
            seen = set()
            for u in order:
                if u[0] == "max":
                    _, c, s, h, ii, kc = u
                    n = number[u]
                    if (c, h) not in seen:
                        seen.add((c, h))
                        pe.wait_ge(stack_in[h], 16 * 12 * (c + 1))
                    if n >= 2:
                        pe.wait_ge(max_done, n - 1)
                    i = 4 * s + ii
                    cols = SUP if kc < s else (ii + 1) * TT
                    bank = ps[MX[n % 2]]
                    mm = pe.matmul(bank[0:TT, 0:cols], q1[h][:, i * TT:(i + 1) * TT], k1[h][:, kc * SUP:kc * SUP + cols],
                                   start=True, stop=(kc < s))
                    if kc == s:
                        mm = pe.matmul(bank[0:TT, ii * TT:(ii + 1) * TT], ident_b[0:TT, 0:TT], causal_q[:], start=False, stop=True)
                    mm.then_inc(max_ready, 1)
                elif u[0] == "row":
                    _, c, s, h = u
                    r = number[u]
                    pe.wait_ge(minus_done, r + 1)
                    if r:
                        pe.wait_ge(row_copied, r)
                    for ii in range(4):
                        mm = pe.matmul(ps[ROW][64:65, ii * TT:(ii + 1) * TT], minus[0:TT, h, ii:ii + 1], ident_b[0:TT, 0:TT],
                                       start=True, stop=True)
                    mm.then_inc(row_ready, 1)
                elif u[0] == "st":
                    _, c, s, j, h = u
                    n, qs = number[u], max(0, j - 4 * s) * TT
                    if j == 0:
                        pe.wait_ge(row_copied, number[("row", c, s, h)] + 1)
                    if n >= 3:
                        pe.wait_ge(exp_done, n - 2)
                    bank = ps[ST[n % 3]]
                    q = slice(s * SUP + qs, (s + 1) * SUP)
                    kt = slice(j * TT, (j + 1) * TT)
                    diag = j >= 4 * s
                    pe.matmul(bank[0:TT, qs:SUP], k1[h][:, kt], q1[h][:, q], start=True, stop=False)
                    mm = pe.matmul(bank[0:TT, qs:SUP], k2[h][:, kt], q2[h][:, q], start=False, stop=not diag)
                    if diag:
                        mm = pe.matmul(bank[0:TT, qs:qs + TT], ident_b[0:TT, 0:TT], causal_k[:], start=False, stop=True)
                    mm.then_inc(st_ready, 1)
                else:
                    _, c, s, j = u
                    n, qs = number[u], max(0, j - 4 * s) * TT
                    if j == 0 and c * NS + s:
                        pe.wait_ge(y_done, c * NS + s)
                    pe.wait_ge(exp_done, HC * (n + 1))
                    last = j == 4 * s + 3
                    for h in range(HC):
                        pr = probs[0:TT, (HC * n + h) % (2 * HC), qs:SUP]
                        o = slice(32 * h, 32 * h + 32)
                        pe.matmul(ps[ACC][o, qs:SUP], values[0:TT, j, c * 128 + 32 * h:c * 128 + 32 * h + 32], pr,
                                  start=(j == 0), stop=last, skip_group_check=True)
                    for h in range(HC):
                        pr = probs[0:TT, (HC * n + h) % (2 * HC), qs:SUP]
                        o = slice(32 * h, 32 * h + 32)
                        mm = pe.matmul(ps[DEN][o, qs:SUP], ones[0:TT, :], pr, start=(j == 0), stop=last, skip_group_check=True)
                    mm.then_inc(pv_done, 1)
                    if last:
                        pe.wait_ge(pv_done, n + 1)
                        pe.sem_inc(sum_ready, 1)


def attention_out(image, nc, sem, ps, ident, ident_b, eps, tiles, wide, stats, w_proj, b_proj, resid, normed_t):
    with ExitStack() as mem:
        def sb(name, shape, dt=F32):
            return mem.enter_context(nc.sbuf_tensor(name, shape, dt))

        w = sb("w_proj1", [128, CC, CH])
        pb_row = sb("pb1_row", [128, CH])
        raw = sb("raw2", [128, NT, 6])
        std = sb("std2", [128, NT])
        rstd = sb("rstd2", [128, NT])
        stream = sb("stream", [128, NT, CH])
        xhat = sb("xhat2", [128, 4, CH])
        both = sb("both", [128, 4, CH])
        turned_sb = sb("turned_sb", [128, 4, CC, TT])

        w_in, added, p_ready, p_done = sem("d_w_in"), sem("d_added"), sem("d_p_ready"), sem("d_p_done")
        raw_done, agg_done, std_done, rstd_done = sem("d_raw_done"), sem("d_agg_done"), sem("d_std_done"), sem("d_rstd_done")
        xhat_done, both_done, turned = sem("d_xhat_done"), sem("d_both_done"), sem("d_turned")
        resid_out = [sem(f"d_resid_out{i}") for i in range(4)]
        normed_out = [sem(f"d_normed_out{i}") for i in range(4)]
        turned_evac = sem("d_turned_evac")
        block = mem.enter_context(nc.Block())

        @block.sync
        def _(sp):
            sp.dma_start(w[:], w_proj.rearrange("(c p) o -> p c o", p=128)).then_inc(w_in, 16)
            sp.dma_start(pb_row[0:TT, :], b_proj.rearrange("(a c) -> a c", a=1).broadcast_to([TT, CH])).then_inc(w_in, 16)
            for i in range(NT):
                sp.wait_ge(both_done, i + 1)
                sp.dma_start(resid[bass.ds(image, 1), i * TT:(i + 1) * TT, :].rearrange("a t c -> (a t) c"), both[0:TT, i % 4, :]).then_inc(resid_out[i % 4], 16)
                sp.wait_ge(turned_evac, i + 1)
                sp.dma_start(normed_t[bass.ds(image, 1), :, i * TT:(i + 1) * TT].rearrange("a (c p) t -> p (a c) t", p=128),
                             turned_sb[:, i % 4]).then_inc(normed_out[i % 4], 16)
            for i in range(4):
                sp.wait_ge(resid_out[i], 16 * NT // 4)
                sp.wait_ge(normed_out[i], 16 * NT // 4)

        @block.scalar
        def _(act):
            act.wait_ge(agg_done, NT)
            act.activation(std[0:TT, :], stats[0:TT, :, 1], ACT.Sqrt, bias=eps[0:TT, 0:1]).then_inc(std_done, 1)
            for i in range(NT):
                act.wait_ge(turned, i + 1)
                if i >= 4:
                    act.wait_ge(normed_out[i % 4], 16 * (i // 4))
                act.activation(turned_sb[:, i % 4], ps[4 + i % 4][:, 0:2 * TT].rearrange("p (c t) -> p c t", c=CC),
                               ACT.Copy).then_inc(turned_evac, 1)

        @block.gpsimd
        def _(pool):
            pool.wait_ge(w_in, 32)
            for i in range(NT):
                pool.tensor_tensor(tiles[0:TT, i, :], tiles[0:TT, i, :], pb_row[0:TT, :], ALU.add).then_inc(added, 1)
            for i in range(NT):
                pool.wait_ge(xhat_done, i + 1)
                if i >= 4:
                    pool.wait_ge(resid_out[i % 4], 16 * (i // 4))
                pool.tensor_tensor(both[0:TT, i % 4, :], xhat[0:TT, i % 4, :], stream[0:TT, i, :], ALU.add).then_inc(both_done, 1)

        @block.vector
        def _(dve):
            for i in range(NT + 1):
                if i < NT:
                    dve.wait_ge(p_ready, i + 1)
                    dve.wait_ge(added, i + 1)
                    dve.tensor_tensor(stream[0:TT, i, :], ps[i % 4][0:TT, 0:CH], tiles[0:TT, i, :], ALU.add).then_inc(p_done, 1)
                if i:
                    dve.wait_ge(p_done, i)
                    dve.bn_stats(raw[0:TT, i - 1, :], stream[0:TT, i - 1, :]).then_inc(raw_done, 1)
            for i in range(NT):
                dve.wait_ge(raw_done, i + 1)
                dve.bn_aggr(stats[0:TT, i, :], raw[0:TT, i, :]).then_inc(agg_done, 1)
            dve.wait_ge(std_done, 1)
            dve.reciprocal(rstd[0:TT, :], std[0:TT, :]).then_inc(rstd_done, 1)
            dve.wait_ge(rstd_done, 1)
            for i in range(NT):
                if i >= 4:
                    dve.wait_ge(turned, i - 3)
                    dve.wait_ge(both_done, i - 3)
                dve.tensor_scalar(xhat[0:TT, i % 4, :], stream[0:TT, i, :], stats[0:TT, i, 0:1], rstd[0:TT, i:i + 1],
                                  ALU.subtract, ALU.mult).then_inc(xhat_done, 1)

        @block.tensor
        def _(pe):
            pe.wait_ge(w_in, 32)
            for i in range(NT):
                if i >= 4:
                    pe.wait_ge(p_done, i - 3)
                for c in range(CC):
                    mm = pe.matmul(ps[i % 4][0:TT, 0:CH], wide[:, c, i * TT:(i + 1) * TT], w[:, c, :], start=(c == 0), stop=(c == CC - 1))
                mm.then_inc(p_ready, 1)
            for i in range(NT):
                pe.wait_ge(xhat_done, i + 1)
                if i >= 4:
                    pe.wait_ge(turned_evac, i - 3)
                for c in range(CC):
                    mm = pe.transpose(ps[4 + i % 4][:, c * TT:(c + 1) * TT], xhat[0:TT, i % 4, c * 128:(c + 1) * 128], ident[0:TT, 0:TT])
                mm.then_inc(turned, 1)


def expert_layer(nc, sem, ps, ident, ident_b, eps, tiles, wide, stats, resid, normed_t, router_t, w1, b1, w2, b2, out):
    with ExitStack() as mem:
        def sb(name, shape, dt=F32):
            return mem.enter_context(nc.sbuf_tensor(name, shape, dt))

        w1_sb = sb("w1_sb", [128, EXPERTS, CC, CH])
        w2_sb = sb("w2_sb", [128, EXPERTS, CC, CH])
        b1_sb = sb("b1_sb", [128, EXPERTS, CC])
        b2_sb = sb("b2_sb", [EXPERTS, CH])
        rt = sb("rt", [128, CC, EXPERTS])
        xg = sb("xg", [128, CC, SUP])
        acc = sb("acc", [128, 4, CH])
        hid = sb("hid", [128, 2, CC, SUP])
        small = {n: sb("e_" + n, [128, 4, EXPERTS]) for n in ("shift", "expo", "prob", "eq", "pos", "one", "left", "eq2", "pos2", "two", "sel", "comb")}
        col = {n: sb("e_" + n, [128, 4, 1]) for n in ("mx", "sum", "rsum", "p1", "i1", "p2", "i2", "tot", "rtot")}
        iota = sb("iota", [128, 4, EXPERTS])
        comb_t = sb("comb_t", [EXPERTS, 4, TT])
        result = sb("result", [128, CC, SUP])

        wt_in, iota_set = sem("e_wt_in"), sem("e_iota_set")
        with nc.Block() as block:
            @block.sync
            def _(sp):
                sp.dma_start(w1_sb[:], w1.rearrange("e (c p) o -> p e c o", p=128)).then_inc(wt_in, 16)
                sp.dma_start(w2_sb[:], w2.rearrange("e (c p) o -> p e c o", p=128)).then_inc(wt_in, 16)
                with nc.allow_non_contiguous_dma(reason="a bias by channel"):
                    for c in range(CC):
                        sp.dma_start(b1_sb[:, :, c], b1[:, c * 128:(c + 1) * 128].rearrange("e p -> p e")).then_inc(wt_in, 16)
                sp.dma_start(b2_sb[:], b2).then_inc(wt_in, 16)
                sp.dma_start(rt[:], router_t.rearrange("(c p) e -> p c e", p=128)).then_inc(wt_in, 16)
                sp.wait_ge(wt_in, 16 * 6)

            @block.gpsimd
            def _(pool):
                for e in range(EXPERTS):
                    pool.memset(iota[:, :, e:e + 1], float(e)).then_inc(iota_set, 1)
                pool.wait_ge(iota_set, EXPERTS)

        mark = []

        def own(name):
            s = sem(name)
            mark.append(s)
            return s

        g_in, lg_ready, chain, comb_done = own("e_g_in"), own("e_lg_ready"), own("e_chain"), own("e_comb_done")
        ct_ready, ct_done, bias_ready, acc_done = own("e_ct_ready"), own("e_ct_done"), own("e_bias_ready"), own("e_acc_done")
        h_ready, h_done, y_ready, exp_done = own("e_h_ready"), own("e_h_done"), own("e_y_ready"), own("e_exp_done")
        o_turned, o_evac, o_out = own("e_o_turned"), own("e_o_evac"), own("e_o_out")

        with nc.Fori(0, IMAGES) as image, nc.Fori(0, NS) as group:
            with nc.Block() as block:
                @block.sync
                def _(sp):
                    sp.dma_start(xg[:], normed_t[bass.ds(image, 1), :, bass.ds(group * SUP, SUP)].rearrange("a (c p) t -> p (a c) t", p=128)).then_inc(g_in, 16)
                    sp.dma_start(acc[0:TT], resid[bass.ds(image, 1), bass.ds(group * SUP, SUP), :].rearrange("a (i t) c -> t (a i) c", t=TT)).then_inc(g_in, 16)
                    sp.wait_ge(o_evac, 2)
                    sp.dma_start(out[bass.ds(image, 1), :, bass.ds(group * SUP, SUP)].rearrange("a (c p) t -> p (a c) t", p=128), result[:]).then_inc(o_out, 16)
                    sp.wait_ge(o_out, 16)

                @block.scalar
                def _(act):
                    act.wait_ge(chain, 2)
                    act.activation(small["expo"][0:TT], small["shift"][0:TT], ACT.Exp).then_inc(lg_ready, 1)
                    act.wait_ge(ct_ready, 1)
                    act.activation(comb_t[:], ps[6][0:EXPERTS, 0:SUP].rearrange("e (i t) -> e i t", i=4), ACT.Copy).then_inc(ct_done, 1)
                    for e in range(EXPERTS):
                        for c in range(CC):
                            n = e * CC + c
                            act.wait_ge(h_ready, n + 1)
                            if e >= 2:
                                act.wait_ge(y_ready, 4 * (e - 1))
                            act.activation(hid[:, e % 2, c, :], ps[n % 4][:, 0:SUP], ACT.Gelu, bias=b1_sb[:, e, c:c + 1]).then_inc(h_done, 1)
                    for c in range(CC):
                        act.wait_ge(o_turned, c + 1)
                        act.activation(result[:, c, :], ps[c][:, 0:SUP], ACT.Copy).then_inc(o_evac, 1)

                @block.vector
                def _(dve):
                    count = [0]

                    def link(ins):
                        ins.then_inc(chain, 1)
                        count[0] += 1
                        dve.wait_ge(chain, count[0])

                    t = {k: v[0:TT] for k, v in (small | col).items()}
                    wide8 = lambda a: a.broadcast_to([TT, 4, EXPERTS])
                    dve.wait_ge(lg_ready, 1)
                    logits = ps[7][0:TT, 0:4 * EXPERTS].rearrange("p (i e) -> p i e", i=4)
                    link(dve.tensor_reduce(t["mx"], logits, AX.X, ALU.max))
                    link(dve.tensor_tensor(t["shift"], logits, wide8(t["mx"]), ALU.subtract))
                    dve.wait_ge(lg_ready, 2)
                    link(dve.tensor_reduce(t["sum"], t["expo"], AX.X, ALU.add))
                    link(dve.reciprocal(t["rsum"], t["sum"]))
                    link(dve.tensor_tensor(t["prob"], t["expo"], wide8(t["rsum"]), ALU.mult))
                    it = iota[0:TT]
                    for p, eq, pos, idx, best, src in (("p1", "eq", "pos", "i1", "one", "prob"), ("p2", "eq2", "pos2", "i2", "two", "left")):
                        link(dve.tensor_reduce(t[p], t[src], AX.X, ALU.max))
                        link(dve.tensor_tensor(t[eq], t[src], wide8(t[p]), ALU.is_equal))
                        link(dve.scalar_tensor_tensor(out=t[pos], in0=t[eq], scalar=-float(EXPERTS), in1=it, op0=ALU.mult, op1=ALU.add))
                        link(dve.tensor_reduce(t[idx], t[pos], AX.X, ALU.min))
                        link(dve.tensor_tensor(t[best], t[pos], wide8(t[idx]), ALU.is_equal))
                        if best == "one":
                            link(dve.scalar_tensor_tensor(out=t["left"], in0=t["one"], scalar=-2.0, in1=t["prob"], op0=ALU.mult, op1=ALU.add))
                    link(dve.tensor_tensor(t["tot"], t["p1"], t["p2"], ALU.add))
                    link(dve.tensor_scalar(t["tot"], t["tot"], 1e-12, None, ALU.max))
                    link(dve.reciprocal(t["rtot"], t["tot"]))
                    link(dve.tensor_tensor(t["sel"], t["one"], t["two"], ALU.add))
                    link(dve.tensor_tensor(t["sel"], t["sel"], t["prob"], ALU.mult))
                    dve.tensor_tensor(t["comb"], t["sel"], wide8(t["rtot"]), ALU.mult).then_inc(comb_done, 1)
                    dve.wait_ge(g_in, 32)
                    for i in range(4):
                        dve.wait_ge(bias_ready, i + 1)
                        dve.tensor_tensor(acc[0:TT, i, :], ps[4 + i % 2][0:TT, 0:CH], acc[0:TT, i, :], ALU.add).then_inc(acc_done, 1)
                    dve.wait_ge(comb_done, 1)
                    for e in range(EXPERTS):
                        for i in range(4):
                            n = 4 * e + i
                            dve.wait_ge(y_ready, n + 1)
                            dve.wait_ge(acc_done, n + 1)
                            dve.scalar_tensor_tensor(out=acc[0:TT, i, :], in0=ps[4 + n % 4][0:TT, 0:CH], scalar=t["comb"][:, i, e:e + 1],
                                                     in1=acc[0:TT, i, :], op0=ALU.mult, op1=ALU.add).then_inc(acc_done, 1)

                @block.tensor
                def _(pe):
                    pe.wait_ge(g_in, 32)
                    for i in range(4):
                        for k in range(CC):
                            mm = pe.matmul(ps[7][0:TT, i * EXPERTS:(i + 1) * EXPERTS], xg[:, k, i * TT:(i + 1) * TT], rt[:, k, :],
                                           start=(k == 0), stop=(k == CC - 1))
                    mm.then_inc(lg_ready, 1)

                    def first_layer(e):
                        for c in range(CC):
                            n = e * CC + c
                            if n >= 4:
                                pe.wait_ge(h_done, n - 3)
                            for k in range(CC):
                                mm = pe.matmul(ps[n % 4][:, 0:SUP], w1_sb[:, e, k, c * 128:(c + 1) * 128], xg[:, k, :],
                                               start=(k == 0), stop=(k == CC - 1))
                            mm.then_inc(h_ready, 1)

                    def second_layer(e):
                        pe.wait_ge(h_done, CC * (e + 1))
                        for i in range(4):
                            n = 4 * e + i
                            pe.wait_ge(acc_done, 4 if n < 4 else n + 1)
                            for k in range(CC):
                                mm = pe.matmul(ps[4 + n % 4][0:TT, 0:CH], hid[:, e % 2, k, i * TT:(i + 1) * TT], w2_sb[:, e, k, :],
                                               start=(k == 0), stop=(k == CC - 1))
                            mm.then_inc(y_ready, 1)

                    first_layer(0)
                    first_layer(1)
                    pe.wait_ge(comb_done, 1)
                    for i in range(4):
                        mm = pe.transpose(ps[6][0:EXPERTS, i * TT:(i + 1) * TT], small["comb"][0:TT, i, :], ident[0:TT, 0:TT])
                    mm.then_inc(ct_ready, 1)
                    pe.wait_ge(ct_done, 1)
                    for i in range(4):
                        if i >= 2:
                            pe.wait_ge(acc_done, i - 1)
                        pe.matmul(ps[4 + i % 2][0:TT, 0:CH], comb_t[:, i, :], b2_sb[:], start=True, stop=True).then_inc(bias_ready, 1)
                    for e in range(EXPERTS):
                        second_layer(e)
                        if e + 2 < EXPERTS:
                            first_layer(e + 2)
                    pe.wait_ge(h_done, CC * EXPERTS)
                    pe.wait_ge(acc_done, 4 * (EXPERTS + 1))
                    for c in range(CC):
                        for i in range(4):
                            mm = pe.transpose(ps[c][:, i * TT:(i + 1) * TT], acc[0:TT, i, c * 128:(c + 1) * 128], ident[0:TT, 0:TT])
                        mm.then_inc(o_turned, 1)

            for s in mark:
                nc.sync.sem_clear(s)
            nc.all_engine_barrier()


def kernel(**inputs):
    import ml_dtypes as _ml
    import numpy as _np
    import concourse.bacc as _bacc
    from concourse import mybir as _mybir
    from concourse.bass_utils import run_bass_kernel_spmd as _run

    a = {k: _np.asarray(v) for k, v in inputs.items()}
    bf16 = _ml.bfloat16
    rows = _np.arange(TT)
    lane = _np.arange(128)
    behind = _np.where(rows[None, :] > rows[:, None], NEG, 0.0)
    arrays = {
        "x": a["x"].reshape(IMAGES * CH, TOK),
        "qkv0_t": a["L0_conv_qkv_w"].T, "qkv0_b": a["L0_conv_qkv_b"],
        "proj0_t": a["L0_conv_proj_w"].T, "proj0_b": a["L0_conv_proj_b"],
        "rel_bias": a["L0_conv_relative_bias"],
        "w_qkv": a["L1_attn_w_qkv"], "b_qkv": a["L1_attn_b_qkv"],
        "w_proj": a["L1_attn_w_proj"], "b_proj": a["L1_attn_b_proj"],
        "router_t": a["L1_ffn_router_w"].T,
        "w1": a["L1_ffn_w1"], "b1": a["L1_ffn_b1"], "w2": a["L1_ffn_w2"], "b2": a["L1_ffn_b2"],
        "ident_in": _np.eye(128, dtype=_np.float32),
        "ident_b_in": _np.eye(128).astype(bf16),
        "group_in": (lane[:, None] // 8 == lane[None, :] // 8).astype(_np.float32) / 8,
        "nmask_in": neighbourhood_mask().astype(bf16),
        "causal_q_in": behind.astype(bf16),
        "causal_k_in": _np.ascontiguousarray(behind.T).astype(bf16),
    }
    arrays = {f"in_{k}": _np.ascontiguousarray(v) for k, v in arrays.items()}
    nc = _bacc.Bacc("TRN2", target_bir_lowering=False, num_devices=1)
    args = [nc.dram_tensor(k, v.shape, _mybir.dt.from_np(v.dtype), kind="ExternalInput").ap() for k, v in arrays.items()]
    args.append(nc.dram_tensor("out_dram", (IMAGES, CH, TOK), F32, kind="ExternalOutput").ap())
    hybrid_kernel(nc, *args)
    r = _run(nc, [arrays], core_ids=[0])
    return r.results[0]["out_dram"].reshape(IMAGES, CH, SIDE, SIDE)
```

```python
from contextlib import ExitStack

import numpy as np

import concourse.bass as bass
from concourse import mybir

F32 = mybir.dt.float32
BF16 = mybir.dt.bfloat16
F16 = mybir.dt.float16
ALU = mybir.AluOpType
ACT = mybir.ActivationFunctionType
AX = mybir.AxisListType

IMAGES, CH, SIDE = 2, 256, 56
TOK = SIDE * SIDE
HEADS, HD = 8, 32
CC = CH // 128
HC = HEADS // CC
TT = 2 * SIDE
NT = TOK // TT
SUP = 4 * TT
NS = TOK // SUP
SCALE = float(HD) ** -0.5

WS = 7
K2 = WS * WS
WIN = SIDE - WS + 1
L = WIN * WIN
HALF = WS // 2
DY, DX, T4 = 356, 51, 4
WCOLS = WS * WS * T4
TAB0 = 147
TABN = TAB0 + 2 * (NT - 1) + 6 * (WS - 1) + 1
PADN = TABN + WIN + SIDE + 2
EDGE = 3
BH = WIN // 2

NEG = -1e30
EPS = 1e-5
SPLIT_MAX = 4096.0
ROW_UNIT = 16384.0
MAX_BANKS, MAX_SLOTS = 1, 3
EXPERTS = 8


def neighbourhood_mask():
    m = np.zeros((TT, NT, WS, WS, T4), np.uint8)
    for tile in range(NT):
        for dy in range(WS):
            for dx in range(WS):
                for p in range(TT):
                    r, c = 2 * tile + p // SIDE - dy, p % SIDE - dx
                    if not (0 <= r < WIN and 0 <= c < WIN):
                        continue
                    f = (WS * dy + dx) * L + r * WIN + c
                    t = f // K2 - (2 * tile + DY * dy + DX * dx)
                    assert 0 <= t < T4
                    m[p, tile, dy, dx, t] = 1
    assert m.sum() == K2 * L
    return m.reshape(TT, NT * WCOLS)


def border_plan():
    left = [0] + [(WIN - i + (i - 1) // WS) * SIDE + (i - 1) % WS for i in range(1, WIN)]
    right = [(WIN - 2 - i + i // WS) * SIDE + i % WS + 1 for i in range(WIN - 1)]
    right.append((SIDE - 1) * SIDE + WS)
    top = [K2 * i for i in range(WIN)]
    bottom = [K2 * i + WIN for i in range(WIN)]
    plan = []
    for side, starts in enumerate((left, right, top, bottom)):
        order = list(range(WIN))[::-1] if side < 2 else list(range(WIN))
        for half in range(2):
            at = order[half * BH:(half + 1) * BH]
            corner = None if side < 2 else (0, BH - 1)[half]
            plan.append((side, at, [starts[i] for i in at], corner))
    return plan


def runs(starts):
    out, i = [], 0
    while i < len(starts):
        n, step = 1, 0
        if i + 1 < len(starts) and starts[i + 1] > starts[i]:
            step = starts[i + 1] - starts[i]
            while i + n < len(starts) and starts[i + n] == starts[i] + n * step:
                n += 1
        out.append((i, starts[i], step, n))
        i += n
    return out


def hybrid_kernel(nc, x, qkv0_t, qkv0_b, proj0_t, proj0_b, rel_bias, w_qkv, b_qkv, w_proj, b_proj,
                  router_t, w1, b1, w2, b2, ident_in, ident_b_in, group_in, nmask_in, causal_q_in,
                  causal_k_in, out):
    dram = lambda name, shape, dt: nc.dram_tensor(name, shape, dt, kind="Internal").ap()
    v_rows = dram("v_rows", [CC, TOK, 128], F32)
    v_top = dram("v_top", [CC, L, 128], F32)
    v_bottom = dram("v_bottom", [CC, L, 128], F32)
    bias_pad = dram("bias_pad", [PADN, HEADS], F32)
    parts = dram("parts", [2, CC, 2, 128, TOK], F16)
    stream_rows = dram("stream_rows", [TOK, CH], F32)
    v1_rows = dram("v1_rows", [TOK, CH], F32)
    resid = dram("resid", [IMAGES, TOK, CH], F32)
    normed_t = dram("normed_t", [IMAGES, CH, TOK], F32)

    ctx = ExitStack()
    sems = []

    def sem(name):
        s = ctx.enter_context(nc.semaphore(name))
        sems.append(s)
        return s

    def persist(name, shape, dt):
        return ctx.enter_context(nc.sbuf_tensor(name, shape, dt))

    with ctx:
        banks = ctx.enter_context(nc.psum_tensor("banks", [128, 8, 512], F32))
        ps = [banks[:, i, :] for i in range(8)]
        ident = persist("ident", [128, 128], F32)
        ident_b = persist("ident_b", [128, 128], BF16)
        eps = persist("eps", [128, 1], F32)
        wide = persist("wide", [128, CC, TOK], F32)
        stats = persist("stats", [128, NT, 2], F32)
        exp_scale = persist("exp_scale", [128, 1], F32)

        const_in = sem("const_in")
        const_set = sem("const_set")

        with ExitStack() as mem, nc.Block() as block:
            zero = mem.enter_context(nc.sbuf_tensor("zero", [128, 64], F32))
            inner = mem.enter_context(nc.sbuf_tensor("inner", [K2, HEADS], F32))
            zero_set = sem("zero_set")
            pad_out = sem("pad_out")
            inner_in = sem("inner_in")

            @block.gpsimd
            def _(pool):
                pool.memset(zero[:], 0.0).then_inc(zero_set, 1)
                pool.memset(eps[:], EPS).then_inc(const_set, 1)

            @block.sync
            def _(sp):
                sp.dma_start(ident[:], ident_in).then_inc(const_in, 16)
                sp.dma_start(ident_b[:], ident_b_in).then_inc(const_in, 16)
                for ki in range(WS):
                    row = (HALF + ki) * (2 * WS - 1) + HALF
                    sp.dma_start(inner[ki * WS:(ki + 1) * WS, :], rel_bias[row:row + WS, :]).then_inc(inner_in, 16)
                sp.wait_ge(zero_set, 1)
                flat = bias_pad.rearrange("a b -> (a b)")
                n, per = PADN * HEADS, 32
                rows = n // per
                for at in range(0, rows, 128):
                    k = min(128, rows - at)
                    sp.dma_start(flat[at * per:(at + k) * per].rearrange("(p a) -> p a", p=k),
                                 zero[0:k, 0:per]).then_inc(pad_out, 16)
                rest = n - rows * per
                if rest:
                    sp.dma_start(flat[rows * per:n].rearrange("(p a) -> p a", p=1), zero[0:1, 0:rest]).then_inc(pad_out, 16)
                chunks = (rows + 127) // 128 + (1 if rest else 0)
                sp.wait_ge(pad_out, 16 * chunks)
                sp.wait_ge(inner_in, 16 * WS)
                sp.dma_start(bias_pad[TAB0:TAB0 + K2, :], inner[:]).then_inc(pad_out, 16)
                sp.wait_ge(pad_out, 16 * (chunks + 1))
                sp.wait_ge(const_in, 32)

        args = dict(nc=nc, sem=sem, ps=ps, ident=ident, ident_b=ident_b, eps=eps, wide=wide, stats=stats)
        first = len(sems)
        with nc.Fori(0, IMAGES) as image:
            with nc.sbuf_tensor("tiles", [128, NT, CH], F32) as tiles:
                neighbourhood_layer(image, tiles=tiles, x=x, qkv0_t=qkv0_t, qkv0_b=qkv0_b, proj0_t=proj0_t, proj0_b=proj0_b,
                                    rel_bias=rel_bias, group_in=group_in, nmask_in=nmask_in, v_rows=v_rows,
                                    v_top=v_top, v_bottom=v_bottom, bias_pad=bias_pad, **args)
                project_qkv(tiles=tiles, exp_scale=exp_scale, w_qkv=w_qkv, b_qkv=b_qkv, parts=parts,
                            stream_rows=stream_rows, v1_rows=v1_rows, **args)
            causal_attention(banks=banks, exp_scale=exp_scale, v1_rows=v1_rows, parts=parts, causal_q_in=causal_q_in,
                             causal_k_in=causal_k_in, **args)
            attention_out(image, stream_rows=stream_rows, w_proj=w_proj, b_proj=b_proj, resid=resid, normed_t=normed_t, **args)
            for s in sems[first:]:
                nc.sync.sem_clear(s)
            nc.all_engine_barrier()
        expert_layer(resid=resid, normed_t=normed_t, router_t=router_t, w1=w1, b1=b1, w2=w2, b2=b2, out=out, **args)


def neighbourhood_layer(image, nc, sem, ps, ident, ident_b, eps, wide, stats, tiles, x, qkv0_t, qkv0_b,
                        proj0_t, proj0_b, rel_bias, group_in, nmask_in, v_rows, v_top, v_bottom, bias_pad):
    plan = border_plan()
    NB = len(plan)
    ITEMS = NT + NB
    QX = BH * HC * EDGE
    QC = HC * EDGE * EDGE

    with ExitStack() as mem:
        def sb(name, shape, dt=F32):
            return mem.enter_context(nc.sbuf_tensor(name, shape, dt))

        xn = sb("xn", [128, CC, TOK])
        q_diag = sb("q_diag", [128, HC, L])
        q_border = sb("q_border", [128, 4, WIN, HC, EDGE])
        q_corner = sb("q_corner", [128, 4, HC, EDGE * EDGE])
        keys = sb("keys", [128, TOK])
        key_list = sb("key_list", [128, L])
        summed = sb("summed", [128, L])
        v_tile = sb("v_tile", [128, 4, 128])
        biased = sb("biased", [128, 2, HC * WCOLS])
        scores = sb("scores", [128, 2, HC * WCOLS])
        wqkv = sb("wqkv", [128, CC, 3 * CH])
        wproj = sb("wproj", [128, CC, CH])
        qkb = sb("qkb", [128, 2 * CC])
        vb_row = sb("vb_row", [128, CH])
        pb_row = sb("pb_row", [128, CH])
        table = sb("table", [128, TABN, HEADS])
        class_bias = sb("class_bias", [K2, K2, HEADS])
        nmask = sb("nmask", [128, NT * WCOLS], BF16)
        group = sb("group", [128, 128])
        raw = sb("raw", [128, CC, 7, 6])
        chan = sb("chan", [128, CC, 2])
        gmean = sb("gmean", [128, CC])
        dev = sb("dev", [128, CC])
        dev2 = sb("dev2", [128, CC])
        spread = sb("spread", [128, CC])
        std = sb("std", [128, CC])
        rstd = sb("rstd", [128, CC])
        t_raw = sb("t_raw", [128, NT, 6])

        tiles_flat = tiles[:].rearrange("p a b -> p (a b)")
        v_border = [tiles_flat[:, i * BH * 128:(i + 1) * BH * 128].rearrange("p (a b) -> p a b", b=128) for i in range(2)]
        queries = tiles_flat[:, BH * 128:BH * 128 + TOK]
        q_grid = queries.rearrange("p (a b) -> p a b", b=SIDE)
        k_grid = keys[:].rearrange("p (a b) -> p a b", b=SIDE)
        o_grid = wide[:].rearrange("p c (a b) -> p c a b", b=SIDE)
        x_again = q_diag[:].rearrange("p a b -> p (a b)")[:, 0:CC * TOK].rearrange("p (c t) -> p c t", c=CC)

        x_in, w_in, tab_in, class_in = sem("x_in"), sem("w_in"), sem("tab_in"), sem("class_in")
        cleared, summed_clear = sem("cleared"), sem("summed_clear")
        raw_done, chan_done, gm_ready, gm_copied = sem("raw_done"), sem("chan_done"), sem("gm_ready"), sem("gm_copied")
        dev_done, gv_ready, std_done, xn_ready = sem("dev_done"), sem("gv_ready"), sem("std_done"), sem("xn_ready")
        qk_ready, q_evac, k_evac = sem("qk_ready"), sem("q_evac"), sem("k_evac")
        diag_done, border_q_done, list_done = sem("diag_done"), sem("border_q_done"), sem("list_done")
        v_ready, v_evac, v_unfolded = sem("v_ready"), sem("v_evac"), sem("v_unfolded")
        v_out = [sem(f"v_out{i}") for i in range(4)]
        vb_in = [sem("vb_in0"), sem("vb_in1")]
        s_ready, bias_done, mask_done, border_done = sem("s_ready"), sem("bias_done"), sem("mask_done"), sem("border_done")
        o_ready, o_used, summed_done, placed = sem("o_ready"), sem("o_used"), sem("summed_done"), sem("placed")
        xres_in, p_ready, p_done, ts_done = sem("xres_in"), sem("p_ready"), sem("p_done"), sem("ts_done")

        def mains(n):
            return (n // ITEMS) * NT + min(n % ITEMS, NT)

        def borders(n):
            return n - mains(n)

        loads, reached, count = [], [], [0, 0]
        for k in range(CC * NB):
            side, at, starts, corner = plan[k % NB]
            loads.append(runs(starts))
            count[k % 2] += 16 * len(loads[-1])
            reached.append(count[k % 2])

        block = mem.enter_context(nc.Block())

        @block.sync
        def _(sp):
            for c in range(CC):
                sp.dma_start(wide[:, c, :], x[bass.ds(image * CH + c * 128, 128), :]).then_inc(x_in, 16)
            sp.dma_start(group[:], group_in).then_inc(w_in, 16)
            sp.dma_start(wqkv[:], qkv0_t.rearrange("(c p) o -> p c o", p=128)).then_inc(w_in, 16)
            with nc.allow_non_contiguous_dma(reason="a bias by channel"):
                sp.dma_start(qkb[:], qkv0_b[0:2 * CH].rearrange("(c p) -> p c", p=128)).then_inc(w_in, 16)
            sp.dma_start(vb_row[0:TT, :], qkv0_b[2 * CH:3 * CH].rearrange("(a c) -> a c", a=1).broadcast_to([TT, CH])).then_inc(w_in, 16)
            sp.dma_start(pb_row[0:TT, :], proj0_b.rearrange("(a c) -> a c", a=1).broadcast_to([TT, CH])).then_inc(w_in, 16)
            sp.dma_start(wproj[:], proj0_t.rearrange("(c p) o -> p c o", p=128)).then_inc(w_in, 16)
            for half in range(2):
                src = bass.AP(bias_pad.tensor, half * WIN * HEADS, [[HEADS, SIDE], [1, TABN * HEADS]])
                sp.dma_start(table[half * SIDE:(half + 1) * SIDE].rearrange("p a b -> p (a b)"), src).then_inc(tab_in, 16)
            sp.dma_start(nmask[0:TT, :], nmask_in).then_inc(tab_in, 16)
            for c in range(CC):
                for r in range(NT):
                    sp.wait_ge(v_evac, c * NT + r + 1)
                    sp.dma_start(v_rows[c, r * TT:(r + 1) * TT, :], v_tile[0:TT, r % 4, :]).then_inc(v_out[r % 4], 16)
                for i in range(4):
                    sp.wait_ge(v_out[i], 16 * NT // 4 * (c + 1))
                for dst, off in ((v_top, 0), (v_bottom, (WS - 1) * SIDE + WS - 1)):
                    src = bass.AP(v_rows.tensor, (c * TOK + off) * 128, [[SIDE * 128, WIN], [1, WIN * 128]])
                    sp.dma_start(dst[c].rearrange("(a b) d -> a (b d)", a=WIN), src).then_inc(v_unfolded, 16)
                sp.wait_ge(v_unfolded, 32 * (c + 1))
                for k in range(NB):
                    n, kk = c * ITEMS + NT + k, c * NB + k
                    if k >= 2:
                        sp.wait_ge(o_ready, n - 1)
                    elif k == 1:
                        sp.wait_ge(diag_done, HC * (c + 1))
                        sp.wait_ge(border_q_done, c + 1)
                    if k < 2 and c:
                        sp.wait_ge(o_ready, c * ITEMS)
                    base = (v_rows, v_rows, v_top, v_bottom)[plan[k][0]]
                    rows = TOK if plan[k][0] < 2 else L
                    for slot, start, step, cnt in loads[kk]:
                        src = bass.AP(base.tensor, (c * rows + start) * 128, [[128, K2], [step * 128, cnt], [1, 128]])
                        sp.dma_start(v_border[kk % 2][0:K2, slot:slot + cnt, :], src).then_inc(vb_in[kk % 2], 16)
            sp.wait_ge(s_ready, CC * ITEMS)
            for c in range(CC):
                sp.dma_start(x_again[:, c, :], x[bass.ds(image * CH + c * 128, 128), :]).then_inc(xres_in, 16)

        @block.gpsimd
        def _(pool):
            pool.memset(q_diag[:], 0.0).then_inc(cleared, 1)
            pool.memset(q_border[:], 0.0).then_inc(cleared, 1)
            pool.memset(q_corner[:], 0.0).then_inc(cleared, 1)
            for c in range(CC):
                if c:
                    pool.wait_ge(placed, c)
                pool.memset(summed[:], 0.0).then_inc(summed_clear, 1)
                pool.wait_ge(tab_in, 48)
                for r in range(NT):
                    n = c * ITEMS + r
                    pool.wait_ge(bias_done, mains(n) + 1)
                    if n >= 2:
                        pool.wait_ge(o_ready, n - 1)
                    m = nmask[0:TT, r * WCOLS:(r + 1) * WCOLS]
                    pool.tensor_tensor(scores[0:TT, n % 2, :].rearrange("p (h w) -> p h w", h=HC),
                                       biased[0:TT, n % 2, :].rearrange("p (h w) -> p h w", h=HC),
                                       bass.AP(m.tensor, m.offset, [list(m.ap[0]), [0, HC], [1, WCOLS]]),
                                       ALU.mult).then_inc(mask_done, 1)

        @block.scalar
        def _(act):
            for ih in range(WS):
                for iw in range(WS):
                    at = ih * (2 * WS - 1) + iw
                    src = bass.AP(rel_bias.tensor, at * HEADS, [[(2 * WS - 1) * HEADS, WS], [HEADS, WS], [1, HEADS]])
                    act.dma_start(class_bias[:, ih * WS + iw, :], src).then_inc(class_in, 16)
            act.wait_ge(gv_ready, 1)
            act.activation(std[:], spread[:], ACT.Sqrt, bias=eps[:, 0:1]).then_inc(std_done, 1)
            for c in range(CC):
                if c:
                    act.wait_ge(s_ready, c * ITEMS)
                for j in range(NS):
                    act.wait_ge(qk_ready, c * 2 * NS + NS + j + 1)
                    act.activation(keys[:, j * SUP:(j + 1) * SUP], ps[(c * 2 * NS + NS + j) % 4][:, 0:SUP], ACT.Identity,
                                   bias=qkb[:, CC + c:CC + c + 1]).then_inc(k_evac, 1)
                act.wait_ge(q_evac, NS * (c + 1))
                if c == 0:
                    act.wait_ge(cleared, 3)
                for h in range(HC):
                    q = slice(32 * h, 32 * h + 32)
                    act.copy(q_border[q, 0, :, h, :], q_grid[q, HALF:HALF + WIN, 0:EDGE])
                    act.copy(q_border[q, 1, :, h, :], q_grid[q, HALF:HALF + WIN, SIDE - EDGE:SIDE])
                    act.copy(q_border[q, 2, :, h, :], q_grid[q, 0:EDGE, HALF:HALF + WIN].rearrange("p a b -> p b a"))
                    act.copy(q_border[q, 3, :, h, :], q_grid[q, SIDE - EDGE:SIDE, HALF:HALF + WIN].rearrange("p a b -> p b a"))
                    for k in range(4):
                        hs, ws = (SIDE - EDGE) * (k // 2), (SIDE - EDGE) * (k % 2)
                        last = act.copy(q_corner[q, k, h, :].rearrange("p (a b) -> p a b", b=EDGE),
                                                q_grid[q, hs:hs + EDGE, ws:ws + EDGE])
                last.then_inc(border_q_done, 1)
                act.wait_ge(k_evac, NS * (c + 1))
                for side in (2, 3):
                    if side == 3:
                        act.wait_ge(s_ready, c * ITEMS + NT + 6)
                    o = (WS - 1) * (side - 2)
                    act.activation(key_list[:].rearrange("p (a b) -> p a b", b=WIN), k_grid[:, o:o + WIN, o:o + WIN],
                                   ACT.Copy).then_inc(list_done, 1)
                    if side == 2:
                        act.wait_ge(summed_done, NT * (c + 1))
                        act.activation(o_grid[:, c, HALF:HALF + WIN, HALF:HALF + WIN],
                                       summed[:].rearrange("p (a b) -> p a b", b=WIN), ACT.Copy).then_inc(placed, 1)

        @block.vector
        def _(dve):
            dve.wait_ge(x_in, 16 * CC)
            for c in range(CC):
                for j in range(NS):
                    dve.bn_stats(raw[:, c, j, :], wide[:, c, j * SUP:(j + 1) * SUP]).then_inc(raw_done, 1)
            for c in range(CC):
                dve.wait_ge(raw_done, NS * (c + 1))
                dve.bn_aggr(chan[:, c, :], raw[:, c].rearrange("p a b -> p (a b)")).then_inc(chan_done, 1)
            dve.wait_ge(gm_ready, 1)
            dve.tensor_copy(gmean[:], ps[6][:, 0:CC]).then_inc(gm_copied, 1)
            dve.wait_ge(gm_copied, 1)
            dve.wait_ge(chan_done, CC)
            dve.tensor_tensor(dev[:], chan[:, :, 0], gmean[:], ALU.subtract).then_inc(dev_done, 1)
            dve.wait_ge(dev_done, 1)
            dve.tensor_tensor(dev2[:], dev[:], dev[:], ALU.mult).then_inc(dev_done, 1)
            dve.wait_ge(dev_done, 2)
            dve.tensor_tensor(dev[:], dev2[:], chan[:, :, 1], ALU.add).then_inc(dev_done, 1)
            dve.wait_ge(gm_ready, 2)
            dve.tensor_copy(spread[:], ps[7][:, 0:CC]).then_inc(gv_ready, 1)
            dve.wait_ge(std_done, 1)
            dve.reciprocal(rstd[:], std[:]).then_inc(std_done, 1)
            dve.wait_ge(std_done, 2)
            for c in range(CC):
                dve.tensor_scalar(xn[:, c, :], wide[:, c, :], gmean[:, c:c + 1], rstd[:, c:c + 1], ALU.subtract,
                                  ALU.mult).then_inc(xn_ready, 1)
            dve.wait_ge(class_in, 16 * K2)

            def add_bias(n):
                c, i = divmod(n, ITEMS)
                dve.wait_ge(s_ready, n + 1)
                if i < NT:
                    if mains(n) >= 2:
                        dve.wait_ge(mask_done, mains(n) - 1)
                    for h in range(HC):
                        tab = table[:]
                        tab = bass.AP(tab.tensor, tab.offset + (TAB0 + 2 * i) * HEADS + c * HC + h,
                                      [[tab.ap[0][0], TT], [6 * HEADS, WS], [0, WS], [-K2 * HEADS, T4]])
                        split = lambda a: a.rearrange("p (y x t) -> p y x t", y=WS, x=WS)
                        at = h % 2 * WCOLS
                        ins = dve.tensor_tensor(split(biased[0:TT, n % 2, h * WCOLS:(h + 1) * WCOLS]),
                                                split(ps[2 * (n % 2) + h // 2][0:TT, at:at + WCOLS]), tab, ALU.add)
                    ins.then_inc(bias_done, 1)
                else:
                    side, at, starts, corner = plan[i - NT]
                    dve.wait_ge(o_ready, n - 1)
                    cb = class_bias[:]
                    k0, dk = ((HALF * WS, 1), (HALF * WS + HALF + 1, 1), (HALF, WS), ((HALF + 1) * WS + HALF, WS))[side]
                    bias = bass.AP(cb.tensor, cb.offset + k0 * HEADS + c * HC,
                                   [list(cb.ap[0]), [0, BH], [1, HC], [dk * HEADS, EDGE]])
                    sv = lambda a: a.rearrange("p (l h q) -> p l h q", l=BH, h=HC)
                    bank = ps[2 * (n % 2)]
                    ins = dve.tensor_tensor(sv(scores[0:K2, n % 2, 0:QX]), sv(bank[0:K2, 0:QX]), bias, ALU.add)
                    if corner is not None:
                        kh, kw = side - 2, 0 if corner == 0 else 1
                        k0 = kh * (HALF + 1) * WS + kw * (HALF + 1)
                        bias = bass.AP(cb.tensor, cb.offset + k0 * HEADS + c * HC,
                                       [list(cb.ap[0]), [1, HC], [WS * HEADS, EDGE], [HEADS, EDGE]])
                        sc = lambda a: a.rearrange("p (h a b) -> p h a b", h=HC, a=EDGE)
                        ins = dve.tensor_tensor(sc(scores[0:K2, n % 2, QX:QX + QC]), sc(bank[0:K2, QX:QX + QC]), bias, ALU.add)
                    ins.then_inc(border_done, 1)

            def evac_values(n):
                c, i = divmod(n, ITEMS)
                m = c * NT + i
                dve.wait_ge(v_ready, m + 1)
                if m >= 4:
                    dve.wait_ge(o_ready, c * ITEMS + i - 3)
                    dve.wait_ge(v_out[m % 4], 16 * (m // 4))
                dve.tensor_tensor(v_tile[0:TT, i % 4, :], ps[4][0:TT, 0:128], vb_row[0:TT, c * 128:(c + 1) * 128],
                                  ALU.add).then_inc(v_evac, 1)

            def take_out(n):
                c, i = divmod(n, ITEMS)
                dve.wait_ge(o_ready, n + 1)
                bank = ps[5 + n % 2]
                if i < NT:
                    if i:
                        dve.wait_ge(summed_done, c * NT + i)
                    s = summed[:]
                    win = bass.AP(s.tensor, s.offset + 2 * i, [list(s.ap[0]), [DY, WS], [DX, WS], [1, T4]])
                    o = bank[:, 0:WCOLS].rearrange("p (y x t) -> p y x t", y=WS, x=WS)
                    dve.tensor_tensor(win, o, win, ALU.add).then_inc(summed_done, 1)
                else:
                    side, at, starts, corner = plan[i - NT]
                    lo = min(at)
                    for h in range(HC):
                        q = slice(32 * h, 32 * h + 32)
                        o = bank[q, 0:QX].rearrange("p (l h q) -> p l h q", l=BH, h=HC)[:, :, h, :]
                        g = o_grid[q, c]
                        rows = slice(HALF + lo, HALF + lo + BH)
                        if side == 0:
                            dst = g[:, rows, 0:EDGE]
                        elif side == 1:
                            dst = g[:, rows, SIDE - EDGE:SIDE]
                        elif side == 2:
                            dst = g[:, 0:EDGE, rows].rearrange("p a b -> p b a")
                        else:
                            dst = g[:, SIDE - EDGE:SIDE, rows].rearrange("p a b -> p b a")
                        ins = dve.tensor_copy(dst, o)
                        if corner is not None:
                            hs, ws = (SIDE - EDGE) * (side - 2), 0 if corner == 0 else SIDE - EDGE
                            o = bank[q, QX:QX + QC].rearrange("p (h a b) -> p h a b", h=HC, a=EDGE)[:, h]
                            ins = dve.tensor_copy(g[:, hs:hs + EDGE, ws:ws + EDGE], o)
                    ins.then_inc(o_used, 1)

            for c in range(CC):
                if c:
                    dve.wait_ge(o_ready, c * ITEMS)
                for j in range(NS):
                    dve.wait_ge(qk_ready, c * 2 * NS + j + 1)
                    if j == 0:
                        dve.wait_ge(w_in, 16 * 6)
                    dve.tensor_scalar(queries[:, j * SUP:(j + 1) * SUP], ps[(c * 2 * NS + j) % 4][:, 0:SUP], qkb[:, c:c + 1],
                                      SCALE, ALU.add, ALU.mult).then_inc(q_evac, 1)
                dve.wait_ge(q_evac, NS * (c + 1))
                dve.wait_ge(cleared, 3)
                for h in range(HC):
                    q = slice(32 * h, 32 * h + 32)
                    dve.tensor_copy(q_diag[q, h, :].rearrange("p (a b) -> p a b", b=WIN),
                                    q_grid[q, HALF:HALF + WIN, HALF:HALF + WIN]).then_inc(diag_done, 1)
                dve.wait_ge(summed_clear, c + 1)
                dve.wait_ge(tab_in, 48)
                for i in range(ITEMS):
                    n = c * ITEMS + i
                    if i < NT:
                        evac_values(n)
                    add_bias(n)
                    if i:
                        take_out(n - 1)
                take_out(c * ITEMS + ITEMS - 1)
            for i in range(NT + 1):
                if i < NT:
                    dve.wait_ge(p_ready, i + 1)
                    dve.tensor_tensor(tiles[0:TT, i, :], ps[i % 4][0:TT, 0:CH], pb_row[0:TT, :], ALU.add).then_inc(p_done, 1)
                if i:
                    dve.wait_ge(p_done, i)
                    dve.bn_stats(t_raw[0:TT, i - 1, :], tiles[0:TT, i - 1, :]).then_inc(ts_done, 1)
            for i in range(NT):
                dve.wait_ge(ts_done, i + 1)
                dve.bn_aggr(stats[0:TT, i, :], t_raw[0:TT, i, :])

        @block.tensor
        def _(pe):
            pe.wait_ge(w_in, 16 * 6)
            pe.wait_ge(chan_done, CC)
            pe.matmul(ps[6][:, 0:CC], group[:], chan[:, :, 0], start=True, stop=True).then_inc(gm_ready, 1)
            pe.wait_ge(dev_done, 3)
            pe.matmul(ps[7][:, 0:CC], group[:], dev[:], start=True, stop=True).then_inc(gm_ready, 1)
            pe.wait_ge(xn_ready, CC)

            def scores_of(n):
                c, i = divmod(n, ITEMS)
                if i < NT:
                    m = c * NT + i
                    if m:
                        pe.wait_ge(v_evac, m)
                    for k in range(CC):
                        mm = pe.matmul(ps[4][0:TT, 0:128], xn[:, k, i * TT:(i + 1) * TT],
                                       wqkv[:, k, 2 * CH + c * 128:2 * CH + (c + 1) * 128], start=(k == 0), stop=(k == CC - 1))
                    mm.then_inc(v_ready, 1)
                if n >= 2:
                    pe.wait_ge(bias_done, mains(n - 1))
                    if borders(n - 1):
                        pe.wait_ge(border_done, borders(n - 1))
                if i < NT:
                    qd = q_diag[:]
                    for h in range(HC):
                        win = bass.AP(qd.tensor, qd.offset + h * L + 2 * i, [list(qd.ap[0]), [DY, WS], [DX, WS], [1, T4]])
                        at = h % 2 * WCOLS
                        mm = pe.matmul(ps[2 * (n % 2) + h // 2][0:TT, at:at + WCOLS], keys[:, i * TT:(i + 1) * TT], win,
                                       start=True, stop=True)
                    mm.then_inc(s_ready, 1)
                else:
                    side, at, starts, corner = plan[i - NT]
                    if i == NT:
                        pe.wait_ge(border_q_done, c + 1)
                    if side == 2:
                        pe.wait_ge(list_done, 2 * c + 1)
                    if side == 3:
                        pe.wait_ge(list_done, 2 * c + 2)
                    src = keys if side < 2 else key_list
                    for slot in range(BH):
                        s, col = starts[slot], (at[slot] - min(at)) * HC * EDGE
                        mm = pe.matmul(ps[2 * (n % 2)][0:K2, col:col + HC * EDGE], src[:, s:s + K2],
                                       q_border[:, side, at[slot], :, :].rearrange("p a b -> p (a b)"), start=True, stop=True)
                    if corner is not None:
                        s = starts[corner]
                        k = 2 * (side - 2) + (0 if corner == 0 else 1)
                        mm = pe.matmul(ps[2 * (n % 2)][0:K2, QX:QX + QC], src[:, s:s + K2],
                                       q_corner[:, k, :, :].rearrange("p a b -> p (a b)"), start=True, stop=True)
                    mm.then_inc(s_ready, 1)

            def weigh_values(n):
                c, i = divmod(n, ITEMS)
                if n >= 2:
                    pe.wait_ge(summed_done, mains(n - 1))
                    if borders(n - 1):
                        pe.wait_ge(o_used, borders(n - 1))
                bank = ps[5 + n % 2]
                if i < NT:
                    pe.wait_ge(mask_done, mains(n) + 1)
                    for h in range(HC):
                        mm = pe.matmul(bank[32 * h:32 * h + 32, 0:WCOLS], v_tile[0:TT, i % 4, 32 * h:32 * h + 32],
                                       scores[0:TT, n % 2, h * WCOLS:(h + 1) * WCOLS], start=True, stop=True)
                    mm.then_inc(o_ready, 1)
                else:
                    kk = c * NB + i - NT
                    side, at, starts, corner = plan[i - NT]
                    pe.wait_ge(border_done, borders(n) + 1)
                    pe.wait_ge(vb_in[kk % 2], reached[kk])
                    for slot in range(BH):
                        col = (at[slot] - min(at)) * HC * EDGE
                        cols = slice(col, col + HC * EDGE)
                        mm = pe.matmul(bank[:, cols], v_border[kk % 2][0:K2, slot, :], scores[0:K2, n % 2, cols], start=True, stop=True)
                    if corner is not None:
                        mm = pe.matmul(bank[:, QX:QX + QC], v_border[kk % 2][0:K2, corner, :], scores[0:K2, n % 2, QX:QX + QC],
                                       start=True, stop=True)
                    mm.then_inc(o_ready, 1)

            for c in range(CC):
                if c:
                    pe.wait_ge(bias_done, mains(c * ITEMS))
                    pe.wait_ge(border_done, borders(c * ITEMS))
                for m in range(2 * NS):
                    if m >= 4:
                        if m - 4 < NS:
                            pe.wait_ge(q_evac, c * NS + m - 3)
                        else:
                            pe.wait_ge(k_evac, c * NS + m - 3 - NS)
                    kind, j = divmod(m, NS)
                    bank = ps[(c * 2 * NS + m) % 4]
                    for k in range(CC):
                        mm = pe.matmul(bank[:, 0:SUP], wqkv[:, k, kind * CH + c * 128:kind * CH + (c + 1) * 128],
                                       xn[:, k, j * SUP:(j + 1) * SUP], start=(k == 0), stop=(k == CC - 1))
                    mm.then_inc(qk_ready, 1)
                pe.wait_ge(k_evac, NS * (c + 1))
                pe.wait_ge(q_evac, NS * (c + 1))
                pe.wait_ge(diag_done, HC * (c + 1))
                for i in range(ITEMS):
                    scores_of(c * ITEMS + i)
                    if i:
                        weigh_values(c * ITEMS + i - 1)
                weigh_values(c * ITEMS + ITEMS - 1)
            pe.wait_ge(o_used, CC * NB)
            pe.wait_ge(placed, CC)
            pe.wait_ge(xres_in, 16 * CC)
            for i in range(NT):
                if i >= 4:
                    pe.wait_ge(p_done, i - 3)
                bank = ps[i % 4]
                pe.matmul(bank[0:TT, 0:CH], wide[:, 0, i * TT:(i + 1) * TT], wproj[:, 0, :], start=True, stop=False)
                for c in range(CC):
                    pe.matmul(bank[0:TT, c * 128:(c + 1) * 128], x_again[:, c, i * TT:(i + 1) * TT], ident[:],
                              start=False, stop=False, skip_group_check=True)
                mm = pe.matmul(bank[0:TT, 0:CH], wide[:, 1, i * TT:(i + 1) * TT], wproj[:, 1, :], start=False, stop=True)
                mm.then_inc(p_ready, 1)


def project_qkv(nc, sem, ps, ident, ident_b, eps, wide, stats, tiles, exp_scale, w_qkv, b_qkv, parts, stream_rows, v1_rows):
    with ExitStack() as mem:
        def sb(name, shape, dt=F32):
            return mem.enter_context(nc.sbuf_tensor(name, shape, dt))

        w = sb("w1_qkv", [128, CC, 3 * CH])
        qkb = sb("b1_qk", [128, 2 * CC])
        vb_row = sb("vb1_row", [128, CH])
        std = sb("std1", [128, NT])
        rstd = sb("rstd1", [128, NT])
        xhat = sb("xhat", [128, 4, CH])
        full = sb("full", [128, 2, CC, TOK])
        split = sb("split", [128, 4, 2, SUP], F16)
        v_tile = sb("v1_tile", [128, 4, CH])
        largest = sb("largest", [128, 2, CC * NS])
        largest_of = sb("largest_of", [128, 2])
        two = sb("two", [2, 4])
        rows2 = sb("rows2", [2, 4])
        ones2 = sb("ones2", [2, 128])
        factors = sb("factors", [128, 4])

        w_in, std_done, rstd_done, xhat_done = sem("b_w_in"), sem("b_std_done"), sem("b_rstd_done"), sem("b_xhat_done")
        turned, turned_evac, stream_out = sem("b_turned"), sem("b_turned_evac"), sem("b_stream_out")
        qk_ready, full_done, largest_done = sem("b_qk_ready"), sem("b_full_done"), sem("b_largest_done")
        across, chain, ones_set, factors_done = sem("b_across"), sem("b_chain"), sem("b_ones_set"), sem("b_factors_done")
        hi_done, lo_done = sem("b_hi_done"), sem("b_lo_done")
        parts_out = [sem(f"b_parts_out{i}") for i in range(4)]
        v_out = [sem(f"b_v_out{i}") for i in range(4)]
        v_ready, v_evac = sem("b_v_ready"), sem("b_v_evac")
        UNITS = 2 * CC * NS
        assert UNITS == NT

        def unit(m):
            kind, rem = divmod(m, CC * NS)
            return kind, rem // NS, slice(rem % NS * SUP, (rem % NS + 1) * SUP)

        block = mem.enter_context(nc.Block())

        @block.sync
        def _(sp):
            sp.dma_start(w[:], w_qkv.rearrange("(c p) o -> p c o", p=128)).then_inc(w_in, 16)
            with nc.allow_non_contiguous_dma(reason="a bias by channel"):
                sp.dma_start(qkb[:], b_qkv[0:2 * CH].rearrange("(c p) -> p c", p=128)).then_inc(w_in, 16)
            sp.dma_start(vb_row[0:TT, :], b_qkv[2 * CH:3 * CH].rearrange("(a c) -> a c", a=1).broadcast_to([TT, CH])).then_inc(w_in, 16)
            sp.dma_start(stream_rows.rearrange("(i t) c -> t i c", t=TT), tiles[0:TT]).then_inc(stream_out, 16)
            for m in range(UNITS):
                kind, c, cols = unit(m)
                sp.wait_ge(lo_done, m + 1)
                sp.dma_start(parts[kind, c, :, :, cols].rearrange("s p t -> p s t"), split[:, m % 4]).then_inc(parts_out[m % 4], 16)
                sp.wait_ge(v_evac, m + 1)
                sp.dma_start(v1_rows[m * TT:(m + 1) * TT, :], v_tile[0:TT, m % 4, :]).then_inc(v_out[m % 4], 16)
            for i in range(4):
                sp.wait_ge(parts_out[i], 16 * UNITS // 4)
                sp.wait_ge(v_out[i], 16 * UNITS // 4)
            sp.wait_ge(stream_out, 16)

        @block.gpsimd
        def _(pool):
            pool.memset(ones2[:], 1.0).then_inc(ones_set, 1)

        @block.scalar
        def _(act):
            act.activation(std[0:TT, :], stats[0:TT, :, 1], ACT.Sqrt, bias=eps[0:TT, 0:1]).then_inc(std_done, 1)
            for i in range(NT):
                act.wait_ge(turned, i + 1)
                act.activation(wide[:, :, i * TT:(i + 1) * TT], ps[i % 4][:, 0:2 * TT].rearrange("p (c t) -> p c t", c=CC),
                               ACT.Copy).then_inc(turned_evac, 1)
            act.wait_ge(factors_done, 1)
            for m in range(UNITS):
                kind, c, cols = unit(m)
                if m >= 4:
                    act.wait_ge(parts_out[m % 4], 16 * (m // 4))
                act.activation(split[:, m % 4, 0, :], full[:, kind, c, cols], ACT.Copy, scale=factors[:, kind:kind + 1]).then_inc(hi_done, 1)

        @block.vector
        def _(dve):
            count = [0]

            def link(ins):
                count[0] += 1
                ins.then_inc(chain, 1)
                dve.wait_ge(chain, count[0])

            dve.wait_ge(std_done, 1)
            dve.reciprocal(rstd[0:TT, :], std[0:TT, :]).then_inc(rstd_done, 1)
            dve.wait_ge(rstd_done, 1)
            for i in range(NT):
                if i >= 4:
                    dve.wait_ge(turned, i - 3)
                dve.tensor_scalar(xhat[0:TT, i % 4, :], tiles[0:TT, i, :], stats[0:TT, i, 0:1], rstd[0:TT, i:i + 1],
                                  ALU.subtract, ALU.mult).then_inc(xhat_done, 1)
            dve.wait_ge(w_in, 48)
            for m in range(UNITS + 1):
                if m < UNITS:
                    kind, c, cols = unit(m)
                    dve.wait_ge(qk_ready, m + 1)
                    dve.tensor_scalar(full[:, kind, c, cols], ps[m % 4][:, 0:SUP], qkb[:, kind * CC + c:kind * CC + c + 1],
                                      SCALE if kind == 0 else 1.0, ALU.add, ALU.mult).then_inc(full_done, 1)
                if m:
                    kind, c, cols = unit(m - 1)
                    dve.wait_ge(full_done, m)
                    k = (m - 1) % (CC * NS)
                    dve.tensor_reduce(largest[:, kind, k:k + 1], full[:, kind, c, cols], AX.X, ALU.max,
                                      apply_absolute_value=True).then_inc(largest_done, 1)
            dve.wait_ge(largest_done, UNITS)
            dve.tensor_reduce(largest_of[:], largest[:], AX.X, ALU.max).then_inc(largest_done, 1)
            dve.wait_ge(across, 1)
            link(dve.tensor_reduce(two[:, 0:1], ps[0][0:2, 0:128], AX.X, ALU.max))
            link(dve.tensor_scalar(two[:, 1:2], two[:, 0:1], 1e-6, None, ALU.max))
            link(dve.reciprocal(two[:, 2:3], two[:, 1:2]))
            dve.tensor_scalar(rows2[:, 0:2], ident[0:2, 0:2], two[:, 2:3], SPLIT_MAX, ALU.mult, ALU.mult)
            link(dve.tensor_scalar(rows2[:, 2:4], ident[0:2, 0:2], two[:, 1:2], 1.0 / SPLIT_MAX, ALU.mult, ALU.mult))
            dve.wait_ge(across, 2)
            dve.tensor_copy(factors[:], ps[1][:, 0:4]).then_inc(factors_done, 1)
            dve.wait_ge(factors_done, 1)
            dve.tensor_tensor(exp_scale[:], factors[:, 2:3], factors[:, 3:4], ALU.mult)
            for m in range(UNITS):
                kind, c, cols = unit(m)
                dve.wait_ge(hi_done, m + 1)
                dve.scalar_tensor_tensor(out=split[:, m % 4, 1, :], in0=full[:, kind, c, cols], scalar=factors[:, kind:kind + 1],
                                         in1=split[:, m % 4, 0, :], op0=ALU.mult, op1=ALU.subtract).then_inc(lo_done, 1)
                dve.wait_ge(v_ready, m + 1)
                if m >= 4:
                    dve.wait_ge(v_out[m % 4], 16 * (m // 4))
                dve.tensor_tensor(v_tile[0:TT, m % 4, :], ps[4 + m % 4][0:TT, 0:CH], vb_row[0:TT, :], ALU.add).then_inc(v_evac, 1)

        @block.tensor
        def _(pe):
            for i in range(NT):
                pe.wait_ge(xhat_done, i + 1)
                if i >= 4:
                    pe.wait_ge(turned_evac, i - 3)
                for c in range(CC):
                    mm = pe.transpose(ps[i % 4][:, c * TT:(c + 1) * TT], xhat[0:TT, i % 4, c * 128:(c + 1) * 128], ident[0:TT, 0:TT])
                mm.then_inc(turned, 1)
            pe.wait_ge(turned_evac, NT)
            pe.wait_ge(w_in, 48)
            for m in range(UNITS):
                kind, c, cols = unit(m)
                if m >= 4:
                    pe.wait_ge(full_done, m - 3)
                for k in range(CC):
                    mm = pe.matmul(ps[m % 4][:, 0:SUP], w[:, k, kind * CH + c * 128:kind * CH + (c + 1) * 128],
                                   wide[:, k, cols], start=(k == 0), stop=(k == CC - 1))
                mm.then_inc(qk_ready, 1)
            pe.wait_ge(largest_done, UNITS + 1)
            pe.transpose(ps[0][0:2, 0:128], largest_of[:], ident[:]).then_inc(across, 1)
            pe.wait_ge(chain, 4)
            pe.wait_ge(ones_set, 1)
            pe.matmul(ps[1][:, 0:4], ones2[:], rows2[:], start=True, stop=True).then_inc(across, 1)
            for i in range(NT):
                if i >= 4:
                    pe.wait_ge(v_evac, i - 3)
                for k in range(CC):
                    mm = pe.matmul(ps[4 + i % 4][0:TT, 0:CH], wide[:, k, i * TT:(i + 1) * TT], w[:, k, 2 * CH:3 * CH],
                                   start=(k == 0), stop=(k == CC - 1))
                mm.then_inc(v_ready, 1)


def attention_order():
    def max_units(c, s):
        out, rows = [], []
        for h in range(HC):
            for ii in range(4):
                if ii == 2:
                    out += rows
                    rows = []
                out += [("max", c, s, h, ii, kc, min(MAX_BANKS, s - kc)) for kc in range(0, s, MAX_BANKS)]
                out.append(("max", c, s, h, ii, s, 0))
            rows.append(("row", c, s, h))
        return out + rows

    def main_units(c, s):
        out, full = [], 4 * s
        for j in range(full + 4):
            out += [("st", c, s, j, 0), ("st", c, s, j, 1)]
            if j:
                out.append(("pv", c, s, j - 1))
            out += [("st", c, s, j, 2), ("st", c, s, j, 3)]
            if j >= 3 and j % 2 and j - 3 < full:
                out.append(("den", c, s, j - 3, 2))
            if j - 1 >= full:
                out.append(("den", c, s, j - 1, 1))
        out += [("pv", c, s, full + 3), ("den", c, s, full + 3, 1)]
        return out

    def cost(u):
        return max(1, u[6]) if u[0] == "max" else 1 if u[0] in ("st", "row") else 4

    steps = [(c, s) for c in range(CC) for s in range(NS)]
    maxima, mains = [max_units(*k) for k in steps], [main_units(*k) for k in steps]
    order = list(maxima[0])
    ahead = [u for units in maxima[1:] for u in units]
    given, due = 0, [0]
    for units in maxima[1:]:
        due.append(due[-1] + sum(map(cost, units)))
    emitted = 0
    for k, units in enumerate(mains):
        left = sum(map(cost, units))
        starts = []
        for later in range(k + 1, len(steps)):
            starts.append((left, due[later]))
            left += sum(map(cost, mains[later]))
        gone, base = 0, given
        for u in units:
            order.append(u)
            gone += cost(u)
            want = base + gone * max([(need - base) / work for work, need in starts], default=0)
            while emitted < len(ahead) and given < want - 1e-6:
                order.append(ahead[emitted])
                given += cost(ahead[emitted])
                emitted += 1
    return order


def causal_attention(nc, sem, ps, ident, ident_b, eps, wide, stats, banks, exp_scale, v1_rows, parts, causal_q_in, causal_k_in):
    with ExitStack() as mem:
        def sb(name, shape, dt=F32):
            return mem.enter_context(nc.sbuf_tensor(name, shape, dt))

        STEPS = 4
        qs_ = [[sb(f"q_{c}{h}", [97, TOK], F16) for h in range(HC)] for c in range(CC)]
        ks_ = [[sb(f"k_{c}{h}", [97, TOK], F16) for h in range(HC)] for c in range(CC)]
        values = sb("values", [128, NT, CH])
        probs = sb("probs", [128, STEPS * HC, SUP])
        pairs = sb("pairs", [128, HC, SUP])
        causal_q = sb("causal_q", [TT, TT], BF16)
        causal_k = sb("causal_k", [TT, TT], BF16)
        ones = sb("ones", [128, 32])
        top = sb("top", [128, HC, 4, NS])
        most = sb("most", [128, HC, 4])
        minus = sb("minus", [128, HC, 4], F16)
        recip = sb("recip", [128, SUP])

        m_in, ones_set, unit_set = sem("c_m_in"), sem("c_ones_set"), sem("c_unit_set")
        stack_in = [[sem(f"c_stack_in{c}{h}") for h in range(HC)] for c in range(CC)]
        max_ready, max_done, most_done, minus_done = sem("c_max_ready"), sem("c_max_done"), sem("c_most_done"), sem("c_minus_done")
        row_ready, row_copied = sem("c_row_ready"), sem("c_row_copied")
        st_ready, exp_done, pv_done, pair_done = sem("c_st_ready"), sem("c_exp_done"), sem("c_pv_done"), sem("c_pair_done")
        den_done, recip_done, y_done = sem("c_den_done"), sem("c_recip_done"), sem("c_y_done")

        MAXIMA = list(range(0, MAX_BANKS * MAX_SLOTS, MAX_BANKS))
        ST = list(range(MAX_BANKS * MAX_SLOTS, 6))
        ACC, DEN = 6, 7

        order = attention_order()
        number = {}
        for kind in ("max", "row", "st", "pv", "den"):
            number.update({u: n for n, u in enumerate([u for u in order if u[0] == kind])})
        wide_units = [u for u in order if u[0] in ("max", "row")]
        slot = {u: n for n, u in enumerate(wide_units)}
        paired = [u for u in order if u[0] == "den" and u[4] == 2]
        pair_no = {u: n for n, u in enumerate(paired)}
        read_by = {}
        for u in order:
            if u[0] == "den":
                for j in range(u[3], u[3] + u[4]):
                    read_by[number[("pv", u[1], u[2], j)]] = u

        def freed(eng, step):
            eng.wait_ge(pv_done, step + 1)
            u = read_by[step]
            if u[4] == 2:
                eng.wait_ge(pair_done, HC * (pair_no[u] + 1))
            else:
                eng.wait_ge(den_done, number[u] + 1)

        block = mem.enter_context(nc.Block())

        @block.sync
        def _(sp):
            sp.dma_start(causal_q[:], causal_q_in).then_inc(m_in, 16)
            sp.dma_start(causal_k[:], causal_k_in).then_inc(m_in, 16)
            for c in range(CC):
                for h in range(HC):
                    rows = slice(32 * h, 32 * h + 32)
                    for dst, kind, terms in ((qs_[c][h][0:32, :], 0, 0), (qs_[c][h][32:64, :], 0, 1), (qs_[c][h][64:96, :], 0, 0),
                                             (ks_[c][h][0:32, :], 1, 0), (ks_[c][h][32:64, :], 1, 0), (ks_[c][h][64:96, :], 1, 1)):
                        sp.dma_start(dst, parts[kind, c, terms, rows, :]).then_inc(stack_in[c][h], 16)
                if c == 0:
                    sp.dma_start(values[0:TT], v1_rows.rearrange("(i t) c -> t i c", t=TT)).then_inc(m_in, 16)

        @block.gpsimd
        def _(pool):
            pool.memset(ones[:], 1.0).then_inc(ones_set, 1)
            pool.wait_ge(ones_set, 1)
            for c in range(CC):
                for h in range(HC):
                    pool.memset(ks_[c][h][96:97, :], ROW_UNIT).then_inc(unit_set, 1)
            pool.wait_ge(unit_set, CC * HC)
            for u in paired:
                _, c, s, j, _ = u
                n, step = pair_no[u], number[("pv", c, s, j)]
                for h in range(HC):
                    pool.wait_ge(exp_done, HC * (step + 1) + h + 1)
                    if n:
                        pool.wait_ge(den_done, number[paired[n - 1]] + 1)
                    a, b = (probs[0:TT, (HC * (step + k) + h) % (STEPS * HC), :] for k in range(2))
                    pool.tensor_tensor(pairs[0:TT, h, :], a, b, ALU.add).then_inc(pair_done, 1)

        @block.scalar
        def _(act):
            for u in order:
                if u[0] == "row":
                    _, c, s, h = u
                    k = MAXIMA[slot[u] % MAX_SLOTS]
                    act.wait_ge(row_ready, number[u] + 1)
                    act.activation(qs_[c][h][96:97, s * SUP:(s + 1) * SUP], ps[k][96:97, 0:SUP], ACT.Copy).then_inc(row_copied, 1)
                if u[0] == "st":
                    _, c, s, j, h = u
                    n, at = number[u], max(0, j - 4 * s) * TT
                    act.wait_ge(st_ready, n + 1)
                    step = n // HC
                    if step >= STEPS and h == 0:
                        freed(act, step - STEPS)
                    act.activation(probs[0:TT, n % (STEPS * HC), at:SUP], ps[ST[n % len(ST)]][0:TT, at:SUP], ACT.Exp,
                                   scale=exp_scale[0:TT, 0:1]).then_inc(exp_done, 1)

        @block.vector
        def _(dve):
            for u in order:
                if u[0] == "max":
                    _, c, s, h, ii, kc, full = u
                    n, k = number[u], MAXIMA[slot[u] % MAX_SLOTS]
                    dve.wait_ge(max_ready, n + 1)
                    if full:
                        src = banks[0:TT, k:k + full, 0:SUP]
                        dve.tensor_reduce(top[0:TT, h, ii, kc // MAX_BANKS:kc // MAX_BANKS + 1], src, AX.XY, ALU.max).then_inc(max_done, 1)
                        continue
                    last = -(-s // MAX_BANKS)
                    dve.tensor_reduce(top[0:TT, h, ii, last:last + 1], ps[k][0:TT, 0:(ii + 1) * TT], AX.X, ALU.max).then_inc(max_done, 1)
                    if ii == 3:
                        r = number[("row", c, s, h)]
                        dve.wait_ge(max_done, n + 1)
                        dve.tensor_reduce(most[0:TT, h, :], top[0:TT, h, :, 0:last + 1], AX.X, ALU.max).then_inc(most_done, 1)
                        dve.wait_ge(most_done, r + 1)
                        if r >= HC:
                            dve.wait_ge(row_ready, r - HC + 1)
                        dve.tensor_scalar(minus[0:TT, h, :], most[0:TT, h, :], -1.0 / ROW_UNIT, None, ALU.mult).then_inc(minus_done, 1)
                if u[0] == "den" and u[3] == 4 * u[2] + 3:
                    _, c, s, _, _ = u
                    n = c * NS + s
                    dve.wait_ge(den_done, number[u] + 1)
                    dve.reciprocal(recip[:], ps[DEN][:, 0:SUP]).then_inc(recip_done, 1)
                    dve.wait_ge(recip_done, n + 1)
                    dve.tensor_tensor(wide[:, c, s * SUP:(s + 1) * SUP], ps[ACC][:, 0:SUP], recip[:], ALU.mult).then_inc(y_done, 1)

        @block.tensor
        def _(pe):
            pe.wait_ge(ones_set, 1)
            seen = set()
            for u in order:
                if u[0] in ("max", "row") and slot[u] >= MAX_SLOTS:
                    before = wide_units[slot[u] - MAX_SLOTS]
                    if before[0] == "max":
                        pe.wait_ge(max_done, number[before] + 1)
                    else:
                        pe.wait_ge(row_copied, number[before] + 1)
                if u[0] == "max":
                    _, c, s, h, ii, kc, full = u
                    n, k = number[u], MAXIMA[slot[u] % MAX_SLOTS]
                    if (c, h) not in seen:
                        seen.add((c, h))
                        pe.wait_ge(stack_in[c][h], 16 * 6)
                    i = 4 * s + ii
                    q = qs_[c][h][0:96, i * TT:(i + 1) * TT]
                    if full:
                        for b in range(full):
                            mm = pe.matmul(ps[k + b][0:TT, 0:SUP], q, ks_[c][h][0:96, (kc + b) * SUP:(kc + b + 1) * SUP], start=True, stop=True)
                    else:
                        if n == 0:
                            pe.wait_ge(m_in, 48)
                        pe.matmul(ps[k][0:TT, 0:(ii + 1) * TT], q, ks_[c][h][0:96, s * SUP:s * SUP + (ii + 1) * TT], start=True, stop=False)
                        mm = pe.matmul(ps[k][0:TT, ii * TT:(ii + 1) * TT], ident_b[0:TT, 0:TT], causal_q[:], start=False, stop=True)
                    mm.then_inc(max_ready, 1)
                elif u[0] == "row":
                    _, c, s, h = u
                    r, k = number[u], MAXIMA[slot[u] % MAX_SLOTS]
                    pe.wait_ge(minus_done, r + 1)
                    for ii in range(4):
                        mm = pe.matmul(ps[k][96:97, ii * TT:(ii + 1) * TT], minus[0:TT, h, ii:ii + 1], ident_b[0:TT, 0:TT],
                                       start=True, stop=True, tile_position=(0, 96))
                    mm.then_inc(row_ready, 1)
                elif u[0] == "st":
                    _, c, s, j, h = u
                    n, at = number[u], max(0, j - 4 * s) * TT
                    if j == 0:
                        pe.wait_ge(row_copied, number[("row", c, s, h)] + 1)
                        if s == 0:
                            pe.wait_ge(unit_set, c * HC + h + 1)
                    if n >= len(ST):
                        pe.wait_ge(exp_done, n - len(ST) + 1)
                    bank = ps[ST[n % len(ST)]]
                    diag = j >= 4 * s
                    mm = pe.matmul(bank[0:TT, at:SUP], ks_[c][h][:, j * TT:(j + 1) * TT], qs_[c][h][:, s * SUP + at:(s + 1) * SUP],
                                   start=True, stop=not diag)
                    if diag:
                        mm = pe.matmul(bank[0:TT, at:at + TT], ident_b[0:TT, 0:TT], causal_k[:], start=False, stop=True)
                    mm.then_inc(st_ready, 1)
                elif u[0] == "pv":
                    _, c, s, j = u
                    n, at = number[u], max(0, j - 4 * s) * TT
                    if j == 0 and c * NS + s:
                        pe.wait_ge(y_done, c * NS + s)
                    pe.wait_ge(exp_done, HC * (n + 1))
                    for h in range(HC):
                        col = c * 128 + 32 * h
                        mm = pe.matmul(ps[ACC][32 * h:32 * h + 32, at:SUP], values[0:TT, j, col:col + 32],
                                       probs[0:TT, (HC * n + h) % (STEPS * HC), at:SUP], start=(j == 0), stop=(j == 4 * s + 3),
                                       skip_group_check=True)
                    mm.then_inc(pv_done, 1)
                else:
                    _, c, s, j, two = u
                    step, at = number[("pv", c, s, j)], max(0, j - 4 * s) * TT
                    if two == 2:
                        pe.wait_ge(pair_done, HC * (pair_no[u] + 1))
                    for h in range(HC):
                        src = pairs[0:TT, h, :] if two == 2 else probs[0:TT, (HC * step + h) % (STEPS * HC), at:SUP]
                        mm = pe.matmul(ps[DEN][32 * h:32 * h + 32, at:SUP], ones[0:TT, :], src, start=(j == 0), stop=(j == 4 * s + 3),
                                       skip_group_check=True)
                    mm.then_inc(den_done, 1)


def attention_out(image, nc, sem, ps, ident, ident_b, eps, wide, stats, stream_rows, w_proj, b_proj, resid, normed_t):
    with ExitStack() as mem:
        def sb(name, shape, dt=F32):
            return mem.enter_context(nc.sbuf_tensor(name, shape, dt))

        w = sb("w_proj1", [128, CC, CH])
        pb_row = sb("pb1_row", [128, CH])
        tiles = sb("tiles_again", [128, NT, CH])
        raw = sb("raw2", [128, NT, 6])
        std = sb("std2", [128, NT])
        rstd = sb("rstd2", [128, NT])
        stream = sb("stream", [128, NT, CH])
        xhat = sb("xhat2", [128, 4, CH])
        both = sb("both", [128, 4, CH])
        turned_sb = sb("turned_sb", [128, 4, CC, TT])

        w_in, added, p_ready, p_done = sem("d_w_in"), sem("d_added"), sem("d_p_ready"), sem("d_p_done")
        raw_done, agg_done, std_done, rstd_done = sem("d_raw_done"), sem("d_agg_done"), sem("d_std_done"), sem("d_rstd_done")
        xhat_done, both_done, turned = sem("d_xhat_done"), sem("d_both_done"), sem("d_turned")
        resid_out = [sem(f"d_resid_out{i}") for i in range(4)]
        normed_out = [sem(f"d_normed_out{i}") for i in range(4)]
        turned_evac = sem("d_turned_evac")
        block = mem.enter_context(nc.Block())

        @block.sync
        def _(sp):
            sp.dma_start(w[:], w_proj.rearrange("(c p) o -> p c o", p=128)).then_inc(w_in, 16)
            sp.dma_start(pb_row[0:TT, :], b_proj.rearrange("(a c) -> a c", a=1).broadcast_to([TT, CH])).then_inc(w_in, 16)
            sp.dma_start(tiles[0:TT], stream_rows.rearrange("(i t) c -> t i c", t=TT)).then_inc(w_in, 16)
            for i in range(NT):
                sp.wait_ge(both_done, i + 1)
                sp.dma_start(resid[bass.ds(image, 1), i * TT:(i + 1) * TT, :].rearrange("a t c -> (a t) c"), both[0:TT, i % 4, :]).then_inc(resid_out[i % 4], 16)
                sp.wait_ge(turned_evac, i + 1)
                sp.dma_start(normed_t[bass.ds(image, 1), :, i * TT:(i + 1) * TT].rearrange("a (c p) t -> p (a c) t", p=128),
                             turned_sb[:, i % 4]).then_inc(normed_out[i % 4], 16)
            for i in range(4):
                sp.wait_ge(resid_out[i], 16 * NT // 4)
                sp.wait_ge(normed_out[i], 16 * NT // 4)

        @block.scalar
        def _(act):
            act.wait_ge(agg_done, NT)
            act.activation(std[0:TT, :], stats[0:TT, :, 1], ACT.Sqrt, bias=eps[0:TT, 0:1]).then_inc(std_done, 1)
            for i in range(NT):
                act.wait_ge(turned, i + 1)
                if i >= 4:
                    act.wait_ge(normed_out[i % 4], 16 * (i // 4))
                act.activation(turned_sb[:, i % 4], ps[4 + i % 4][:, 0:2 * TT].rearrange("p (c t) -> p c t", c=CC),
                               ACT.Copy).then_inc(turned_evac, 1)

        @block.gpsimd
        def _(pool):
            pool.wait_ge(w_in, 48)
            for i in range(NT):
                pool.tensor_tensor(tiles[0:TT, i, :], tiles[0:TT, i, :], pb_row[0:TT, :], ALU.add).then_inc(added, 1)
            for i in range(NT):
                pool.wait_ge(xhat_done, i + 1)
                if i >= 4:
                    pool.wait_ge(resid_out[i % 4], 16 * (i // 4))
                pool.tensor_tensor(both[0:TT, i % 4, :], xhat[0:TT, i % 4, :], stream[0:TT, i, :], ALU.add).then_inc(both_done, 1)

        @block.vector
        def _(dve):
            for i in range(NT + 1):
                if i < NT:
                    dve.wait_ge(p_ready, i + 1)
                    dve.wait_ge(added, i + 1)
                    dve.tensor_tensor(stream[0:TT, i, :], ps[i % 4][0:TT, 0:CH], tiles[0:TT, i, :], ALU.add).then_inc(p_done, 1)
                if i:
                    dve.wait_ge(p_done, i)
                    dve.bn_stats(raw[0:TT, i - 1, :], stream[0:TT, i - 1, :]).then_inc(raw_done, 1)
            for i in range(NT):
                dve.wait_ge(raw_done, i + 1)
                dve.bn_aggr(stats[0:TT, i, :], raw[0:TT, i, :]).then_inc(agg_done, 1)
            dve.wait_ge(std_done, 1)
            dve.reciprocal(rstd[0:TT, :], std[0:TT, :]).then_inc(rstd_done, 1)
            dve.wait_ge(rstd_done, 1)
            for i in range(NT):
                if i >= 4:
                    dve.wait_ge(turned, i - 3)
                    dve.wait_ge(both_done, i - 3)
                dve.tensor_scalar(xhat[0:TT, i % 4, :], stream[0:TT, i, :], stats[0:TT, i, 0:1], rstd[0:TT, i:i + 1],
                                  ALU.subtract, ALU.mult).then_inc(xhat_done, 1)

        @block.tensor
        def _(pe):
            pe.wait_ge(w_in, 48)
            for i in range(NT):
                if i >= 4:
                    pe.wait_ge(p_done, i - 3)
                for c in range(CC):
                    mm = pe.matmul(ps[i % 4][0:TT, 0:CH], wide[:, c, i * TT:(i + 1) * TT], w[:, c, :], start=(c == 0), stop=(c == CC - 1))
                mm.then_inc(p_ready, 1)
            for i in range(NT):
                pe.wait_ge(xhat_done, i + 1)
                if i >= 4:
                    pe.wait_ge(turned_evac, i - 3)
                for c in range(CC):
                    mm = pe.transpose(ps[4 + i % 4][:, c * TT:(c + 1) * TT], xhat[0:TT, i % 4, c * 128:(c + 1) * 128], ident[0:TT, 0:TT])
                mm.then_inc(turned, 1)


def expert_layer(nc, sem, ps, ident, ident_b, eps, wide, stats, resid, normed_t, router_t, w1, b1, w2, b2, out):
    with ExitStack() as mem:
        def sb(name, shape, dt=F32):
            return mem.enter_context(nc.sbuf_tensor(name, shape, dt))

        w1_sb = sb("w1_sb", [128, EXPERTS, CC, CH])
        w2_sb = sb("w2_sb", [128, EXPERTS, CC, CH])
        b1_sb = sb("b1_sb", [128, EXPERTS, CC])
        b2_sb = sb("b2_sb", [EXPERTS, CH])
        rt = sb("rt", [128, CC, EXPERTS])
        xg = [sb(f"xg{k}", [128, CC, SUP]) for k in range(2)]
        acc = [sb(f"acc{k}", [128, 4, CH]) for k in range(2)]
        hid = sb("hid", [128, 2, CC, SUP])
        small = {n: sb("e_" + n, [128, 4, EXPERTS]) for n in ("shift", "expo", "prob", "eq", "pos", "one", "left", "eq2", "pos2", "two", "sel")}
        col = {n: sb("e_" + n, [128, 4, 1]) for n in ("mx", "sum", "rsum", "p1", "i1", "p2", "i2", "tot", "rtot")}
        comb = [sb(f"comb{k}", [128, 4, EXPERTS]) for k in range(2)]
        iota = sb("iota", [128, 4, EXPERTS])
        comb_t = sb("comb_t", [EXPERTS, 4, TT])
        result = sb("result", [128, CC, SUP])

        wt_in, iota_set = sem("e_wt_in"), sem("e_iota_set")
        with nc.Block() as block:
            @block.sync
            def _(sp):
                sp.dma_start(w1_sb[:], w1.rearrange("e (c p) o -> p e c o", p=128)).then_inc(wt_in, 16)
                sp.dma_start(w2_sb[:], w2.rearrange("e (c p) o -> p e c o", p=128)).then_inc(wt_in, 16)
                with nc.allow_non_contiguous_dma(reason="a bias by channel"):
                    for c in range(CC):
                        sp.dma_start(b1_sb[:, :, c], b1[:, c * 128:(c + 1) * 128].rearrange("e p -> p e")).then_inc(wt_in, 16)
                sp.dma_start(b2_sb[:], b2).then_inc(wt_in, 16)
                sp.dma_start(rt[:], router_t.rearrange("(c p) e -> p c e", p=128)).then_inc(wt_in, 16)
                sp.wait_ge(wt_in, 16 * 6)

            @block.gpsimd
            def _(pool):
                for e in range(EXPERTS):
                    pool.memset(iota[:, :, e:e + 1], float(e)).then_inc(iota_set, 1)
                pool.wait_ge(iota_set, EXPERTS)

        mark = []

        def own(name):
            s = sem(name)
            mark.append(s)
            return s

        x_in, acc_in = [own("e_x_in0"), own("e_x_in1")], [own("e_acc_in0"), own("e_acc_in1")]
        lg_ready, lg_read, chain, exp_done, comb_done = own("e_lg_ready"), own("e_lg_read"), own("e_chain"), own("e_exp_done"), own("e_comb_done")
        ct_ready, ct_done, bias_ready, bias_done = own("e_ct_ready"), own("e_ct_done"), own("e_bias_ready"), own("e_bias_done")
        h_ready, h_done, y_ready, y_done = own("e_h_ready"), own("e_h_done"), own("e_y_ready"), own("e_y_done")
        o_turned, o_evac, o_out = own("e_o_turned"), own("e_o_evac"), own("e_o_out")

        HID, OUTS, MISC, TURNS = [0, 1, 2], [3, 4, 5], 6, 7
        LAST = NS * EXPERTS
        STEPS = 21

        with nc.Fori(0, IMAGES) as image:
            with nc.Block() as block:
                @block.sync
                def _(sp):
                    def load_x(g):
                        if g >= 2:
                            sp.wait_ge(h_ready, CC * EXPERTS * (g - 1))
                        sp.dma_start(xg[g % 2][:], normed_t[bass.ds(image, 1), :, g * SUP:(g + 1) * SUP].rearrange(
                            "a (c p) t -> p (a c) t", p=128)).then_inc(x_in[g % 2], 16)

                    def load_acc(g):
                        if g >= 2:
                            sp.wait_ge(o_turned, CC * (g - 1))
                        sp.dma_start(acc[g % 2][0:TT], resid[bass.ds(image, 1), g * SUP:(g + 1) * SUP, :].rearrange(
                            "a (i t) c -> t (a i) c", t=TT)).then_inc(acc_in[g % 2], 16)

                    def store(g):
                        sp.wait_ge(o_evac, CC * (g + 1))
                        sp.dma_start(out[bass.ds(image, 1), :, g * SUP:(g + 1) * SUP].rearrange(
                            "a (c p) t -> p (a c) t", p=128), result[:]).then_inc(o_out, 16)

                    load_x(0)
                    load_acc(0)
                    for g in range(NS):
                        if g + 1 < NS:
                            load_x(g + 1)
                            load_acc(g + 1)
                        if g:
                            store(g - 1)
                    store(NS - 1)
                    sp.wait_ge(o_out, 16 * NS)

                @block.scalar
                def _(act):
                    def router_exp(g):
                        act.wait_ge(chain, STEPS * g + 2)
                        act.activation(small["expo"][0:TT], small["shift"][0:TT], ACT.Exp).then_inc(exp_done, 1)

                    def copy_weights(g):
                        act.wait_ge(ct_ready, g + 1)
                        if g:
                            act.wait_ge(bias_ready, 2 * g)
                        act.activation(comb_t[:], ps[MISC][0:EXPERTS, 0:SUP].rearrange("e (i t) -> e i t", i=4), ACT.Copy).then_inc(ct_done, 1)

                    def hidden(turn):
                        for c in range(CC):
                            n = turn * CC + c
                            act.wait_ge(h_ready, n + 1)
                            if turn >= 2:
                                act.wait_ge(y_ready, 4 * (turn - 1))
                            act.activation(hid[:, turn % 2, c, :], ps[HID[n % 3]][:, 0:SUP], ACT.Gelu,
                                           bias=b1_sb[:, turn % EXPERTS, c:c + 1]).then_inc(h_done, 1)

                    def take_out(g):
                        for c in range(CC):
                            act.wait_ge(o_turned, CC * g + c + 1)
                            if g and c == 0:
                                act.wait_ge(o_out, 16 * g)
                            act.activation(result[:, c, :], ps[TURNS - c][:, 0:SUP], ACT.Copy).then_inc(o_evac, 1)

                    router_exp(0)
                    hidden(0)
                    hidden(1)
                    copy_weights(0)
                    for turn in range(LAST):
                        g, e = divmod(turn, EXPERTS)
                        if turn + 2 < LAST:
                            hidden(turn + 2)
                        if e == 1 and g:
                            take_out(g - 1)
                        if e == 3 and g + 1 < NS:
                            router_exp(g + 1)
                        if e == EXPERTS - 1 and g + 1 < NS:
                            copy_weights(g + 1)
                    take_out(NS - 1)

                @block.vector
                def _(dve):
                    t = {k: v[0:TT] for k, v in (small | col).items()}
                    wide8 = lambda a: a.broadcast_to([TT, 4, EXPERTS])

                    def router(g):
                        count = STEPS * g
                        logits = ps[MISC][0:TT, 0:4 * EXPERTS].rearrange("p (i e) -> p i e", i=4)
                        dve.wait_ge(lg_ready, g + 1)
                        dve.tensor_reduce(t["mx"], logits, AX.X, ALU.max).then_inc(chain, 1)
                        yield
                        dve.wait_ge(chain, count + 1)
                        dve.tensor_tensor(t["shift"], logits, wide8(t["mx"]), ALU.subtract).then_inc(chain, 1)
                        yield
                        dve.wait_ge(exp_done, g + 1)
                        dve.tensor_reduce(t["sum"], t["expo"], AX.X, ALU.add).then_inc(chain, 1)
                        yield
                        dve.wait_ge(chain, count + 3)
                        dve.reciprocal(t["rsum"], t["sum"]).then_inc(chain, 1)
                        yield
                        dve.wait_ge(chain, count + 4)
                        dve.tensor_tensor(t["prob"], t["expo"], wide8(t["rsum"]), ALU.mult).then_inc(chain, 1)
                        yield
                        count += 5
                        for p, eq, pos, idx, best, src in (("p1", "eq", "pos", "i1", "one", "prob"), ("p2", "eq2", "pos2", "i2", "two", "left")):
                            dve.wait_ge(chain, count)
                            dve.tensor_reduce(t[p], t[src], AX.X, ALU.max).then_inc(chain, 1)
                            yield
                            dve.wait_ge(chain, count + 1)
                            dve.tensor_tensor(t[eq], t[src], wide8(t[p]), ALU.is_equal).then_inc(chain, 1)
                            yield
                            dve.wait_ge(chain, count + 2)
                            dve.scalar_tensor_tensor(out=t[pos], in0=t[eq], scalar=-float(EXPERTS), in1=iota[0:TT],
                                                     op0=ALU.mult, op1=ALU.add).then_inc(chain, 1)
                            yield
                            dve.wait_ge(chain, count + 3)
                            dve.tensor_reduce(t[idx], t[pos], AX.X, ALU.min).then_inc(chain, 1)
                            yield
                            dve.wait_ge(chain, count + 4)
                            dve.tensor_tensor(t[best], t[pos], wide8(t[idx]), ALU.is_equal).then_inc(chain, 1)
                            yield
                            count += 5
                            if best == "one":
                                dve.wait_ge(chain, count)
                                dve.scalar_tensor_tensor(out=t["left"], in0=t["one"], scalar=-2.0, in1=t["prob"],
                                                         op0=ALU.mult, op1=ALU.add).then_inc(chain, 1)
                                yield
                                count += 1
                        dve.wait_ge(chain, count)
                        dve.tensor_tensor(t["tot"], t["p1"], t["p2"], ALU.add).then_inc(chain, 1)
                        yield
                        dve.wait_ge(chain, count + 1)
                        dve.tensor_scalar(t["tot"], t["tot"], 1e-12, None, ALU.max).then_inc(chain, 1)
                        yield
                        dve.wait_ge(chain, count + 2)
                        dve.reciprocal(t["rtot"], t["tot"]).then_inc(chain, 1)
                        yield
                        dve.tensor_tensor(t["sel"], t["one"], t["two"], ALU.add).then_inc(chain, 1)
                        yield
                        dve.wait_ge(chain, count + 4)
                        dve.tensor_tensor(t["sel"], t["sel"], t["prob"], ALU.mult).then_inc(chain, 1)
                        yield
                        dve.wait_ge(chain, count + 5)
                        if g >= 2:
                            dve.wait_ge(ct_ready, g - 1)
                        dve.tensor_tensor(comb[g % 2][0:TT], t["sel"], wide8(t["rtot"]), ALU.mult).then_inc(comb_done, 1)
                        dve.wait_ge(comb_done, g + 1)
                        assert count + 5 == STEPS * g + STEPS, count
                        yield

                    def add_bias(g):
                        for k, bank in enumerate((TURNS, MISC)):
                            dve.wait_ge(bias_ready, 2 * g + k + 1)
                            dve.wait_ge(y_done, 4 * EXPERTS * g + 4)
                            pair = acc[g % 2][0:TT, 2 * k:2 * k + 2, :]
                            dve.tensor_tensor(pair, ps[bank][0:TT, 0:2 * CH].rearrange("t (i c) -> t i c", i=2), pair, ALU.add).then_inc(bias_done, 1)

                    for _ in router(0):
                        pass
                    for turn in range(LAST):
                        g, e = divmod(turn, EXPERTS)
                        if e == 0:
                            dve.wait_ge(acc_in[g % 2], 16 * (g // 2 + 1))
                        if e == 1:
                            add_bias(g)
                            dve.wait_ge(bias_done, 2 * g + 2)
                        if e == 3 and g + 1 < NS:
                            steps = router(g + 1)
                        for i in range(4):
                            n = 4 * turn + i
                            dve.wait_ge(y_ready, n + 1)
                            if e:
                                dve.wait_ge(y_done, n - 3)
                            tile = acc[g % 2][0:TT, i, :]
                            dve.scalar_tensor_tensor(out=tile, in0=ps[OUTS[n % 3]][0:TT, 0:CH], scalar=comb[g % 2][0:TT, i, e:e + 1],
                                                     in1=tile, op0=ALU.mult, op1=ALU.add).then_inc(y_done, 1)
                            if g + 1 < NS and e == 3 and i < 2:
                                next(steps)
                            if g + 1 < NS and e > 3:
                                for _ in range(2):
                                    next(steps, None)

                @block.tensor
                def _(pe):
                    def logits(g):
                        pe.wait_ge(x_in[g % 2], 16 * (g // 2 + 1))
                        if g >= 2:
                            pe.wait_ge(o_evac, CC * (g - 1))
                        for i in range(4):
                            for k in range(CC):
                                mm = pe.matmul(ps[MISC][0:TT, i * EXPERTS:(i + 1) * EXPERTS], xg[g % 2][:, k, i * TT:(i + 1) * TT], rt[:, k, :],
                                               start=(k == 0), stop=(k == CC - 1))
                        mm.then_inc(lg_ready, 1)

                    def turn_weights(g):
                        pe.wait_ge(comb_done, g + 1)
                        for i in range(4):
                            mm = pe.transpose(ps[MISC][0:EXPERTS, i * TT:(i + 1) * TT], comb[g % 2][0:TT, i, :], ident[0:TT, 0:TT])
                        mm.then_inc(ct_ready, 1)

                    def bias(g):
                        pe.wait_ge(ct_done, g + 1)
                        for k, bank in enumerate((TURNS, MISC)):
                            for i in range(2):
                                mm = pe.matmul(ps[bank][0:TT, i * CH:(i + 1) * CH], comb_t[:, 2 * k + i, :], b2_sb[:], start=True, stop=True)
                            mm.then_inc(bias_ready, 1)

                    def turn_results(g):
                        pe.wait_ge(y_done, 4 * EXPERTS * (g + 1))
                        pe.wait_ge(bias_done, 2 * min(g + 2, NS))
                        for c in range(CC):
                            for i in range(4):
                                mm = pe.transpose(ps[TURNS - c][:, i * TT:(i + 1) * TT], acc[g % 2][0:TT, i, c * 128:(c + 1) * 128], ident[0:TT, 0:TT])
                            mm.then_inc(o_turned, 1)

                    def first_layer(turn):
                        g, e = divmod(turn, EXPERTS)
                        for c in range(CC):
                            n = turn * CC + c
                            if n >= 3:
                                pe.wait_ge(h_done, n - 2)
                            for k in range(CC):
                                mm = pe.matmul(ps[HID[n % 3]][:, 0:SUP], w1_sb[:, e, k, c * 128:(c + 1) * 128], xg[g % 2][:, k, :],
                                               start=(k == 0), stop=(k == CC - 1))
                            mm.then_inc(h_ready, 1)

                    def second_layer(turn):
                        pe.wait_ge(h_done, CC * (turn + 1))
                        for i in range(4):
                            n = 4 * turn + i
                            if n >= 3:
                                pe.wait_ge(y_done, n - 2)
                            for k in range(CC):
                                mm = pe.matmul(ps[OUTS[n % 3]][0:TT, 0:CH], hid[:, turn % 2, k, i * TT:(i + 1) * TT], w2_sb[:, turn % EXPERTS, k, :],
                                               start=(k == 0), stop=(k == CC - 1))
                            mm.then_inc(y_ready, 1)

                    logits(0)
                    first_layer(0)
                    first_layer(1)
                    turn_weights(0)
                    for turn in range(LAST):
                        g, e = divmod(turn, EXPERTS)
                        second_layer(turn)
                        if turn + 2 < LAST:
                            first_layer(turn + 2)
                        if e == 0:
                            bias(g)
                        if e == 1 and g:
                            turn_results(g - 1)
                        if e == 2 and g + 1 < NS:
                            logits(g + 1)
                        if e == EXPERTS - 1 and g + 1 < NS:
                            turn_weights(g + 1)
                    turn_results(NS - 1)

            for s in mark:
                nc.sync.sem_clear(s)
            nc.all_engine_barrier()


def kernel(**inputs):
    import ml_dtypes as _ml
    import numpy as _np
    import concourse.bacc as _bacc
    from concourse import mybir as _mybir
    from concourse.bass_utils import run_bass_kernel_spmd as _run

    a = {k: _np.asarray(v) for k, v in inputs.items()}
    bf16 = _ml.bfloat16
    rows = _np.arange(TT)
    lane = _np.arange(128)
    behind = _np.where(rows[None, :] > rows[:, None], NEG, 0.0)
    arrays = {
        "x": a["x"].reshape(IMAGES * CH, TOK),
        "qkv0_t": a["L0_conv_qkv_w"].T, "qkv0_b": a["L0_conv_qkv_b"],
        "proj0_t": a["L0_conv_proj_w"].T, "proj0_b": a["L0_conv_proj_b"],
        "rel_bias": a["L0_conv_relative_bias"],
        "w_qkv": a["L1_attn_w_qkv"], "b_qkv": a["L1_attn_b_qkv"],
        "w_proj": a["L1_attn_w_proj"], "b_proj": a["L1_attn_b_proj"],
        "router_t": a["L1_ffn_router_w"].T,
        "w1": a["L1_ffn_w1"], "b1": a["L1_ffn_b1"], "w2": a["L1_ffn_w2"], "b2": a["L1_ffn_b2"],
        "ident_in": _np.eye(128, dtype=_np.float32),
        "ident_b_in": _np.eye(128).astype(bf16),
        "group_in": (lane[:, None] // 8 == lane[None, :] // 8).astype(_np.float32) / 8,
        "nmask_in": neighbourhood_mask().astype(bf16),
        "causal_q_in": behind.astype(bf16),
        "causal_k_in": _np.ascontiguousarray(behind.T).astype(bf16),
    }
    arrays = {f"in_{k}": _np.ascontiguousarray(v) for k, v in arrays.items()}
    nc = _bacc.Bacc("TRN2", target_bir_lowering=False, num_devices=1)
    args = [nc.dram_tensor(k, v.shape, _mybir.dt.from_np(v.dtype), kind="ExternalInput").ap() for k, v in arrays.items()]
    args.append(nc.dram_tensor("out_dram", (IMAGES, CH, TOK), F32, kind="ExternalOutput").ap())
    hybrid_kernel(nc, *args)
    r = _run(nc, [arrays], core_ids=[0])
    return r.results[0]["out_dram"].reshape(IMAGES, CH, SIDE, SIDE)
```

```python
from contextlib import ExitStack

import numpy as np

import concourse.bass as bass
from concourse import mybir

F32 = mybir.dt.float32
BF16 = mybir.dt.bfloat16
F16 = mybir.dt.float16
ALU = mybir.AluOpType
ACT = mybir.ActivationFunctionType
AX = mybir.AxisListType

IMAGES, CH, SIDE = 2, 256, 56
TOK = SIDE * SIDE
HEADS, HD = 8, 32
CC = CH // 128
HC = HEADS // CC
TT = 2 * SIDE
NT = TOK // TT
SUP = 4 * TT
NS = TOK // SUP
SCALE = float(HD) ** -0.5

WS = 7
K2 = WS * WS
WIN = SIDE - WS + 1
L = WIN * WIN
HALF = WS // 2
DY, DX, T4 = 356, 51, 4
WCOLS = WS * WS * T4
TAB0 = 147
TABN = TAB0 + 2 * (NT - 1) + 6 * (WS - 1) + 1
PADN = TABN + WIN + SIDE + 2
EDGE = 3
BH = WIN // 2

NEG = -1e30
EPS = 1e-5
SPLIT_MAX = 4096.0
ROW_UNIT = 16384.0
MAX_BANKS, MAX_SLOTS = 1, 3
X_SCALE, HID_MAX = 256.0, 32768.0
assert CH == 256
EXPERTS = 8


def neighbourhood_mask():
    m = np.zeros((TT, NT, WS, WS, T4), np.uint8)
    for tile in range(NT):
        for dy in range(WS):
            for dx in range(WS):
                for p in range(TT):
                    r, c = 2 * tile + p // SIDE - dy, p % SIDE - dx
                    if not (0 <= r < WIN and 0 <= c < WIN):
                        continue
                    f = (WS * dy + dx) * L + r * WIN + c
                    t = f // K2 - (2 * tile + DY * dy + DX * dx)
                    assert 0 <= t < T4
                    m[p, tile, dy, dx, t] = 1
    assert m.sum() == K2 * L
    return m.reshape(TT, NT * WCOLS)


def border_plan():
    left = [0] + [(WIN - i + (i - 1) // WS) * SIDE + (i - 1) % WS for i in range(1, WIN)]
    right = [(WIN - 2 - i + i // WS) * SIDE + i % WS + 1 for i in range(WIN - 1)]
    right.append((SIDE - 1) * SIDE + WS)
    top = [K2 * i for i in range(WIN)]
    bottom = [K2 * i + WIN for i in range(WIN)]
    plan = []
    for side, starts in enumerate((left, right, top, bottom)):
        order = list(range(WIN))[::-1] if side < 2 else list(range(WIN))
        for half in range(2):
            at = order[half * BH:(half + 1) * BH]
            corner = None if side < 2 else (0, BH - 1)[half]
            plan.append((side, at, [starts[i] for i in at], corner))
    return plan


def runs(starts):
    out, i = [], 0
    while i < len(starts):
        n, step = 1, 0
        if i + 1 < len(starts) and starts[i + 1] > starts[i]:
            step = starts[i + 1] - starts[i]
            while i + n < len(starts) and starts[i + n] == starts[i] + n * step:
                n += 1
        out.append((i, starts[i], step, n))
        i += n
    return out


def hybrid_kernel(nc, x, qkv0_t, qkv0_b, proj0_t, proj0_b, rel_bias, w_qkv, b_qkv, w_proj, b_proj,
                  router_t, w1, b1, w2, b2, ident_in, ident_b_in, group_in, nmask_in, causal_q_in,
                  causal_k_in, unit_row_in, out):
    dram = lambda name, shape, dt: nc.dram_tensor(name, shape, dt, kind="Internal").ap()
    v_rows = dram("v_rows", [CC, TOK, 128], F32)
    v_top = dram("v_top", [CC, L, 128], F32)
    v_bottom = dram("v_bottom", [CC, L, 128], F32)
    bias_pad = dram("bias_pad", [PADN, HEADS], F32)
    parts = dram("parts", [2, CC, 2, 128, TOK], F16)
    stream_rows = dram("stream_rows", [TOK, CH], F32)
    v1_rows = dram("v1_rows", [TOK, CH], F32)
    resid = dram("resid", [IMAGES, TOK, CH], F32)
    normed_t = dram("normed_t", [IMAGES, CH, TOK], F32)

    ctx = ExitStack()
    sems = []

    def sem(name):
        s = ctx.enter_context(nc.semaphore(name))
        sems.append(s)
        return s

    def persist(name, shape, dt):
        return ctx.enter_context(nc.sbuf_tensor(name, shape, dt))

    with ctx:
        banks = ctx.enter_context(nc.psum_tensor("banks", [128, 8, 512], F32))
        ps = [banks[:, i, :] for i in range(8)]
        ident = persist("ident", [128, 128], F32)
        ident_b = persist("ident_b", [128, 128], BF16)
        eps = persist("eps", [128, 1], F32)
        wide = persist("wide", [128, CC, TOK], F32)
        stats = persist("stats", [128, NT, 2], F32)
        exp_scale = persist("exp_scale", [128, 1], F32)

        const_in = sem("const_in")
        const_set = sem("const_set")

        with ExitStack() as mem, nc.Block() as block:
            zero = mem.enter_context(nc.sbuf_tensor("zero", [128, 64], F32))
            inner = mem.enter_context(nc.sbuf_tensor("inner", [K2, HEADS], F32))
            zero_set = sem("zero_set")
            pad_out = sem("pad_out")
            inner_in = sem("inner_in")

            @block.gpsimd
            def _(pool):
                pool.memset(zero[:], 0.0).then_inc(zero_set, 1)
                pool.memset(eps[:], EPS).then_inc(const_set, 1)

            @block.sync
            def _(sp):
                sp.dma_start(ident[:], ident_in).then_inc(const_in, 16)
                sp.dma_start(ident_b[:], ident_b_in).then_inc(const_in, 16)
                for ki in range(WS):
                    row = (HALF + ki) * (2 * WS - 1) + HALF
                    sp.dma_start(inner[ki * WS:(ki + 1) * WS, :], rel_bias[row:row + WS, :]).then_inc(inner_in, 16)
                sp.wait_ge(zero_set, 1)
                flat = bias_pad.rearrange("a b -> (a b)")
                n, per = PADN * HEADS, 32
                rows = n // per
                for at in range(0, rows, 128):
                    k = min(128, rows - at)
                    sp.dma_start(flat[at * per:(at + k) * per].rearrange("(p a) -> p a", p=k),
                                 zero[0:k, 0:per]).then_inc(pad_out, 16)
                rest = n - rows * per
                if rest:
                    sp.dma_start(flat[rows * per:n].rearrange("(p a) -> p a", p=1), zero[0:1, 0:rest]).then_inc(pad_out, 16)
                chunks = (rows + 127) // 128 + (1 if rest else 0)
                sp.wait_ge(pad_out, 16 * chunks)
                sp.wait_ge(inner_in, 16 * WS)
                sp.dma_start(bias_pad[TAB0:TAB0 + K2, :], inner[:]).then_inc(pad_out, 16)
                sp.wait_ge(pad_out, 16 * (chunks + 1))
                sp.wait_ge(const_in, 32)

        args = dict(nc=nc, sem=sem, ps=ps, ident=ident, ident_b=ident_b, eps=eps, wide=wide, stats=stats)
        first = len(sems)
        with nc.Fori(0, IMAGES) as image:
            with nc.sbuf_tensor("tiles", [128, NT, CH], F32) as tiles:
                neighbourhood_layer(image, tiles=tiles, x=x, qkv0_t=qkv0_t, qkv0_b=qkv0_b, proj0_t=proj0_t, proj0_b=proj0_b,
                                    rel_bias=rel_bias, group_in=group_in, nmask_in=nmask_in, v_rows=v_rows,
                                    v_top=v_top, v_bottom=v_bottom, bias_pad=bias_pad, **args)
                project_qkv(tiles=tiles, exp_scale=exp_scale, w_qkv=w_qkv, b_qkv=b_qkv, parts=parts,
                            stream_rows=stream_rows, v1_rows=v1_rows, **args)
            causal_attention(banks=banks, exp_scale=exp_scale, v1_rows=v1_rows, parts=parts, causal_q_in=causal_q_in,
                             causal_k_in=causal_k_in, unit_row_in=unit_row_in, **args)
            attention_out(image, stream_rows=stream_rows, w_proj=w_proj, b_proj=b_proj, resid=resid, normed_t=normed_t, **args)
            for s in sems[first:]:
                nc.sync.sem_clear(s)
            nc.all_engine_barrier()
        expert_layer(resid=resid, normed_t=normed_t, router_t=router_t, w1=w1, b1=b1, w2=w2, b2=b2, out=out, **args)


def neighbourhood_layer(image, nc, sem, ps, ident, ident_b, eps, wide, stats, tiles, x, qkv0_t, qkv0_b,
                        proj0_t, proj0_b, rel_bias, group_in, nmask_in, v_rows, v_top, v_bottom, bias_pad):
    plan = border_plan()
    NB = len(plan)
    ITEMS = NT + NB
    PB = (BH + 1) // 2
    HALVES = ((0, PB), (64, BH - PB))
    PQ = HC * EDGE
    HX = 2 * PB * EDGE
    QX = HC * HX
    QC = HC * EDGE * EDGE

    with ExitStack() as mem:
        def sb(name, shape, dt=F32):
            return mem.enter_context(nc.sbuf_tensor(name, shape, dt))

        xn = sb("xn", [128, CC, TOK])
        q_diag = sb("q_diag", [128, HC, L])
        q_border = sb("q_border", [128, 4, WIN, HC, EDGE])
        q_corner = sb("q_corner", [128, 4, HC, EDGE * EDGE])
        keys = sb("keys", [128, TOK])
        key_list = sb("key_list", [128, L])
        summed = sb("summed", [128, L])
        v_tile = sb("v_tile", [128, 4, 128])
        biased = sb("biased", [128, 2, HC * WCOLS])
        scores = sb("scores", [128, 2, HC * WCOLS])
        wqkv = sb("wqkv", [128, CC, 3 * CH])
        wproj = sb("wproj", [128, CC, CH])
        qkb = sb("qkb", [128, 2 * CC])
        vb_row = sb("vb_row", [128, CH])
        pb_row = sb("pb_row", [128, CH])
        table = sb("table", [128, TABN, HEADS])
        class_bias = sb("class_bias", [128, K2, HEADS])
        edge = sb("edge", [128, 2, QX + QC])
        nmask = sb("nmask", [128, NT * WCOLS], BF16)
        group = sb("group", [128, 128])
        raw = sb("raw", [128, CC, 7, 6])
        chan = sb("chan", [128, CC, 2])
        gmean = sb("gmean", [128, CC])
        dev = sb("dev", [128, CC])
        dev2 = sb("dev2", [128, CC])
        spread = sb("spread", [128, CC])
        std = sb("std", [128, CC])
        rstd = sb("rstd", [128, CC])
        t_raw = sb("t_raw", [128, NT, 6])

        tiles_flat = tiles[:].rearrange("p a b -> p (a b)")
        v_border = [tiles_flat[:, i * PB * 128:(i + 1) * PB * 128].rearrange("p (a b) -> p a b", b=128) for i in range(2)]
        queries = tiles_flat[:, 2 * PB * 128:2 * PB * 128 + TOK]
        q_grid = queries.rearrange("p (a b) -> p a b", b=SIDE)
        k_grid = keys[:].rearrange("p (a b) -> p a b", b=SIDE)
        o_grid = wide[:].rearrange("p c (a b) -> p c a b", b=SIDE)
        x_again = q_diag[:].rearrange("p a b -> p (a b)")[:, 0:CC * TOK].rearrange("p (c t) -> p c t", c=CC)

        x_in = [sem(f"x_in{c}") for c in range(CC)]
        w_in, tab_in, class_in = sem("w_in"), sem("tab_in"), sem("class_in")
        cleared, summed_clear = sem("cleared"), sem("summed_clear")
        raw_done, chan_done, gm_ready, gm_copied = sem("raw_done"), sem("chan_done"), sem("gm_ready"), sem("gm_copied")
        dev_done, gv_ready, std_done, xn_ready = sem("dev_done"), sem("gv_ready"), sem("std_done"), sem("xn_ready")
        qk_ready, q_evac, k_evac = sem("qk_ready"), sem("q_evac"), sem("k_evac")
        diag_done, border_q_done, list_done = sem("diag_done"), sem("border_q_done"), sem("list_done")
        v_ready, v_evac, v_unfolded = sem("v_ready"), sem("v_evac"), sem("v_unfolded")
        v_out = [sem(f"v_out{i}") for i in range(4)]
        vb_in = [sem("vb_in0"), sem("vb_in1")]
        s_ready, bias_done, mask_done, border_done = sem("s_ready"), sem("bias_done"), sem("mask_done"), sem("border_done")
        o_ready, o_used, summed_done, placed = sem("o_ready"), sem("o_used"), sem("summed_done"), sem("placed")
        xres_in, p_ready, p_done, ts_done = sem("xres_in"), sem("p_ready"), sem("p_done"), sem("ts_done")

        def mains(n):
            return (n // ITEMS) * NT + min(n % ITEMS, NT)

        def borders(n):
            return n - mains(n)

        loads, reached, count = [], [], [0, 0]
        for k in range(CC * NB):
            side, at, starts, corner = plan[k % NB]
            loads.append([(part,) + run for part in range(2) for run in runs(starts[part::2])])
            count[k % 2] += 16 * len(loads[-1])
            reached.append(count[k % 2])

        block = mem.enter_context(nc.Block())

        @block.sync
        def _(sp):
            for c in range(CC):
                sp.dma_start(wide[:, c, :], x[bass.ds(image * CH + c * 128, 128), :]).then_inc(x_in[c], 16)
            sp.dma_start(group[:], group_in).then_inc(w_in, 16)
            sp.dma_start(wqkv[:], qkv0_t.rearrange("(c p) o -> p c o", p=128)).then_inc(w_in, 16)
            with nc.allow_non_contiguous_dma(reason="a bias by channel"):
                sp.dma_start(qkb[:], qkv0_b[0:2 * CH].rearrange("(c p) -> p c", p=128)).then_inc(w_in, 16)
            sp.dma_start(vb_row[0:TT, :], qkv0_b[2 * CH:3 * CH].rearrange("(a c) -> a c", a=1).broadcast_to([TT, CH])).then_inc(w_in, 16)
            sp.dma_start(pb_row[0:TT, :], proj0_b.rearrange("(a c) -> a c", a=1).broadcast_to([TT, CH])).then_inc(w_in, 16)
            sp.dma_start(wproj[:], proj0_t.rearrange("(c p) o -> p c o", p=128)).then_inc(w_in, 16)
            for half in range(2):
                src = bass.AP(bias_pad.tensor, half * WIN * HEADS, [[HEADS, SIDE], [1, TABN * HEADS]])
                sp.dma_start(table[half * SIDE:(half + 1) * SIDE].rearrange("p a b -> p (a b)"), src).then_inc(tab_in, 16)
            sp.dma_start(nmask[0:TT, :], nmask_in).then_inc(tab_in, 16)
            line = (2 * WS - 1) * HEADS
            for base, _ in HALVES:
                for ki in range(WS):
                    src = bass.AP(rel_bias.tensor, ki * line, [[HEADS, WS], [line, WS], [1, WS * HEADS]])
                    dst = class_bias[base + ki * WS:base + (ki + 1) * WS].rearrange("p (a b) h -> p a (b h)", a=WS)
                    sp.dma_start(dst, src).then_inc(class_in, 16)
            sp.wait_ge(cleared, 5)
            for c in range(CC):
                for r in range(NT):
                    sp.wait_ge(v_evac, c * NT + r + 1)
                    sp.dma_start(v_rows[c, r * TT:(r + 1) * TT, :], v_tile[0:TT, r % 4, :]).then_inc(v_out[r % 4], 16)
                for i in range(4):
                    sp.wait_ge(v_out[i], 16 * NT // 4 * (c + 1))
                for k in range(NB):
                    n, kk = c * ITEMS + NT + k, c * NB + k
                    if k == 2:
                        for dst, off in ((v_top, 0), (v_bottom, (WS - 1) * SIDE + WS - 1)):
                            src = bass.AP(v_rows.tensor, (c * TOK + off) * 128, [[SIDE * 128, WIN], [1, WIN * 128]])
                            sp.dma_start(dst[c].rearrange("(a b) d -> a (b d)", a=WIN), src).then_inc(v_unfolded, 16)
                    if k == 4:
                        sp.wait_ge(v_unfolded, 32 * (c + 1))
                    if k >= 2:
                        sp.wait_ge(o_ready, n - 1)
                    elif c:
                        sp.wait_ge(o_ready, c * ITEMS)
                    base = (v_rows, v_rows, v_top, v_bottom)[plan[k][0]]
                    rows = TOK if plan[k][0] < 2 else L
                    for part, pair, start, step, cnt in loads[kk]:
                        src = bass.AP(base.tensor, (c * rows + start) * 128, [[128, K2], [step * 128, cnt], [1, 128]])
                        lane = HALVES[part][0]
                        sp.dma_start(v_border[kk % 2][lane:lane + K2, pair:pair + cnt, :], src).then_inc(vb_in[kk % 2], 16)
            sp.wait_ge(s_ready, CC * ITEMS)
            for c in range(CC):
                sp.dma_start(x_again[:, c, :], x[bass.ds(image * CH + c * 128, 128), :]).then_inc(xres_in, 16)

        @block.gpsimd
        def _(pool):
            pool.memset(q_diag[:], 0.0).then_inc(cleared, 1)
            pool.memset(q_border[:], 0.0).then_inc(cleared, 1)
            pool.memset(q_corner[:], 0.0).then_inc(cleared, 1)
            pool.memset(edge[:], 0.0).then_inc(cleared, 1)
            pool.memset(tiles_flat[:, 0:2 * PB * 128], 0.0).then_inc(cleared, 1)
            for c in range(CC):
                if c:
                    pool.wait_ge(placed, c)
                pool.memset(summed[:], 0.0).then_inc(summed_clear, 1)
                pool.wait_ge(tab_in, 48)
                for r in range(NT):
                    n = c * ITEMS + r
                    pool.wait_ge(bias_done, mains(n) + 1)
                    if n >= 2:
                        pool.wait_ge(o_ready, n - 1)
                    m = nmask[0:TT, r * WCOLS:(r + 1) * WCOLS]
                    pool.tensor_tensor(scores[0:TT, n % 2, :].rearrange("p (h w) -> p h w", h=HC),
                                       biased[0:TT, n % 2, :].rearrange("p (h w) -> p h w", h=HC),
                                       bass.AP(m.tensor, m.offset, [list(m.ap[0]), [0, HC], [1, WCOLS]]),
                                       ALU.mult).then_inc(mask_done, 1)

        @block.scalar
        def _(act):
            act.wait_ge(gv_ready, 1)
            act.activation(std[:], spread[:], ACT.Sqrt, bias=eps[:, 0:1]).then_inc(std_done, 1)
            for c in range(CC):
                if c:
                    act.wait_ge(s_ready, c * ITEMS)
                for j in range(NS):
                    act.wait_ge(qk_ready, c * 2 * NS + NS + j + 1)
                    act.activation(keys[:, j * SUP:(j + 1) * SUP], ps[(c * 2 * NS + NS + j) % 4][:, 0:SUP], ACT.Identity,
                                   bias=qkb[:, CC + c:CC + c + 1]).then_inc(k_evac, 1)
                act.wait_ge(q_evac, NS * (c + 1))
                if c == 0:
                    act.wait_ge(cleared, 3)
                for h in range(HC):
                    q = slice(32 * h, 32 * h + 32)
                    act.copy(q_border[q, 0, :, h, :], q_grid[q, HALF:HALF + WIN, 0:EDGE])
                    act.copy(q_border[q, 1, :, h, :], q_grid[q, HALF:HALF + WIN, SIDE - EDGE:SIDE])
                    act.copy(q_border[q, 2, :, h, :], q_grid[q, 0:EDGE, HALF:HALF + WIN].rearrange("p a b -> p b a"))
                    act.copy(q_border[q, 3, :, h, :], q_grid[q, SIDE - EDGE:SIDE, HALF:HALF + WIN].rearrange("p a b -> p b a"))
                    for k in range(4):
                        hs, ws = (SIDE - EDGE) * (k // 2), (SIDE - EDGE) * (k % 2)
                        last = act.copy(q_corner[q, k, h, :].rearrange("p (a b) -> p a b", b=EDGE),
                                                q_grid[q, hs:hs + EDGE, ws:ws + EDGE])
                last.then_inc(border_q_done, 1)
                act.wait_ge(k_evac, NS * (c + 1))
                for side in (2, 3):
                    if side == 3:
                        act.wait_ge(s_ready, c * ITEMS + NT + 6)
                    o = (WS - 1) * (side - 2)
                    act.activation(key_list[:].rearrange("p (a b) -> p a b", b=WIN), k_grid[:, o:o + WIN, o:o + WIN],
                                   ACT.Copy).then_inc(list_done, 1)
                    if side == 2:
                        act.wait_ge(summed_done, NT * (c + 1))
                        act.activation(o_grid[:, c, HALF:HALF + WIN, HALF:HALF + WIN],
                                       summed[:].rearrange("p (a b) -> p a b", b=WIN), ACT.Copy).then_inc(placed, 1)

        @block.vector
        def _(dve):
            for c in range(CC):
                dve.wait_ge(x_in[c], 16)
                for j in range(NS):
                    dve.bn_stats(raw[:, c, j, :], wide[:, c, j * SUP:(j + 1) * SUP]).then_inc(raw_done, 1)
            for c in range(CC):
                dve.wait_ge(raw_done, NS * (c + 1))
                dve.bn_aggr(chan[:, c, :], raw[:, c].rearrange("p a b -> p (a b)")).then_inc(chan_done, 1)
            dve.wait_ge(gm_ready, 1)
            dve.tensor_copy(gmean[:], ps[6][:, 0:CC]).then_inc(gm_copied, 1)
            dve.wait_ge(gm_copied, 1)
            dve.wait_ge(chan_done, CC)
            dve.tensor_tensor(dev[:], chan[:, :, 0], gmean[:], ALU.subtract).then_inc(dev_done, 1)
            dve.wait_ge(dev_done, 1)
            dve.tensor_tensor(dev2[:], dev[:], dev[:], ALU.mult).then_inc(dev_done, 1)
            dve.wait_ge(dev_done, 2)
            dve.tensor_tensor(dev[:], dev2[:], chan[:, :, 1], ALU.add).then_inc(dev_done, 1)
            dve.wait_ge(gm_ready, 2)
            dve.tensor_copy(spread[:], ps[7][:, 0:CC]).then_inc(gv_ready, 1)
            dve.wait_ge(std_done, 1)
            dve.reciprocal(rstd[:], std[:]).then_inc(std_done, 1)
            dve.wait_ge(std_done, 2)
            for c in range(CC):
                dve.tensor_scalar(xn[:, c, :], wide[:, c, :], gmean[:, c:c + 1], rstd[:, c:c + 1], ALU.subtract,
                                  ALU.mult).then_inc(xn_ready, 1)

            def add_bias(n):
                c, i = divmod(n, ITEMS)
                dve.wait_ge(s_ready, n + 1)
                if i < NT:
                    if mains(n) >= 2:
                        dve.wait_ge(mask_done, mains(n) - 1)
                    for h in range(HC):
                        tab = table[:]
                        tab = bass.AP(tab.tensor, tab.offset + (TAB0 + 2 * i) * HEADS + c * HC + h,
                                      [[tab.ap[0][0], TT], [6 * HEADS, WS], [0, WS], [-K2 * HEADS, T4]])
                        split = lambda a: a.rearrange("p (y x t) -> p y x t", y=WS, x=WS)
                        at = h % 2 * WCOLS
                        ins = dve.tensor_tensor(split(biased[0:TT, n % 2, h * WCOLS:(h + 1) * WCOLS]),
                                                split(ps[2 * (n % 2) + h // 2][0:TT, at:at + WCOLS]), tab, ALU.add)
                    ins.then_inc(bias_done, 1)
                else:
                    side, at, starts, corner = plan[i - NT]
                    if i == NT:
                        dve.wait_ge(class_in, 16 * 2 * WS)
                        dve.wait_ge(cleared, 4)
                    dve.wait_ge(o_ready, n - 1)
                    k0, dk = ((HALF * WS, 1), (HALF * WS + HALF + 1, 1), (HALF, WS), ((HALF + 1) * WS + HALF, WS))[side]
                    bank = ps[2 * (n % 2)]
                    for part, (lane, slots) in enumerate(HALVES):
                        rows = slice(lane, lane + K2)
                        cb = class_bias[rows]
                        bias = bass.AP(cb.tensor, cb.offset + k0 * HEADS + c * HC,
                                       [list(cb.ap[0]), [0, slots], [1, HC], [dk * HEADS, EDGE]])
                        dst = edge[rows, n % 2, 0:QX].rearrange("p (h l s q) -> p s l h q", h=HC, l=PB, s=2)[:, part, 0:slots]
                        src = bank[rows, 0:slots * PQ].rearrange("p (l h q) -> p l h q", l=slots, h=HC)
                        ins = dve.tensor_tensor(dst, src, bias, ALU.add)
                    if corner is not None:
                        kh, kw = side - 2, 0 if corner == 0 else 1
                        k0 = kh * (HALF + 1) * WS + kw * (HALF + 1)
                        cb = class_bias[0:K2]
                        bias = bass.AP(cb.tensor, cb.offset + k0 * HEADS + c * HC,
                                       [list(cb.ap[0]), [1, HC], [WS * HEADS, EDGE], [HEADS, EDGE]])
                        sc = lambda a: a.rearrange("p (h a b) -> p h a b", h=HC, a=EDGE)
                        ins = dve.tensor_tensor(sc(edge[0:K2, n % 2, QX:QX + QC]), sc(bank[0:K2, PB * PQ:PB * PQ + QC]), bias, ALU.add)
                    ins.then_inc(border_done, 1)

            def evac_values(n):
                c, i = divmod(n, ITEMS)
                m = c * NT + i
                dve.wait_ge(v_ready, m + 1)
                if m >= 4:
                    dve.wait_ge(o_ready, c * ITEMS + i - 3)
                    dve.wait_ge(v_out[m % 4], 16 * (m // 4))
                dve.tensor_tensor(v_tile[0:TT, i % 4, :], ps[4][0:TT, 0:128], vb_row[0:TT, c * 128:(c + 1) * 128],
                                  ALU.add).then_inc(v_evac, 1)

            def take_out(n):
                c, i = divmod(n, ITEMS)
                dve.wait_ge(o_ready, n + 1)
                bank = ps[5 + n % 2]
                if i < NT:
                    if i:
                        dve.wait_ge(summed_done, c * NT + i)
                    s = summed[:]
                    win = bass.AP(s.tensor, s.offset + 2 * i, [list(s.ap[0]), [DY, WS], [DX, WS], [1, T4]])
                    o = bank[:, 0:WCOLS].rearrange("p (y x t) -> p y x t", y=WS, x=WS)
                    dve.tensor_tensor(win, o, win, ALU.add).then_inc(summed_done, 1)
                else:
                    side, at, starts, corner = plan[i - NT]
                    lo = min(at)
                    for h in range(HC):
                        q = slice(32 * h, 32 * h + 32)
                        o = bank[q, h * HX:h * HX + BH * EDGE].rearrange("p (l q) -> p l q", q=EDGE)
                        if side < 2:
                            o = bass.AP(o.tensor, o.offset + (BH - 1) * EDGE, [list(o.ap[0]), [-EDGE, BH], [1, EDGE]])
                        g = o_grid[q, c]
                        rows = slice(HALF + lo, HALF + lo + BH)
                        if side == 0:
                            dst = g[:, rows, 0:EDGE]
                        elif side == 1:
                            dst = g[:, rows, SIDE - EDGE:SIDE]
                        elif side == 2:
                            dst = g[:, 0:EDGE, rows].rearrange("p a b -> p b a")
                        else:
                            dst = g[:, SIDE - EDGE:SIDE, rows].rearrange("p a b -> p b a")
                        ins = dve.tensor_copy(dst, o)
                        if corner is not None:
                            hs, ws = (SIDE - EDGE) * (side - 2), 0 if corner == 0 else SIDE - EDGE
                            o = bank[q, QX:QX + QC].rearrange("p (h a b) -> p h a b", h=HC, a=EDGE)[:, h]
                            ins = dve.tensor_copy(g[:, hs:hs + EDGE, ws:ws + EDGE], o)
                    ins.then_inc(o_used, 1)

            for c in range(CC):
                if c:
                    dve.wait_ge(o_ready, c * ITEMS)
                for j in range(NS):
                    dve.wait_ge(qk_ready, c * 2 * NS + j + 1)
                    if j == 0:
                        dve.wait_ge(w_in, 16 * 6)
                    dve.tensor_scalar(queries[:, j * SUP:(j + 1) * SUP], ps[(c * 2 * NS + j) % 4][:, 0:SUP], qkb[:, c:c + 1],
                                      SCALE, ALU.add, ALU.mult).then_inc(q_evac, 1)
                dve.wait_ge(q_evac, NS * (c + 1))
                dve.wait_ge(cleared, 3)
                for h in range(HC):
                    q = slice(32 * h, 32 * h + 32)
                    dve.tensor_copy(q_diag[q, h, :].rearrange("p (a b) -> p a b", b=WIN),
                                    q_grid[q, HALF:HALF + WIN, HALF:HALF + WIN]).then_inc(diag_done, 1)
                dve.wait_ge(summed_clear, c + 1)
                dve.wait_ge(tab_in, 48)
                for i in range(ITEMS):
                    n = c * ITEMS + i
                    if i < NT:
                        evac_values(n)
                    add_bias(n)
                    if i >= 2:
                        take_out(n - 2)
                take_out(c * ITEMS + ITEMS - 2)
                take_out(c * ITEMS + ITEMS - 1)
            for i in range(NT + 1):
                if i < NT:
                    dve.wait_ge(p_ready, i + 1)
                    dve.tensor_tensor(tiles[0:TT, i, :], ps[i % 4][0:TT, 0:CH], pb_row[0:TT, :], ALU.add).then_inc(p_done, 1)
                if i:
                    dve.wait_ge(p_done, i)
                    dve.bn_stats(t_raw[0:TT, i - 1, :], tiles[0:TT, i - 1, :]).then_inc(ts_done, 1)
            for i in range(NT):
                dve.wait_ge(ts_done, i + 1)
                dve.bn_aggr(stats[0:TT, i, :], t_raw[0:TT, i, :])

        @block.tensor
        def _(pe):
            pe.wait_ge(w_in, 16 * 6)
            pe.wait_ge(chan_done, CC)
            pe.matmul(ps[6][:, 0:CC], group[:], chan[:, :, 0], start=True, stop=True).then_inc(gm_ready, 1)
            pe.wait_ge(dev_done, 3)
            pe.matmul(ps[7][:, 0:CC], group[:], dev[:], start=True, stop=True).then_inc(gm_ready, 1)
            pe.wait_ge(xn_ready, CC)

            def scores_of(n):
                c, i = divmod(n, ITEMS)
                if i < NT:
                    m = c * NT + i
                    if m:
                        pe.wait_ge(v_evac, m)
                    for k in range(CC):
                        mm = pe.matmul(ps[4][0:TT, 0:128], xn[:, k, i * TT:(i + 1) * TT],
                                       wqkv[:, k, 2 * CH + c * 128:2 * CH + (c + 1) * 128], start=(k == 0), stop=(k == CC - 1))
                    mm.then_inc(v_ready, 1)
                if n >= 2:
                    pe.wait_ge(bias_done, mains(n - 1))
                    if borders(n - 1):
                        pe.wait_ge(border_done, borders(n - 1))
                if i < NT:
                    qd = q_diag[:]
                    for h in range(HC):
                        win = bass.AP(qd.tensor, qd.offset + h * L + 2 * i, [list(qd.ap[0]), [DY, WS], [DX, WS], [1, T4]])
                        at = h % 2 * WCOLS
                        mm = pe.matmul(ps[2 * (n % 2) + h // 2][0:TT, at:at + WCOLS], keys[:, i * TT:(i + 1) * TT], win,
                                       start=True, stop=True)
                    mm.then_inc(s_ready, 1)
                else:
                    side, at, starts, corner = plan[i - NT]
                    if i == NT:
                        pe.wait_ge(border_q_done, c + 1)
                    if side == 2:
                        pe.wait_ge(list_done, 2 * c + 1)
                    if side == 3:
                        pe.wait_ge(list_done, 2 * c + 2)
                    src = keys if side < 2 else key_list
                    bank = ps[2 * (n % 2)]
                    for slot in range(BH):
                        pair, part = divmod(slot, 2)
                        lane, first = HALVES[part][0], starts[slot]
                        mm = pe.matmul(bank[lane:lane + K2, pair * PQ:(pair + 1) * PQ], src[:, first:first + K2],
                                       q_border[:, side, at[slot], :, :].rearrange("p a b -> p (a b)"), start=True, stop=True)
                    if corner is not None:
                        assert corner % 2 == 0
                        first = starts[corner]
                        k = 2 * (side - 2) + (0 if corner == 0 else 1)
                        mm = pe.matmul(bank[0:K2, PB * PQ:PB * PQ + QC], src[:, first:first + K2],
                                       q_corner[:, k, :, :].rearrange("p a b -> p (a b)"), start=True, stop=True)
                    mm.then_inc(s_ready, 1)

            def weigh_values(n):
                c, i = divmod(n, ITEMS)
                if n >= 2:
                    pe.wait_ge(summed_done, mains(n - 1))
                    if borders(n - 1):
                        pe.wait_ge(o_used, borders(n - 1))
                bank = ps[5 + n % 2]
                if i < NT:
                    pe.wait_ge(mask_done, mains(n) + 1)
                    for h in range(HC):
                        mm = pe.matmul(bank[32 * h:32 * h + 32, 0:WCOLS], v_tile[0:TT, i % 4, 32 * h:32 * h + 32],
                                       scores[0:TT, n % 2, h * WCOLS:(h + 1) * WCOLS], start=True, stop=True)
                    mm.then_inc(o_ready, 1)
                else:
                    kk = c * NB + i - NT
                    side, at, starts, corner = plan[i - NT]
                    pe.wait_ge(border_done, borders(n) + 1)
                    pe.wait_ge(vb_in[kk % 2], reached[kk])
                    lanes = HALVES[1][0] + K2
                    for pair in range(PB):
                        for h in range(HC):
                            rows, cols = slice(32 * h, 32 * h + 32), slice(h * HX + 2 * pair * EDGE, h * HX + 2 * (pair + 1) * EDGE)
                            mm = pe.matmul(bank[rows, cols], v_border[kk % 2][0:lanes, pair, rows], edge[0:lanes, n % 2, cols],
                                           start=True, stop=True)
                    if corner is not None:
                        for h in range(HC):
                            rows, cols = slice(32 * h, 32 * h + 32), slice(QX + h * EDGE * EDGE, QX + (h + 1) * EDGE * EDGE)
                            mm = pe.matmul(bank[rows, cols], v_border[kk % 2][0:K2, corner // 2, rows], edge[0:K2, n % 2, cols],
                                           start=True, stop=True)
                    mm.then_inc(o_ready, 1)

            for c in range(CC):
                if c:
                    pe.wait_ge(bias_done, mains(c * ITEMS))
                    pe.wait_ge(border_done, borders(c * ITEMS))
                for m in range(2 * NS):
                    if m >= 4:
                        if m - 4 < NS:
                            pe.wait_ge(q_evac, c * NS + m - 3)
                        else:
                            pe.wait_ge(k_evac, c * NS + m - 3 - NS)
                    kind, j = divmod(m, NS)
                    bank = ps[(c * 2 * NS + m) % 4]
                    for k in range(CC):
                        mm = pe.matmul(bank[:, 0:SUP], wqkv[:, k, kind * CH + c * 128:kind * CH + (c + 1) * 128],
                                       xn[:, k, j * SUP:(j + 1) * SUP], start=(k == 0), stop=(k == CC - 1))
                    mm.then_inc(qk_ready, 1)
                pe.wait_ge(k_evac, NS * (c + 1))
                pe.wait_ge(q_evac, NS * (c + 1))
                pe.wait_ge(diag_done, HC * (c + 1))
                for i in range(ITEMS):
                    scores_of(c * ITEMS + i)
                    if i >= 2:
                        weigh_values(c * ITEMS + i - 2)
                weigh_values(c * ITEMS + ITEMS - 2)
                weigh_values(c * ITEMS + ITEMS - 1)
            pe.wait_ge(o_used, CC * NB)
            pe.wait_ge(placed, CC)
            pe.wait_ge(xres_in, 16 * CC)
            for i in range(NT):
                if i >= 4:
                    pe.wait_ge(p_done, i - 3)
                bank = ps[i % 4]
                pe.matmul(bank[0:TT, 0:CH], wide[:, 0, i * TT:(i + 1) * TT], wproj[:, 0, :], start=True, stop=False)
                for c in range(CC):
                    pe.matmul(bank[0:TT, c * 128:(c + 1) * 128], x_again[:, c, i * TT:(i + 1) * TT], ident[:],
                              start=False, stop=False, skip_group_check=True)
                mm = pe.matmul(bank[0:TT, 0:CH], wide[:, 1, i * TT:(i + 1) * TT], wproj[:, 1, :], start=False, stop=True)
                mm.then_inc(p_ready, 1)


def project_qkv(nc, sem, ps, ident, ident_b, eps, wide, stats, tiles, exp_scale, w_qkv, b_qkv, parts, stream_rows, v1_rows):
    with ExitStack() as mem:
        def sb(name, shape, dt=F32):
            return mem.enter_context(nc.sbuf_tensor(name, shape, dt))

        w = sb("w1_qkv", [128, CC, 3 * CH])
        qkb = sb("b1_qk", [128, 2 * CC])
        vb_row = sb("vb1_row", [128, CH])
        std = sb("std1", [128, NT])
        rstd = sb("rstd1", [128, NT])
        xhat = sb("xhat", [128, 4, CH])
        full = sb("full", [128, 2, CC, TOK])
        split = sb("split", [128, 4, 2, SUP], F16)
        v_tile = sb("v1_tile", [128, 4, CH])
        largest = sb("largest", [128, 2, CC * NS])
        largest_of = sb("largest_of", [128, 2])
        two = sb("two", [2, 4])
        rows2 = sb("rows2", [2, 4])
        ones2 = sb("ones2", [2, 128])
        factors = sb("factors", [128, 4])

        w_in, std_done, rstd_done, xhat_done = sem("b_w_in"), sem("b_std_done"), sem("b_rstd_done"), sem("b_xhat_done")
        turned, turned_evac, stream_out = sem("b_turned"), sem("b_turned_evac"), sem("b_stream_out")
        qk_ready, full_done, largest_done = sem("b_qk_ready"), sem("b_full_done"), sem("b_largest_done")
        across, chain, ones_set, factors_done = sem("b_across"), sem("b_chain"), sem("b_ones_set"), sem("b_factors_done")
        hi_done, lo_done = sem("b_hi_done"), sem("b_lo_done")
        parts_out = [sem(f"b_parts_out{i}") for i in range(4)]
        v_out = [sem(f"b_v_out{i}") for i in range(4)]
        v_ready, v_evac = sem("b_v_ready"), sem("b_v_evac")
        UNITS = 2 * CC * NS
        assert UNITS == NT

        def unit(m):
            kind, rem = divmod(m, CC * NS)
            return kind, rem // NS, slice(rem % NS * SUP, (rem % NS + 1) * SUP)

        block = mem.enter_context(nc.Block())

        @block.sync
        def _(sp):
            sp.dma_start(w[:], w_qkv.rearrange("(c p) o -> p c o", p=128)).then_inc(w_in, 16)
            with nc.allow_non_contiguous_dma(reason="a bias by channel"):
                sp.dma_start(qkb[:], b_qkv[0:2 * CH].rearrange("(c p) -> p c", p=128)).then_inc(w_in, 16)
            sp.dma_start(vb_row[0:TT, :], b_qkv[2 * CH:3 * CH].rearrange("(a c) -> a c", a=1).broadcast_to([TT, CH])).then_inc(w_in, 16)
            sp.dma_start(stream_rows.rearrange("(i t) c -> t i c", t=TT), tiles[0:TT]).then_inc(stream_out, 16)
            for m in range(UNITS):
                kind, c, cols = unit(m)
                sp.wait_ge(lo_done, m + 1)
                sp.dma_start(parts[kind, c, :, :, cols].rearrange("s p t -> p s t"), split[:, m % 4]).then_inc(parts_out[m % 4], 16)
                sp.wait_ge(v_evac, m + 1)
                sp.dma_start(v1_rows[m * TT:(m + 1) * TT, :], v_tile[0:TT, m % 4, :]).then_inc(v_out[m % 4], 16)
            for i in range(4):
                sp.wait_ge(parts_out[i], 16 * UNITS // 4)
                sp.wait_ge(v_out[i], 16 * UNITS // 4)
            sp.wait_ge(stream_out, 16)

        @block.gpsimd
        def _(pool):
            pool.memset(ones2[:], 1.0).then_inc(ones_set, 1)

        @block.scalar
        def _(act):
            act.activation(std[0:TT, :], stats[0:TT, :, 1], ACT.Sqrt, bias=eps[0:TT, 0:1]).then_inc(std_done, 1)
            for i in range(NT):
                act.wait_ge(turned, i + 1)
                act.activation(wide[:, :, i * TT:(i + 1) * TT], ps[i % 4][:, 0:2 * TT].rearrange("p (c t) -> p c t", c=CC),
                               ACT.Copy).then_inc(turned_evac, 1)
            act.wait_ge(factors_done, 1)
            for m in range(UNITS):
                kind, c, cols = unit(m)
                if m >= 4:
                    act.wait_ge(parts_out[m % 4], 16 * (m // 4))
                act.activation(split[:, m % 4, 0, :], full[:, kind, c, cols], ACT.Copy, scale=factors[:, kind:kind + 1]).then_inc(hi_done, 1)

        @block.vector
        def _(dve):
            count = [0]

            def link(ins):
                count[0] += 1
                ins.then_inc(chain, 1)
                dve.wait_ge(chain, count[0])

            dve.wait_ge(std_done, 1)
            dve.reciprocal(rstd[0:TT, :], std[0:TT, :]).then_inc(rstd_done, 1)
            dve.wait_ge(rstd_done, 1)
            for i in range(NT):
                if i >= 4:
                    dve.wait_ge(turned, i - 3)
                dve.tensor_scalar(xhat[0:TT, i % 4, :], tiles[0:TT, i, :], stats[0:TT, i, 0:1], rstd[0:TT, i:i + 1],
                                  ALU.subtract, ALU.mult).then_inc(xhat_done, 1)
            dve.wait_ge(w_in, 48)
            for m in range(UNITS + 1):
                if m < UNITS:
                    kind, c, cols = unit(m)
                    dve.wait_ge(qk_ready, m + 1)
                    dve.tensor_scalar(full[:, kind, c, cols], ps[m % 4][:, 0:SUP], qkb[:, kind * CC + c:kind * CC + c + 1],
                                      SCALE if kind == 0 else 1.0, ALU.add, ALU.mult).then_inc(full_done, 1)
                if m:
                    kind, c, cols = unit(m - 1)
                    dve.wait_ge(full_done, m)
                    k = (m - 1) % (CC * NS)
                    dve.tensor_reduce(largest[:, kind, k:k + 1], full[:, kind, c, cols], AX.X, ALU.max,
                                      apply_absolute_value=True).then_inc(largest_done, 1)
            dve.wait_ge(largest_done, UNITS)
            dve.tensor_reduce(largest_of[:], largest[:], AX.X, ALU.max).then_inc(largest_done, 1)
            dve.wait_ge(across, 1)
            link(dve.tensor_reduce(two[:, 0:1], ps[0][0:2, 0:128], AX.X, ALU.max))
            link(dve.tensor_scalar(two[:, 1:2], two[:, 0:1], 1e-6, None, ALU.max))
            link(dve.reciprocal(two[:, 2:3], two[:, 1:2]))
            dve.tensor_scalar(rows2[:, 0:2], ident[0:2, 0:2], two[:, 2:3], SPLIT_MAX, ALU.mult, ALU.mult)
            link(dve.tensor_scalar(rows2[:, 2:4], ident[0:2, 0:2], two[:, 1:2], 1.0 / SPLIT_MAX, ALU.mult, ALU.mult))
            dve.wait_ge(across, 2)
            dve.tensor_copy(factors[:], ps[1][:, 0:4]).then_inc(factors_done, 1)
            dve.wait_ge(factors_done, 1)
            dve.tensor_tensor(exp_scale[:], factors[:, 2:3], factors[:, 3:4], ALU.mult)
            for m in range(UNITS):
                kind, c, cols = unit(m)
                dve.wait_ge(hi_done, m + 1)
                dve.scalar_tensor_tensor(out=split[:, m % 4, 1, :], in0=full[:, kind, c, cols], scalar=factors[:, kind:kind + 1],
                                         in1=split[:, m % 4, 0, :], op0=ALU.mult, op1=ALU.subtract).then_inc(lo_done, 1)
                dve.wait_ge(v_ready, m + 1)
                if m >= 4:
                    dve.wait_ge(v_out[m % 4], 16 * (m // 4))
                dve.tensor_tensor(v_tile[0:TT, m % 4, :], ps[4 + m % 4][0:TT, 0:CH], vb_row[0:TT, :], ALU.add).then_inc(v_evac, 1)

        @block.tensor
        def _(pe):
            for i in range(NT):
                pe.wait_ge(xhat_done, i + 1)
                if i >= 4:
                    pe.wait_ge(turned_evac, i - 3)
                for c in range(CC):
                    mm = pe.transpose(ps[i % 4][:, c * TT:(c + 1) * TT], xhat[0:TT, i % 4, c * 128:(c + 1) * 128], ident[0:TT, 0:TT])
                mm.then_inc(turned, 1)
            pe.wait_ge(turned_evac, NT)
            pe.wait_ge(w_in, 48)
            for m in range(UNITS):
                kind, c, cols = unit(m)
                if m >= 4:
                    pe.wait_ge(full_done, m - 3)
                for k in range(CC):
                    mm = pe.matmul(ps[m % 4][:, 0:SUP], w[:, k, kind * CH + c * 128:kind * CH + (c + 1) * 128],
                                   wide[:, k, cols], start=(k == 0), stop=(k == CC - 1))
                mm.then_inc(qk_ready, 1)
            pe.wait_ge(largest_done, UNITS + 1)
            pe.transpose(ps[0][0:2, 0:128], largest_of[:], ident[:]).then_inc(across, 1)
            pe.wait_ge(chain, 4)
            pe.wait_ge(ones_set, 1)
            pe.matmul(ps[1][:, 0:4], ones2[:], rows2[:], start=True, stop=True).then_inc(across, 1)
            for i in range(NT):
                if i >= 4:
                    pe.wait_ge(v_evac, i - 3)
                for k in range(CC):
                    mm = pe.matmul(ps[4 + i % 4][0:TT, 0:CH], wide[:, k, i * TT:(i + 1) * TT], w[:, k, 2 * CH:3 * CH],
                                   start=(k == 0), stop=(k == CC - 1))
                mm.then_inc(v_ready, 1)


def attention_order():
    def max_units(c, s):
        out, rows = [], []
        for h in range(HC):
            for ii in range(4):
                if ii == 2:
                    out += rows
                    rows = []
                out += [("max", c, s, h, ii, kc, min(MAX_BANKS, s - kc)) for kc in range(0, s, MAX_BANKS)]
                out.append(("max", c, s, h, ii, s, 0))
            rows.append(("row", c, s, h))
        return out + rows

    def main_units(c, s):
        out, full = [], 4 * s
        for j in range(full + 4):
            out += [("st", c, s, j, 0), ("st", c, s, j, 1)]
            if j >= 2:
                out.append(("pv", c, s, j - 2))
            out += [("st", c, s, j, 2), ("st", c, s, j, 3)]
            if j >= 4 and j % 2 == 0 and j - 4 < full:
                out.append(("den", c, s, j - 4, 2))
            if j - 2 >= full:
                out.append(("den", c, s, j - 2, 1))
        for j in (full + 2, full + 3):
            out += [("pv", c, s, j), ("den", c, s, j, 1)]
        return out

    def cost(u):
        return max(1, u[6]) if u[0] == "max" else 1 if u[0] in ("st", "row") else 4

    steps = [(c, s) for c in range(CC) for s in range(NS)]
    maxima, mains = [max_units(*k) for k in steps], [main_units(*k) for k in steps]
    order = list(maxima[0])
    ahead = [u for units in maxima[1:] for u in units]
    given, due = 0, [0]
    for units in maxima[1:]:
        due.append(due[-1] + sum(map(cost, units)))
    emitted = 0
    for k, units in enumerate(mains):
        left = sum(map(cost, units))
        starts = []
        for later in range(k + 1, len(steps)):
            starts.append((left, due[later]))
            left += sum(map(cost, mains[later]))
        gone, base = 0, given
        for u in units:
            order.append(u)
            gone += cost(u)
            want = base + gone * max([(need - base) / work for work, need in starts], default=0)
            if u is units[-1]:
                want, most = due[k + 1] if k + 1 < len(due) else given, len(ahead)
            else:
                most = 1
            while emitted < len(ahead) and given < want - 1e-6 and most:
                order.append(ahead[emitted])
                given += cost(ahead[emitted])
                emitted += 1
                most -= 1
    return order


def causal_attention(nc, sem, ps, ident, ident_b, eps, wide, stats, banks, exp_scale, v1_rows, parts, causal_q_in, causal_k_in, unit_row_in):
    with ExitStack() as mem:
        def sb(name, shape, dt=F32):
            return mem.enter_context(nc.sbuf_tensor(name, shape, dt))

        STEPS = 4
        qs_ = [sb(f"q_terms{c}", [97, HC, TOK], F16) for c in range(CC)]
        ks_ = [sb(f"k_terms{c}", [97, HC, TOK], F16) for c in range(CC)]
        values = sb("values", [128, NT, CH])
        probs = sb("probs", [128, STEPS * HC, SUP])
        pairs = sb("pairs", [128, 2, HC, SUP])
        causal_q = sb("causal_q", [TT, TT], BF16)
        causal_k = sb("causal_k", [TT, TT], BF16)
        ones = sb("ones", [128, 32])
        top = sb("top", [128, HC, 4, NS])
        most = sb("most", [128, HC, 4])
        minus = sb("minus", [128, HC, 4], F16)
        recip = sb("recip", [128, SUP])

        m_in, v_in, ones_set = sem("c_m_in"), sem("c_v_in"), sem("c_ones_set")
        unit_in = [sem(f"c_unit_in{c}") for c in range(CC)]
        PIECES = [[(0, 1), (1, 3), (3, NS)], [(0, NS)]]
        terms_in = [[sem(f"c_terms_in{c}{k}") for k in range(len(PIECES[c]))] for c in range(CC)]
        max_ready, max_done, most_done, minus_done = sem("c_max_ready"), sem("c_max_done"), sem("c_most_done"), sem("c_minus_done")
        row_ready, row_copied = sem("c_row_ready"), sem("c_row_copied")
        st_ready, exp_done, pv_done, pair_done = sem("c_st_ready"), sem("c_exp_done"), sem("c_pv_done"), sem("c_pair_done")
        den_done, recip_done, y_done = sem("c_den_done"), sem("c_recip_done"), sem("c_y_done")

        MAXIMA = list(range(0, MAX_BANKS * MAX_SLOTS, MAX_BANKS))
        ST = list(range(MAX_BANKS * MAX_SLOTS, 6))
        ACC, DEN = 6, 7

        order = attention_order()
        number = {}
        for kind in ("max", "row", "st", "pv", "den"):
            number.update({u: n for n, u in enumerate([u for u in order if u[0] == kind])})
        wide_units = [u for u in order if u[0] in ("max", "row")]
        slot = {u: n for n, u in enumerate(wide_units)}
        paired = [u for u in order if u[0] == "den" and u[4] == 2]
        pair_no = {u: n for n, u in enumerate(paired)}
        read_by = {}
        for u in order:
            if u[0] == "den":
                for j in range(u[3], u[3] + u[4]):
                    read_by[number[("pv", u[1], u[2], j)]] = u

        def freed(eng, step):
            eng.wait_ge(pv_done, step + 1)
            u = read_by[step]
            if u[4] == 2:
                eng.wait_ge(pair_done, HC * (pair_no[u] + 1))
            else:
                eng.wait_ge(den_done, number[u] + 1)

        block = mem.enter_context(nc.Block())

        def load_terms(eng, kind):
            for c in range(CC):
                dst = (qs_, ks_)[kind][c]
                for k, (a, b) in enumerate(PIECES[c]):
                    cols = slice(a * SUP, b * SUP)
                    for at, term in enumerate(((0, 1, 0), (0, 0, 1))[kind]):
                        eng.dma_start(dst[32 * at:32 * at + 32, :, cols],
                                      parts[kind, c, term, :, cols].rearrange("(h p) t -> p h t", h=HC)).then_inc(terms_in[c][k], 16)
                    if c == 0 and k == 0:
                        eng.wait_ge(terms_in[0][0], 16 * 6)
                    if c == 0 and k == 0 and kind == 1:
                        eng.dma_start(values[0:TT], v1_rows.rearrange("(i t) c -> t i c", t=TT)).then_inc(v_in, 16)

        @block.sync
        def _(sp):
            sp.dma_start(causal_q[:], causal_q_in).then_inc(m_in, 16)
            sp.dma_start(causal_k[:], causal_k_in).then_inc(m_in, 16)
            for c in range(CC):
                sp.dma_start(ks_[c][96:97], unit_row_in.rearrange("(a h t) -> a h t", a=1, h=HC)).then_inc(unit_in[c], 16)
            load_terms(sp, 0)

        @block.gpsimd
        def _(pool):
            pool.memset(ones[:], 1.0).then_inc(ones_set, 1)
            pool.wait_ge(ones_set, 1)
            for u in paired:
                _, c, s, j, _ = u
                n, step = pair_no[u], number[("pv", c, s, j)]
                for h in range(HC):
                    pool.wait_ge(exp_done, HC * (step + 1) + h + 1)
                    if n >= 2:
                        pool.wait_ge(den_done, number[paired[n - 2]] + 1)
                    a, b = (probs[0:TT, (HC * (step + k) + h) % (STEPS * HC), :] for k in range(2))
                    pool.tensor_tensor(pairs[0:TT, n % 2, h, :], a, b, ALU.add).then_inc(pair_done, 1)

        @block.scalar
        def _(act):
            load_terms(act, 1)
            for u in order:
                if u[0] == "row":
                    _, c, s, h = u
                    k = MAXIMA[slot[u] % MAX_SLOTS]
                    act.wait_ge(row_ready, number[u] + 1)
                    act.activation(qs_[c][96:97, h, s * SUP:(s + 1) * SUP], ps[k][96:97, 0:SUP], ACT.Copy).then_inc(row_copied, 1)
                if u[0] == "st":
                    _, c, s, j, h = u
                    n, at = number[u], max(0, j - 4 * s) * TT
                    act.wait_ge(st_ready, n + 1)
                    step = n // HC
                    if step >= STEPS and h == 0:
                        freed(act, step - STEPS)
                    act.activation(probs[0:TT, n % (STEPS * HC), at:SUP], ps[ST[n % len(ST)]][0:TT, at:SUP], ACT.Exp,
                                   scale=exp_scale[0:TT, 0:1]).then_inc(exp_done, 1)

        @block.vector
        def _(dve):
            for u in order:
                if u[0] == "max":
                    _, c, s, h, ii, kc, full = u
                    n, k = number[u], MAXIMA[slot[u] % MAX_SLOTS]
                    dve.wait_ge(max_ready, n + 1)
                    if full:
                        src = banks[0:TT, k:k + full, 0:SUP]
                        dve.tensor_reduce(top[0:TT, h, ii, kc // MAX_BANKS:kc // MAX_BANKS + 1], src, AX.XY, ALU.max).then_inc(max_done, 1)
                        continue
                    last = -(-s // MAX_BANKS)
                    dve.tensor_reduce(top[0:TT, h, ii, last:last + 1], ps[k][0:TT, 0:(ii + 1) * TT], AX.X, ALU.max).then_inc(max_done, 1)
                    if ii == 3:
                        r = number[("row", c, s, h)]
                        dve.wait_ge(max_done, n + 1)
                        dve.tensor_reduce(most[0:TT, h, :], top[0:TT, h, :, 0:last + 1], AX.X, ALU.max).then_inc(most_done, 1)
                        dve.wait_ge(most_done, r + 1)
                        if r >= HC:
                            dve.wait_ge(row_ready, r - HC + 1)
                        dve.tensor_scalar(minus[0:TT, h, :], most[0:TT, h, :], -1.0 / ROW_UNIT, None, ALU.mult).then_inc(minus_done, 1)
                if u[0] == "den" and u[3] == 4 * u[2] + 3:
                    _, c, s, _, _ = u
                    n = c * NS + s
                    dve.wait_ge(den_done, number[u] + 1)
                    dve.reciprocal(recip[:], ps[DEN][:, 0:SUP]).then_inc(recip_done, 1)
                    dve.wait_ge(recip_done, n + 1)
                    dve.tensor_tensor(wide[:, c, s * SUP:(s + 1) * SUP], ps[ACC][:, 0:SUP], recip[:], ALU.mult).then_inc(y_done, 1)

        @block.tensor
        def _(pe):
            pe.wait_ge(ones_set, 1)
            seen = set()
            for u in order:
                if u[0] in ("max", "row") and slot[u] >= MAX_SLOTS:
                    before = wide_units[slot[u] - MAX_SLOTS]
                    if before[0] == "max":
                        pe.wait_ge(max_done, number[before] + 1)
                    else:
                        pe.wait_ge(row_copied, number[before] + 1)
                if u[0] == "max":
                    _, c, s, h, ii, kc, full = u
                    n, k = number[u], MAXIMA[slot[u] % MAX_SLOTS]
                    for piece, (a, _) in enumerate(PIECES[c]):
                        if s >= a and (c, piece) not in seen:
                            seen.add((c, piece))
                            pe.wait_ge(terms_in[c][piece], 16 * 6)
                    i = 4 * s + ii
                    q = qs_[c][0:96, h, i * TT:(i + 1) * TT]
                    if full:
                        for b in range(full):
                            mm = pe.matmul(ps[k + b][0:TT, 0:SUP], q, ks_[c][0:96, h, (kc + b) * SUP:(kc + b + 1) * SUP], start=True, stop=True)
                    else:
                        if n == 0:
                            pe.wait_ge(m_in, 32)
                        pe.matmul(ps[k][0:TT, 0:(ii + 1) * TT], q, ks_[c][0:96, h, s * SUP:s * SUP + (ii + 1) * TT], start=True, stop=False)
                        mm = pe.matmul(ps[k][0:TT, ii * TT:(ii + 1) * TT], ident_b[0:TT, 0:TT], causal_q[:], start=False, stop=True)
                    mm.then_inc(max_ready, 1)
                elif u[0] == "row":
                    _, c, s, h = u
                    r, k = number[u], MAXIMA[slot[u] % MAX_SLOTS]
                    pe.wait_ge(minus_done, r + 1)
                    for ii in range(4):
                        mm = pe.matmul(ps[k][96:97, ii * TT:(ii + 1) * TT], minus[0:TT, h, ii:ii + 1], ident_b[0:TT, 0:TT],
                                       start=True, stop=True, tile_position=(0, 96))
                    mm.then_inc(row_ready, 1)
                elif u[0] == "st":
                    _, c, s, j, h = u
                    n, at = number[u], max(0, j - 4 * s) * TT
                    if j == 0:
                        pe.wait_ge(row_copied, number[("row", c, s, h)] + 1)
                        if s == 0:
                            pe.wait_ge(unit_in[c], 16)
                    if n >= len(ST):
                        pe.wait_ge(exp_done, n - len(ST) + 1)
                    bank = ps[ST[n % len(ST)]]
                    diag = j >= 4 * s
                    mm = pe.matmul(bank[0:TT, at:SUP], ks_[c][:, h, j * TT:(j + 1) * TT], qs_[c][:, h, s * SUP + at:(s + 1) * SUP],
                                   start=True, stop=not diag)
                    if diag:
                        mm = pe.matmul(bank[0:TT, at:at + TT], ident_b[0:TT, 0:TT], causal_k[:], start=False, stop=True)
                    mm.then_inc(st_ready, 1)
                elif u[0] == "pv":
                    _, c, s, j = u
                    n, at = number[u], max(0, j - 4 * s) * TT
                    if j == 0 and c * NS + s:
                        pe.wait_ge(y_done, c * NS + s)
                    if n == 0:
                        pe.wait_ge(v_in, 16)
                    pe.wait_ge(exp_done, HC * (n + 1))
                    for h in range(HC):
                        col = c * 128 + 32 * h
                        mm = pe.matmul(ps[ACC][32 * h:32 * h + 32, at:SUP], values[0:TT, j, col:col + 32],
                                       probs[0:TT, (HC * n + h) % (STEPS * HC), at:SUP], start=(j == 0), stop=(j == 4 * s + 3),
                                       skip_group_check=True)
                    mm.then_inc(pv_done, 1)
                else:
                    _, c, s, j, two = u
                    step, at = number[("pv", c, s, j)], max(0, j - 4 * s) * TT
                    if two == 2:
                        pe.wait_ge(pair_done, HC * (pair_no[u] + 1))
                    for h in range(HC):
                        src = pairs[0:TT, pair_no[u] % 2, h, :] if two == 2 else probs[0:TT, (HC * step + h) % (STEPS * HC), at:SUP]
                        mm = pe.matmul(ps[DEN][32 * h:32 * h + 32, at:SUP], ones[0:TT, :], src, start=(j == 0), stop=(j == 4 * s + 3),
                                       skip_group_check=True)
                    mm.then_inc(den_done, 1)


def attention_out(image, nc, sem, ps, ident, ident_b, eps, wide, stats, stream_rows, w_proj, b_proj, resid, normed_t):
    with ExitStack() as mem:
        def sb(name, shape, dt=F32):
            return mem.enter_context(nc.sbuf_tensor(name, shape, dt))

        GT = SUP // TT
        w = sb("w_proj1", [128, CC, CH])
        pb_row = sb("pb1_row", [128, CH])
        tiles = sb("tiles_again", [128, NT, CH])
        raw = sb("raw2", [128, NT, 6])
        std = sb("std2", [128, NT])
        rstd = sb("rstd2", [128, NT])
        stream = sb("stream", [128, NT, CH])
        xhat = sb("xhat2", [128, 2 * GT, CH])
        both = sb("both", [128, 2, GT, CH])
        turned_sb = sb("turned_sb", [128, 2, CC, SUP])

        w_in, added, p_ready, p_done = sem("d_w_in"), sem("d_added"), sem("d_p_ready"), sem("d_p_done")
        bias_in, tiles_in = sem("d_bias_in"), [sem(f"d_tiles_in{g}") for g in range(NS)]
        raw_done, agg_done, std_done, rstd_done = sem("d_raw_done"), sem("d_agg_done"), sem("d_std_done"), sem("d_rstd_done")
        xhat_done, both_done, turned, turned_evac = sem("d_xhat_done"), sem("d_both_done"), sem("d_turned"), sem("d_turned_evac")
        resid_out = [sem(f"d_resid_out{i}") for i in range(2)]
        normed_out = [sem(f"d_normed_out{i}") for i in range(2)]
        block = mem.enter_context(nc.Block())

        @block.sync
        def _(sp):
            sp.dma_start(w[:], w_proj.rearrange("(c p) o -> p c o", p=128)).then_inc(w_in, 16)
            sp.dma_start(pb_row[0:TT, :], b_proj.rearrange("(a c) -> a c", a=1).broadcast_to([TT, CH])).then_inc(bias_in, 16)
            for g in range(NS):
                sp.dma_start(tiles[0:TT, g * GT:(g + 1) * GT, :],
                             stream_rows[g * SUP:(g + 1) * SUP, :].rearrange("(i t) c -> t i c", t=TT)).then_inc(tiles_in[g], 16)
            for g in range(NS):
                cols = slice(g * SUP, (g + 1) * SUP)
                sp.wait_ge(both_done, GT * (g + 1))
                sp.dma_start(resid[bass.ds(image, 1), cols, :].rearrange("a (i t) c -> t (a i) c", t=TT), both[0:TT, g % 2]).then_inc(resid_out[g % 2], 16)
                sp.wait_ge(turned_evac, GT * (g + 1))
                sp.dma_start(normed_t[bass.ds(image, 1), :, cols].rearrange("a (c p) t -> p (a c) t", p=128),
                             turned_sb[:, g % 2]).then_inc(normed_out[g % 2], 16)
            for i in range(2):
                sp.wait_ge(resid_out[i], 16 * ((NS + 1 - i) // 2))
                sp.wait_ge(normed_out[i], 16 * ((NS + 1 - i) // 2))

        @block.scalar
        def _(act):
            for g in range(NS + 1):
                if g < NS:
                    cols = slice(g * GT, (g + 1) * GT)
                    act.wait_ge(agg_done, GT * (g + 1))
                    act.activation(std[0:TT, cols], stats[0:TT, cols, 1], ACT.Sqrt, bias=eps[0:TT, 0:1]).then_inc(std_done, 1)
                if g:
                    for i in range(GT * (g - 1), GT * g):
                        act.wait_ge(turned, i + 1)
                        if g >= 3:
                            act.wait_ge(normed_out[(g - 1) % 2], 16 * ((g - 1) // 2))
                        at = i % GT * TT
                        act.activation(turned_sb[:, (g - 1) % 2, :, at:at + TT], ps[4 + i % 4][:, 0:2 * TT].rearrange("p (c t) -> p c t", c=CC),
                                       ACT.Copy).then_inc(turned_evac, 1)

        @block.gpsimd
        def _(pool):
            pool.wait_ge(bias_in, 16)
            for g in range(NS + 1):
                if g < NS:
                    pool.wait_ge(tiles_in[g], 16)
                    for i in range(GT * g, GT * (g + 1)):
                        pool.tensor_tensor(tiles[0:TT, i, :], tiles[0:TT, i, :], pb_row[0:TT, :], ALU.add).then_inc(added, 1)
                if g:
                    for i in range(GT * (g - 1), GT * g):
                        pool.wait_ge(xhat_done, i + 1)
                        if g >= 3:
                            pool.wait_ge(resid_out[(g - 1) % 2], 16 * ((g - 1) // 2))
                        pool.tensor_tensor(both[0:TT, (g - 1) % 2, i % GT, :], xhat[0:TT, i % (2 * GT), :], stream[0:TT, i, :], ALU.add).then_inc(both_done, 1)

        @block.vector
        def _(dve):
            for g in range(NS + 1):
                if g < NS:
                    for k in range(GT + 1):
                        i = GT * g + k
                        if k < GT:
                            dve.wait_ge(p_ready, i + 1)
                            dve.wait_ge(added, i + 1)
                            dve.tensor_tensor(stream[0:TT, i, :], ps[i % 4][0:TT, 0:CH], tiles[0:TT, i, :], ALU.add).then_inc(p_done, 1)
                        if k:
                            dve.wait_ge(p_done, i)
                            dve.bn_stats(raw[0:TT, i - 1, :], stream[0:TT, i - 1, :]).then_inc(raw_done, 1)
                    for i in range(GT * g, GT * (g + 1)):
                        dve.wait_ge(raw_done, i + 1)
                        dve.bn_aggr(stats[0:TT, i, :], raw[0:TT, i, :]).then_inc(agg_done, 1)
                if g:
                    cols = slice((g - 1) * GT, g * GT)
                    dve.wait_ge(std_done, g)
                    dve.reciprocal(rstd[0:TT, cols], std[0:TT, cols]).then_inc(rstd_done, 1)
                    dve.wait_ge(rstd_done, g)
                    for i in range(GT * (g - 1), GT * g):
                        if i >= 2 * GT:
                            dve.wait_ge(turned, i - 2 * GT + 1)
                            dve.wait_ge(both_done, i - 2 * GT + 1)
                        dve.tensor_scalar(xhat[0:TT, i % (2 * GT), :], stream[0:TT, i, :], stats[0:TT, i, 0:1], rstd[0:TT, i:i + 1],
                                          ALU.subtract, ALU.mult).then_inc(xhat_done, 1)

        @block.tensor
        def _(pe):
            def turn(g):
                for i in range(GT * g, GT * (g + 1)):
                    pe.wait_ge(xhat_done, i + 1)
                    if i >= 4:
                        pe.wait_ge(turned_evac, i - 3)
                    for c in range(CC):
                        mm = pe.transpose(ps[4 + i % 4][:, c * TT:(c + 1) * TT], xhat[0:TT, i % (2 * GT), c * 128:(c + 1) * 128], ident[0:TT, 0:TT])
                    mm.then_inc(turned, 1)

            pe.wait_ge(w_in, 16)
            for g in range(NS + 1):
                if g < NS:
                    for i in range(GT * g, GT * (g + 1)):
                        if i >= 4:
                            pe.wait_ge(p_done, i - 3)
                        for c in range(CC):
                            mm = pe.matmul(ps[i % 4][0:TT, 0:CH], wide[:, c, i * TT:(i + 1) * TT], w[:, c, :], start=(c == 0), stop=(c == CC - 1))
                        mm.then_inc(p_ready, 1)
                if g > 1:
                    turn(g - 2)
            turn(NS - 1)


def expert_layer(nc, sem, ps, ident, ident_b, eps, wide, stats, resid, normed_t, router_t, w1, b1, w2, b2, out):
    with ExitStack() as mem:
        def sb(name, shape, dt=F32):
            return mem.enter_context(nc.sbuf_tensor(name, shape, dt))

        full1 = sb("full1", [128, EXPERTS, CC * CH])
        full2 = sb("full2", [128, EXPERTS, CC * CH])
        w1_sb = sb("w1_sb", [128, 2, EXPERTS, CC, CH], F16)
        w2_sb = sb("w2_sb", [128, 2, EXPERTS, CC, CH], F16)
        b1_sb = sb("b1_sb", [128, EXPERTS, CC])
        b2_sb = sb("b2_sb", [EXPERTS, CH])
        rt = sb("rt", [128, CC, EXPERTS])
        xg = [sb(f"xg{k}", [128, CC, SUP]) for k in range(2)]
        xs = [sb(f"xs{k}", [128, 2, CC, SUP], F16) for k in range(2)]
        acc = [sb(f"acc{k}", [128, 4, CH]) for k in range(2)]
        gel = sb("gel", [128, 2, CC, SUP])
        hid = sb("hid", [128, 2, 2, CC, SUP], F16)
        small = {n: sb("e_" + n, [128, 4, EXPERTS]) for n in ("shift", "expo", "prob", "eq", "pos", "one", "left", "eq2", "pos2", "two", "sel")}
        col = {n: sb("e_" + n, [128, 4, 1]) for n in ("mx", "sum", "rsum", "p1", "i1", "p2", "i2", "tot", "rtot")}
        comb = [sb(f"comb{k}", [128, 4, EXPERTS]) for k in range(2)]
        comb_y = [sb(f"comb_y{k}", [128, 4, EXPERTS]) for k in range(2)]
        iota = sb("iota", [128, 4, EXPERTS])
        comb_t = sb("comb_t", [EXPERTS, 4, TT])
        result = sb("result", [128, CC, SUP])
        lane_max = sb("lane_max", [128, 3])
        most3 = sb("most3", [3, 1])
        diag3 = sb("diag3", [3, 3])
        ones3 = sb("ones3", [3, 128])
        most = sb("most_w", [128, 3])
        inverse = sb("inverse", [128, 2])
        up_w = sb("up_w", [128, 2])
        bound = sb("bound", [128, 1])
        per_bound = sb("per_bound", [128, 1])
        up_h = sb("up_h", [128, 1])
        down_h = sb("down_h", [128, 1])
        bound_w = sb("bound_w", [128, 1])
        down_y = sb("down_y", [128, 1])

        w1_in, w2_in, b1_in = sem("e_w1_in"), sem("e_w2_in"), sem("e_b1_in")
        iota_set, bias_in = sem("e_iota_set"), sem("e_bias_in")
        lane_done, set_up, over, w_hi, w_lo = sem("e_lane_done"), sem("e_set_up"), sem("e_over"), sem("e_w_hi"), sem("e_w_lo")
        with nc.Block() as block:
            @block.sync
            def _(sp):
                sp.dma_start(full1[:].rearrange("p e (c o) -> p e c o", c=CC), w1.rearrange("e (c p) o -> p e c o", p=128)).then_inc(w1_in, 16)
                sp.dma_start(full2[:].rearrange("p e (c o) -> p e c o", c=CC), w2.rearrange("e (c p) o -> p e c o", p=128)).then_inc(w2_in, 16)
                sp.dma_start(b2_sb[:], b2).then_inc(bias_in, 16)
                sp.dma_start(rt[:], router_t.rearrange("(c p) e -> p c e", p=128)).then_inc(bias_in, 16)
                sp.wait_ge(bias_in, 16 * 2)

            @block.gpsimd
            def _(pool):
                pool.memset(ones3[:], 1.0).then_inc(iota_set, 1)
                for e in range(EXPERTS):
                    pool.memset(iota[:, :, e:e + 1], float(e)).then_inc(iota_set, 1)
                pool.wait_ge(iota_set, EXPERTS + 1)

            @block.scalar
            def _(act):
                with nc.allow_non_contiguous_dma(reason="a bias by channel"):
                    for c in range(CC):
                        act.dma_start(b1_sb[:, :, c], b1[:, c * 128:(c + 1) * 128].rearrange("e p -> p e")).then_inc(b1_in, 16)
                act.wait_ge(set_up, 9)
                for k, (full, parts) in enumerate(((full1, w1_sb), (full2, w2_sb))):
                    for e in range(EXPERTS):
                        act.activation(parts[:, 0, e].rearrange("p c o -> p (c o)"), full[:, e, :], ACT.Copy, scale=up_w[:, k:k + 1]).then_inc(w_hi, 1)

            @block.tensor
            def _(pe):
                pe.wait_ge(lane_done, 3)
                pe.transpose(ps[0][0:3, 0:128], lane_max[:], ident[:]).then_inc(over, 1)
                pe.wait_ge(set_up, 2)
                pe.wait_ge(iota_set, 1)
                pe.matmul(ps[1][:, 0:3], ones3[:], diag3[:], start=True, stop=True).then_inc(over, 1)

            @block.vector
            def _(dve):
                count = [0]

                def link(ins):
                    count[0] += 1
                    ins.then_inc(set_up, 1)
                    dve.wait_ge(set_up, count[0])

                for k, src in enumerate((full1, full2)):
                    dve.wait_ge((w1_in, w2_in)[k], 16)
                    dve.tensor_reduce(lane_max[:, k:k + 1], src[:].rearrange("p e o -> p (e o)"), AX.X, ALU.max, apply_absolute_value=True).then_inc(lane_done, 1)
                dve.wait_ge(b1_in, 16 * CC)
                dve.tensor_reduce(lane_max[:, 2:3], b1_sb[:].rearrange("p e c -> p (e c)"), AX.X, ALU.max, apply_absolute_value=True).then_inc(lane_done, 1)
                dve.wait_ge(over, 1)
                link(dve.tensor_reduce(most3[:], ps[0][0:3, 0:128], AX.X, ALU.max))
                link(dve.tensor_scalar(diag3[:], ident[0:3, 0:3], most3[:, 0:1], None, ALU.mult))
                dve.wait_ge(over, 2)
                link(dve.tensor_scalar(most[:], ps[1][:, 0:3], 1e-6, None, ALU.max))
                link(dve.reciprocal(inverse[:], most[:, 0:2]))
                link(dve.tensor_scalar(bound[:], most[:, 0:1], float(CH), most[:, 2:3], ALU.mult, ALU.add))
                link(dve.reciprocal(per_bound[:], bound[:]))
                link(dve.tensor_scalar(up_h[:], per_bound[:], HID_MAX, None, ALU.mult))
                link(dve.tensor_scalar(down_h[:], most[:, 0:1], 1.0 / (SPLIT_MAX * X_SCALE), None, ALU.mult))
                link(dve.tensor_scalar(up_w[:], inverse[:], SPLIT_MAX, None, ALU.mult))
                link(dve.tensor_tensor(bound_w[:], bound[:], most[:, 1:2], ALU.mult))
                link(dve.tensor_scalar(down_y[:], bound_w[:], 1.0 / (HID_MAX * SPLIT_MAX), None, ALU.mult))
                for k, (full, parts) in enumerate(((full1, w1_sb), (full2, w2_sb))):
                    for e in range(EXPERTS):
                        dve.wait_ge(w_hi, k * EXPERTS + e + 1)
                        dve.scalar_tensor_tensor(out=parts[:, 1, e].rearrange("p c o -> p (c o)"), in0=full[:, e, :], scalar=up_w[:, k:k + 1],
                                                 in1=parts[:, 0, e].rearrange("p c o -> p (c o)"), op0=ALU.mult, op1=ALU.subtract).then_inc(w_lo, 1)

        mark = []

        def own(name):
            s = sem(name)
            mark.append(s)
            return s

        x_in, acc_in = [own("e_x_in0"), own("e_x_in1")], [own("e_acc_in0"), own("e_acc_in1")]
        lg_ready, lg_read, chain, exp_done, comb_done = own("e_lg_ready"), own("e_lg_read"), own("e_chain"), own("e_exp_done"), own("e_comb_done")
        comb_y_done, xh_done, xl_done = own("e_comb_y_done"), own("e_xh_done"), own("e_xl_done")
        ct_ready, ct_done, bias_ready, bias_done = own("e_ct_ready"), own("e_ct_done"), own("e_bias_ready"), own("e_bias_done")
        h_ready, gel_done, hh_done, hl_done = own("e_h_ready"), own("e_gel_done"), own("e_hh_done"), own("e_hl_done")
        y_ready, y_done = own("e_y_ready"), own("e_y_done")
        o_turned, o_evac, o_out = own("e_o_turned"), own("e_o_evac"), own("e_o_out")

        HID, OUTS, MISC, TURNS = [0, 1, 2], [3, 4, 5], 6, 7
        LAST = NS * EXPERTS
        STEPS = 21

        with nc.Fori(0, IMAGES) as image:
            with nc.Block() as block:
                @block.sync
                def _(sp):
                    def load_x(g):
                        if g >= 2:
                            sp.wait_ge(lg_ready, g - 1)
                            sp.wait_ge(xh_done, g - 1)
                            sp.wait_ge(xl_done, g - 1)
                        sp.dma_start(xg[g % 2][:], normed_t[bass.ds(image, 1), :, g * SUP:(g + 1) * SUP].rearrange(
                            "a (c p) t -> p (a c) t", p=128)).then_inc(x_in[g % 2], 16)

                    def load_acc(g):
                        if g >= 2:
                            sp.wait_ge(o_turned, CC * (g - 1))
                        sp.dma_start(acc[g % 2][0:TT], resid[bass.ds(image, 1), g * SUP:(g + 1) * SUP, :].rearrange(
                            "a (i t) c -> t (a i) c", t=TT)).then_inc(acc_in[g % 2], 16)

                    def store(g):
                        sp.wait_ge(o_evac, CC * (g + 1))
                        sp.dma_start(out[bass.ds(image, 1), :, g * SUP:(g + 1) * SUP].rearrange(
                            "a (c p) t -> p (a c) t", p=128), result[:]).then_inc(o_out, 16)

                    load_x(0)
                    load_acc(0)
                    for g in range(NS):
                        if g + 1 < NS:
                            load_x(g + 1)
                            load_acc(g + 1)
                        if g:
                            store(g - 1)
                    store(NS - 1)
                    sp.wait_ge(o_out, 16 * NS)

                @block.scalar
                def _(act):
                    def router_exp(g):
                        act.wait_ge(chain, STEPS * g + 2)
                        act.activation(small["expo"][0:TT], small["shift"][0:TT], ACT.Exp).then_inc(exp_done, 1)

                    def copy_weights(g):
                        act.wait_ge(ct_ready, g + 1)
                        if g:
                            act.wait_ge(bias_ready, 2 * g)
                        act.activation(comb_t[:], ps[MISC][0:EXPERTS, 0:SUP].rearrange("e (i t) -> e i t", i=4), ACT.Copy).then_inc(ct_done, 1)

                    def split_x(g):
                        act.wait_ge(x_in[g % 2], 16 * (g // 2 + 1))
                        if g >= 2:
                            act.wait_ge(h_ready, CC * EXPERTS * (g - 1))
                        act.activation(xs[g % 2][:, 0], xg[g % 2][:], ACT.Copy, scale=X_SCALE).then_inc(xh_done, 1)

                    def hidden(turn):
                        for c in range(CC):
                            n = turn * CC + c
                            act.wait_ge(h_ready, n + 1)
                            if turn >= 2:
                                act.wait_ge(hl_done, CC * (turn - 2) + c + 1)
                            act.activation(gel[:, turn % 2, c, :], ps[HID[n % 3]][:, 0:SUP], ACT.Gelu,
                                           bias=b1_sb[:, turn % EXPERTS, c:c + 1], scale=down_h[:, 0:1]).then_inc(gel_done, 1)
                        for c in range(CC):
                            act.wait_ge(gel_done, turn * CC + c + 1)
                            if turn >= 2:
                                act.wait_ge(y_ready, 4 * (turn - 1))
                            act.activation(hid[:, turn % 2, 0, c, :], gel[:, turn % 2, c, :], ACT.Copy, scale=up_h[:, 0:1]).then_inc(hh_done, 1)

                    def take_out(g):
                        for c in range(CC):
                            act.wait_ge(o_turned, CC * g + c + 1)
                            if g and c == 0:
                                act.wait_ge(o_out, 16 * g)
                            act.activation(result[:, c, :], ps[TURNS - c][:, 0:SUP], ACT.Copy).then_inc(o_evac, 1)

                    split_x(0)
                    router_exp(0)
                    hidden(0)
                    hidden(1)
                    copy_weights(0)
                    for turn in range(LAST):
                        g, e = divmod(turn, EXPERTS)
                        if turn + 2 < LAST:
                            hidden(turn + 2)
                        if e == 1 and g:
                            take_out(g - 1)
                        if e == 2 and g + 1 < NS:
                            split_x(g + 1)
                        if e == 3 and g + 1 < NS:
                            router_exp(g + 1)
                        if e == EXPERTS - 1 and g + 1 < NS:
                            copy_weights(g + 1)
                    take_out(NS - 1)

                @block.vector
                def _(dve):
                    t = {k: v[0:TT] for k, v in (small | col).items()}
                    wide8 = lambda a: a.broadcast_to([TT, 4, EXPERTS])

                    def router(g):
                        count = STEPS * g
                        logits = ps[MISC][0:TT, 0:4 * EXPERTS].rearrange("p (i e) -> p i e", i=4)
                        dve.wait_ge(lg_ready, g + 1)
                        dve.tensor_reduce(t["mx"], logits, AX.X, ALU.max).then_inc(chain, 1)
                        yield
                        dve.wait_ge(chain, count + 1)
                        dve.tensor_tensor(t["shift"], logits, wide8(t["mx"]), ALU.subtract).then_inc(chain, 1)
                        yield
                        dve.wait_ge(exp_done, g + 1)
                        dve.tensor_reduce(t["sum"], t["expo"], AX.X, ALU.add).then_inc(chain, 1)
                        yield
                        dve.wait_ge(chain, count + 3)
                        dve.reciprocal(t["rsum"], t["sum"]).then_inc(chain, 1)
                        yield
                        dve.wait_ge(chain, count + 4)
                        dve.tensor_tensor(t["prob"], t["expo"], wide8(t["rsum"]), ALU.mult).then_inc(chain, 1)
                        yield
                        count += 5
                        for p, eq, pos, idx, best, src in (("p1", "eq", "pos", "i1", "one", "prob"), ("p2", "eq2", "pos2", "i2", "two", "left")):
                            dve.wait_ge(chain, count)
                            dve.tensor_reduce(t[p], t[src], AX.X, ALU.max).then_inc(chain, 1)
                            yield
                            dve.wait_ge(chain, count + 1)
                            dve.tensor_tensor(t[eq], t[src], wide8(t[p]), ALU.is_equal).then_inc(chain, 1)
                            yield
                            dve.wait_ge(chain, count + 2)
                            dve.scalar_tensor_tensor(out=t[pos], in0=t[eq], scalar=-float(EXPERTS), in1=iota[0:TT],
                                                     op0=ALU.mult, op1=ALU.add).then_inc(chain, 1)
                            yield
                            dve.wait_ge(chain, count + 3)
                            dve.tensor_reduce(t[idx], t[pos], AX.X, ALU.min).then_inc(chain, 1)
                            yield
                            dve.wait_ge(chain, count + 4)
                            dve.tensor_tensor(t[best], t[pos], wide8(t[idx]), ALU.is_equal).then_inc(chain, 1)
                            yield
                            count += 5
                            if best == "one":
                                dve.wait_ge(chain, count)
                                dve.scalar_tensor_tensor(out=t["left"], in0=t["one"], scalar=-2.0, in1=t["prob"],
                                                         op0=ALU.mult, op1=ALU.add).then_inc(chain, 1)
                                yield
                                count += 1
                        dve.wait_ge(chain, count)
                        dve.tensor_tensor(t["tot"], t["p1"], t["p2"], ALU.add).then_inc(chain, 1)
                        yield
                        dve.wait_ge(chain, count + 1)
                        dve.tensor_scalar(t["tot"], t["tot"], 1e-12, None, ALU.max).then_inc(chain, 1)
                        yield
                        dve.wait_ge(chain, count + 2)
                        dve.reciprocal(t["rtot"], t["tot"]).then_inc(chain, 1)
                        yield
                        dve.tensor_tensor(t["sel"], t["one"], t["two"], ALU.add).then_inc(chain, 1)
                        yield
                        dve.wait_ge(chain, count + 4)
                        dve.tensor_tensor(t["sel"], t["sel"], t["prob"], ALU.mult).then_inc(chain, 1)
                        yield
                        dve.wait_ge(chain, count + 5)
                        if g >= 2:
                            dve.wait_ge(ct_ready, g - 1)
                        dve.tensor_tensor(comb[g % 2][0:TT], t["sel"], wide8(t["rtot"]), ALU.mult).then_inc(comb_done, 1)
                        yield
                        dve.wait_ge(comb_done, g + 1)
                        dve.tensor_scalar(comb_y[g % 2][0:TT], comb[g % 2][0:TT], down_y[0:TT, 0:1], None, ALU.mult).then_inc(comb_y_done, 1)
                        assert count + 5 == STEPS * g + STEPS, count
                        yield

                    def add_bias(g):
                        for k, bank in enumerate((TURNS, MISC)):
                            dve.wait_ge(bias_ready, 2 * g + k + 1)
                            dve.wait_ge(y_done, 4 * EXPERTS * g + 4)
                            pair = acc[g % 2][0:TT, 2 * k:2 * k + 2, :]
                            dve.tensor_tensor(pair, ps[bank][0:TT, 0:2 * CH].rearrange("t (i c) -> t i c", i=2), pair, ALU.add).then_inc(bias_done, 1)

                    def split_x(g):
                        dve.wait_ge(xh_done, g + 1)
                        dve.scalar_tensor_tensor(out=xs[g % 2][:, 1], in0=xg[g % 2][:], scalar=X_SCALE, in1=xs[g % 2][:, 0],
                                                 op0=ALU.mult, op1=ALU.subtract).then_inc(xl_done, 1)

                    def split_hidden(turn):
                        for c in range(CC):
                            dve.wait_ge(hh_done, turn * CC + c + 1)
                            dve.scalar_tensor_tensor(out=hid[:, turn % 2, 1, c, :], in0=gel[:, turn % 2, c, :], scalar=up_h[:, 0:1],
                                                     in1=hid[:, turn % 2, 0, c, :], op0=ALU.mult, op1=ALU.subtract).then_inc(hl_done, 1)

                    split_x(0)
                    steps = router(0)
                    for _ in range(2):
                        next(steps)
                    split_hidden(0)
                    for _ in steps:
                        pass
                    for turn in range(LAST):
                        g, e = divmod(turn, EXPERTS)
                        if e == 0:
                            dve.wait_ge(acc_in[g % 2], 16 * (g // 2 + 1))
                            dve.wait_ge(comb_y_done, g + 1)
                        if e == 1:
                            add_bias(g)
                            dve.wait_ge(bias_done, 2 * g + 2)
                        if e == 3 and g + 1 < NS:
                            split_x(g + 1)
                            steps = router(g + 1)
                        for i in range(4):
                            n = 4 * turn + i
                            dve.wait_ge(y_ready, n + 1)
                            if e:
                                dve.wait_ge(y_done, n - 3)
                            tile = acc[g % 2][0:TT, i, :]
                            dve.scalar_tensor_tensor(out=tile, in0=ps[OUTS[n % 3]][0:TT, 0:CH], scalar=comb_y[g % 2][0:TT, i, e:e + 1],
                                                     in1=tile, op0=ALU.mult, op1=ALU.add).then_inc(y_done, 1)
                            if i == 1 and turn + 1 < LAST:
                                split_hidden(turn + 1)
                            if g + 1 < NS and e == 3 and i < 2:
                                next(steps)
                            if g + 1 < NS and e > 3:
                                for _ in range(2):
                                    next(steps, None)

                @block.tensor
                def _(pe):
                    def logits(g):
                        pe.wait_ge(x_in[g % 2], 16 * (g // 2 + 1))
                        if g >= 2:
                            pe.wait_ge(o_evac, CC * (g - 1))
                        for i in range(4):
                            for k in range(CC):
                                mm = pe.matmul(ps[MISC][0:TT, i * EXPERTS:(i + 1) * EXPERTS], xg[g % 2][:, k, i * TT:(i + 1) * TT], rt[:, k, :],
                                               start=(k == 0), stop=(k == CC - 1))
                        mm.then_inc(lg_ready, 1)

                    def turn_weights(g):
                        pe.wait_ge(comb_done, g + 1)
                        for i in range(4):
                            mm = pe.transpose(ps[MISC][0:EXPERTS, i * TT:(i + 1) * TT], comb[g % 2][0:TT, i, :], ident[0:TT, 0:TT])
                        mm.then_inc(ct_ready, 1)

                    def bias(g):
                        pe.wait_ge(ct_done, g + 1)
                        for k, bank in enumerate((TURNS, MISC)):
                            for i in range(2):
                                mm = pe.matmul(ps[bank][0:TT, i * CH:(i + 1) * CH], comb_t[:, 2 * k + i, :], b2_sb[:], start=True, stop=True)
                            mm.then_inc(bias_ready, 1)

                    def turn_results(g):
                        pe.wait_ge(y_done, 4 * EXPERTS * (g + 1))
                        pe.wait_ge(bias_done, 2 * min(g + 2, NS))
                        for c in range(CC):
                            for i in range(4):
                                mm = pe.transpose(ps[TURNS - c][:, i * TT:(i + 1) * TT], acc[g % 2][0:TT, i, c * 128:(c + 1) * 128], ident[0:TT, 0:TT])
                            mm.then_inc(o_turned, 1)

                    PRODUCTS = ((0, 0), (0, 1), (1, 0))

                    def first_layer(turn):
                        g, e = divmod(turn, EXPERTS)
                        if e == 0:
                            pe.wait_ge(xl_done, g + 1)
                        for c in range(CC):
                            n = turn * CC + c
                            if n >= 3:
                                pe.wait_ge(gel_done, n - 2)
                            for k in range(CC):
                                for a, b in PRODUCTS:
                                    mm = pe.matmul(ps[HID[n % 3]][:, 0:SUP], w1_sb[:, a, e, k, c * 128:(c + 1) * 128], xs[g % 2][:, b, k, :],
                                                   start=(k + a + b == 0), stop=(k == CC - 1 and a == 1))
                            mm.then_inc(h_ready, 1)

                    def second_layer(turn):
                        pe.wait_ge(hl_done, CC * (turn + 1))
                        for i in range(4):
                            n = 4 * turn + i
                            if n >= 3:
                                pe.wait_ge(y_done, n - 2)
                            for k in range(CC):
                                for a, b in PRODUCTS:
                                    mm = pe.matmul(ps[OUTS[n % 3]][0:TT, 0:CH], hid[:, turn % 2, a, k, i * TT:(i + 1) * TT],
                                                   w2_sb[:, b, turn % EXPERTS, k, :], start=(k + a + b == 0), stop=(k == CC - 1 and a == 1))
                            mm.then_inc(y_ready, 1)

                    logits(0)
                    first_layer(0)
                    first_layer(1)
                    turn_weights(0)
                    for turn in range(LAST):
                        g, e = divmod(turn, EXPERTS)
                        second_layer(turn)
                        if turn + 2 < LAST:
                            first_layer(turn + 2)
                        if e == 0:
                            bias(g)
                        if e == 1 and g:
                            turn_results(g - 1)
                        if e == 2 and g + 1 < NS:
                            logits(g + 1)
                        if e == EXPERTS - 1 and g + 1 < NS:
                            turn_weights(g + 1)
                    turn_results(NS - 1)

            for s in mark:
                nc.sync.sem_clear(s)
            nc.all_engine_barrier()


def kernel(**inputs):
    import ml_dtypes as _ml
    import numpy as _np
    import concourse.bacc as _bacc
    from concourse import mybir as _mybir
    from concourse.bass_utils import run_bass_kernel_spmd as _run

    a = {k: _np.asarray(v) for k, v in inputs.items()}
    bf16 = _ml.bfloat16
    rows = _np.arange(TT)
    lane = _np.arange(128)
    behind = _np.where(rows[None, :] > rows[:, None], NEG, 0.0)
    arrays = {
        "x": a["x"].reshape(IMAGES * CH, TOK),
        "qkv0_t": a["L0_conv_qkv_w"].T, "qkv0_b": a["L0_conv_qkv_b"],
        "proj0_t": a["L0_conv_proj_w"].T, "proj0_b": a["L0_conv_proj_b"],
        "rel_bias": a["L0_conv_relative_bias"],
        "w_qkv": a["L1_attn_w_qkv"], "b_qkv": a["L1_attn_b_qkv"],
        "w_proj": a["L1_attn_w_proj"], "b_proj": a["L1_attn_b_proj"],
        "router_t": a["L1_ffn_router_w"].T,
        "w1": a["L1_ffn_w1"], "b1": a["L1_ffn_b1"], "w2": a["L1_ffn_w2"], "b2": a["L1_ffn_b2"],
        "ident_in": _np.eye(128, dtype=_np.float32),
        "ident_b_in": _np.eye(128).astype(bf16),
        "group_in": (lane[:, None] // 8 == lane[None, :] // 8).astype(_np.float32) / 8,
        "nmask_in": neighbourhood_mask().astype(bf16),
        "causal_q_in": behind.astype(bf16),
        "causal_k_in": _np.ascontiguousarray(behind.T).astype(bf16),
        "unit_row_in": _np.full(HC * TOK, ROW_UNIT, _np.float16),
    }
    arrays = {f"in_{k}": _np.ascontiguousarray(v) for k, v in arrays.items()}
    nc = _bacc.Bacc("TRN2", target_bir_lowering=False, num_devices=1)
    args = [nc.dram_tensor(k, v.shape, _mybir.dt.from_np(v.dtype), kind="ExternalInput").ap() for k, v in arrays.items()]
    args.append(nc.dram_tensor("out_dram", (IMAGES, CH, TOK), F32, kind="ExternalOutput").ap())
    hybrid_kernel(nc, *args)
    r = _run(nc, [arrays], core_ids=[0])
    return r.results[0]["out_dram"].reshape(IMAGES, CH, SIDE, SIDE)
```
